# Optimizing a Trainium2 kernel written in Bass

```python
import numpy as np
import jax
import jax.numpy as jnp

def _softmax(x, axis=-1):
    return jax.nn.softmax(x, axis=axis)

def _gelu(x):
    return jax.nn.gelu(x, approximate=True)

def _silu(x):
    return jax.nn.silu(x)

def _sigmoid(x):
    return jax.nn.sigmoid(x)

def _layernorm(x, axis=-1, eps=1e-05):
    m = jnp.mean(x, axis=axis, keepdims=True)
    v = jnp.var(x, axis=axis, keepdims=True)
    return (x - m) / jnp.sqrt(v + eps)

def _scatter_add(tgt, idx, src, axis=0):
    return tgt.at[idx].add(src)

def _segment_sum(src, seg, n):
    return jax.ops.segment_sum(src, seg, n)
kernel_name = 'mk_xattn_ffn_d4_seqx_r4_6c7928'

def setup_inputs(seed: int=0):
    np.random.seed(seed)
    _w = jnp.asarray

    def _rec_inputs():
        import jax
        import jax.numpy as jnp
        _rk = jax.random.key(seed)
        x = -0.0002928 + 1 * jax.random.normal(jax.random.fold_in(_rk, 1), (8, 256, 256), jnp.float32)
        _lenS = 256 - jax.random.randint(jax.random.fold_in(_rk, 7), (8,), 0, max(1, 256 // 4) + 1, jnp.int32)
        _lenS2 = 77 - jax.random.randint(jax.random.fold_in(_rk, 8), (8,), 0, max(1, 77 // 4) + 1, jnp.int32)
        _ctx_1024P = jax.random.normal(jax.random.fold_in(_rk, 11), (8, 16, 256), jnp.float32)
        _ctx_1024c = jax.random.dirichlet(jax.random.fold_in(_rk, 511), 0.3 * jnp.ones((16,), jnp.float32), (8, 77))
        _ctx_1024t = jnp.einsum('bsk,bkd->bsd', _ctx_1024c, _ctx_1024P)
        _ctx_1024t = _ctx_1024t * jax.lax.rsqrt(jnp.mean(jnp.square(_ctx_1024t)) + 1e-12) * 0.953939
        ctx_1024 = -1.39393e-06 + 0.999914 * (_ctx_1024t + 0.3 * jax.random.normal(jax.random.fold_in(_rk, 611), (8, 77, 256), jnp.float32))
        fside_BxSxS2_0 = -0.000354355 + 1.00006 * jax.random.normal(jax.random.fold_in(_rk, 13), (8, 256, 77), jnp.float32)
        _validS = jnp.arange(256)[None, :] < _lenS[:, None]
        _validS2 = jnp.arange(77)[None, :] < _lenS2[:, None]
        _causal = jnp.tril(jnp.ones((256, 256), dtype=bool))
        mask_BxS2_ik0 = jnp.where(jnp.broadcast_to(_validS2[:, :], (8, 77)), 0, 1).astype(jnp.int32)
        mask_BxS2_if0 = jnp.where(jnp.ones((8, 77), dtype=bool), 0, 1).astype(jnp.int32)
        return (x, ctx_1024, fside_BxSxS2_0, mask_BxS2_ik0, mask_BxS2_if0)
    x, ctx_1024, fside_BxSxS2_0, mask_BxS2_ik0, mask_BxS2_if0 = _rec_inputs()

    def _L0_xattn_setup():
        import jax, jax.numpy as jnp
        import numpy as np
        import math
        D_MODEL = 256
        NUM_HEADS = 16
        D_K = D_MODEL // NUM_HEADS
        B, NQ, NK = (2, 512, 512)
        key = jax.random.key(seed)
        ks = jax.random.split(key, 14)
        s = 1.0 / math.sqrt(D_MODEL)
        inp = {'query': jax.random.normal(ks[0], (B, NQ, D_MODEL), jnp.float32), 'key': jax.random.normal(ks[1], (B, NK, D_MODEL), jnp.float32), 'value': jax.random.normal(ks[2], (B, NK, D_MODEL), jnp.float32), 'mask': jax.random.randint(ks[3], (B, NK), 0, 2, jnp.int32), 'attn_bias': jax.random.normal(ks[4], (B, NQ, NK), jnp.float32), 'w_q': jax.random.normal(ks[5], (D_MODEL, D_MODEL), jnp.float32) * s, 'b_q': jnp.zeros((D_MODEL,), jnp.float32), 'w_k': jax.random.normal(ks[6], (D_MODEL, D_MODEL), jnp.float32) * s, 'b_k': jnp.zeros((D_MODEL,), jnp.float32), 'w_v': jax.random.normal(ks[7], (D_MODEL, D_MODEL), jnp.float32) * s, 'b_v': jnp.zeros((D_MODEL,), jnp.float32), 'w_o': jax.random.normal(ks[8], (D_MODEL, D_MODEL), jnp.float32) * s, 'b_o': jnp.zeros((D_MODEL,), jnp.float32)}
        return inp
    _L0_xattn_all = _L0_xattn_setup()
    _L0_xattn_in = {k: v for k, v in _L0_xattn_all.items() if k in ('w_q', 'b_q', 'w_k', 'b_k', 'w_v', 'b_v', 'w_o', 'b_o')}
    del _L0_xattn_all

    def _L0_ffn_setup():
        import jax, jax.numpy as jnp
        import numpy as np
        DIM = 256

        def _reference_tuple_inner(x, W_r, W_k, W_v, mu_r, mu_k):
            B, T, C = x.shape
            x_prev = jnp.concatenate([jnp.zeros((B, 1, C), x.dtype), x[:, :-1, :]], axis=1)
            xr = mu_r * x + (1.0 - mu_r) * x_prev
            xk = mu_k * x + (1.0 - mu_k) * x_prev
            r = jax.nn.sigmoid(jnp.einsum('btc,dc->btd', xr, W_r))
            k = jnp.einsum('btc,dc->btd', xk, W_k)
            k_act = jnp.square(jax.nn.relu(k))
            out = r * jnp.einsum('btc,dc->btd', k_act, W_v)
            new_state = x[:, -1, :]
            return (out, new_state)
        key = jax.random.key(seed)
        ks = jax.random.split(key, 6)
        B, T, C = (8, 512, DIM)
        x = jax.random.normal(ks[0], (B, T, C), dtype=jnp.float32)
        s = 1.0 / np.sqrt(C)
        W_r = jax.random.uniform(ks[1], (C, C), jnp.float32, -s, s)
        W_k = jax.random.uniform(ks[2], (C, C), jnp.float32, -s, s)
        W_v = jax.random.uniform(ks[3], (C, C), jnp.float32, -s, s)
        mu_r = jax.random.uniform(ks[4], (C,), jnp.float32)
        mu_k = jax.random.uniform(ks[5], (C,), jnp.float32)
        return {'x': x, 'W_r': W_r, 'W_k': W_k, 'W_v': W_v, 'mu_r': mu_r, 'mu_k': mu_k}
    _L0_ffn_all = _L0_ffn_setup()
    _L0_ffn_in = {k: v for k, v in _L0_ffn_all.items() if k in ('W_r', 'W_k', 'W_v', 'mu_r', 'mu_k')}
    del _L0_ffn_all

    def _L1_xattn_setup():
        import jax, jax.numpy as jnp
        import numpy as np
        E, T, H, F = (8, 256, 256, 1024)
        key = jax.random.key(seed)
        k1, k2, k3 = jax.random.split(key, 3)
        x = jax.random.normal(k1, (E, T, H), dtype=jnp.float32)
        w1 = jax.random.normal(k2, (E, F, H), dtype=jnp.float32) * (1.0 / np.sqrt(H))
        w2 = jax.random.normal(k3, (E, F, H), dtype=jnp.float32) * (1.0 / np.sqrt(F))
        return {'x': x, 'w1': w1, 'w2': w2}
    _L1_xattn_all = _L1_xattn_setup()
    _L1_xattn_in = {k: v for k, v in _L1_xattn_all.items() if k in ()}
    del _L1_xattn_all

    def _L1_ffn_setup():
        import jax, jax.numpy as jnp
        import numpy as np
        B, S, D = (4, 512, 256)
        E, K = (8, 2)
        H = 352
        key = jax.random.key(seed)
        kx, kr, k1, k2, k3 = jax.random.split(key, 5)
        s = 0.02
        return {'x': jax.random.normal(kx, (B, S, D), dtype=jnp.float32), 'w_router': jax.random.normal(kr, (E, D), dtype=jnp.float32) * s, 'w1': jax.random.normal(k1, (E, D, H), dtype=jnp.float32) * s, 'w2': jax.random.normal(k2, (E, H, D), dtype=jnp.float32) * s, 'w3': jax.random.normal(k3, (E, D, H), dtype=jnp.float32) * s}
    _L1_ffn_all = _L1_ffn_setup()
    _L1_ffn_in = {k: v for k, v in _L1_ffn_all.items() if k in ('w_router', 'w1', 'w2', 'w3')}
    del _L1_ffn_all

    def _L2_xattn_setup():
        import jax, jax.numpy as jnp
        import numpy as np
        HEAD_NUM = 16
        NEG_INF = float('-inf')
        key = jax.random.key(seed)
        ks = jax.random.split(key, 4)
        B, S, D = (4, 512, 256)
        q = jax.random.normal(ks[0], (B, S, D), dtype=jnp.float32)
        k = jax.random.normal(ks[1], (B, S, D), dtype=jnp.float32)
        v = jax.random.normal(ks[2], (B, S, D), dtype=jnp.float32)
        W = jax.random.normal(ks[3], (D, D), dtype=jnp.float32) / np.sqrt(D)
        b = jnp.zeros((D,), dtype=jnp.float32)
        mask = jnp.zeros((B, S), dtype=jnp.int32)
        return {'q': q, 'k': k, 'v': v, 'W': W, 'b': b, 'mask': mask}
    _L2_xattn_all = _L2_xattn_setup()
    _L2_xattn_in = {k: v for k, v in _L2_xattn_all.items() if k in ('W', 'b')}
    del _L2_xattn_all

    def _L2_ffn_setup():
        import jax, jax.numpy as jnp
        import numpy as np
        B, S, H, F, E = (1, 512, 256, 512, 8)

        def _swiglu(x, wg, wu, wd):
            return jax.nn.silu(x @ wg.T) * (x @ wu.T) @ wd.T
        key = jax.random.key(seed)
        ks = jax.random.split(key, 8)
        sc = 1.0 / np.sqrt(H)
        scf = 1.0 / np.sqrt(F)
        return {'hidden_states': jax.random.normal(ks[0], (B, S, H), jnp.float32), 'gate_w': jax.random.normal(ks[1], (E, H), jnp.float32) * sc, 'shared_gate': jax.random.normal(ks[2], (F, H), jnp.float32) * sc, 'shared_up': jax.random.normal(ks[3], (F, H), jnp.float32) * sc, 'shared_down': jax.random.normal(ks[4], (H, F), jnp.float32) * scf, 'r_gate': jax.random.normal(ks[5], (E, F, H), jnp.float32) * sc, 'r_up': jax.random.normal(ks[6], (E, F, H), jnp.float32) * sc, 'r_down': jax.random.normal(ks[7], (E, H, F), jnp.float32) * scf}
    _L2_ffn_all = _L2_ffn_setup()
    _L2_ffn_in = {k: v for k, v in _L2_ffn_all.items() if k in ('gate_w', 'shared_gate', 'shared_up', 'shared_down', 'r_gate', 'r_up', 'r_down')}
    del _L2_ffn_all

    def _L3_xattn_setup():
        import jax, jax.numpy as jnp
        import numpy as np
        NUM_HEADS = 16
        D_MODEL = 256
        NEG_INF = -1e+30

        def _split_heads(x, h):
            B, S, D = x.shape
            return x.reshape(B, S, h, D // h).transpose(0, 2, 1, 3)
        key = jax.random.key(seed)
        ks = jax.random.split(key, 7)
        B, S, D = (2, 512, D_MODEL)
        scale = 1.0 / np.sqrt(D)
        return {'queries': jax.random.normal(ks[0], (B, S, D), dtype=jnp.float32), 'keys': jax.random.normal(ks[1], (B, S, D), dtype=jnp.float32), 'values': jax.random.normal(ks[2], (B, S, D), dtype=jnp.float32), 'Wq': jax.random.normal(ks[3], (D, D), dtype=jnp.float32) * scale, 'Wk': jax.random.normal(ks[4], (D, D), dtype=jnp.float32) * scale, 'Wv': jax.random.normal(ks[5], (D, D), dtype=jnp.float32) * scale, 'Wo': jax.random.normal(ks[6], (D, D), dtype=jnp.float32) * scale}
    _L3_xattn_all = _L3_xattn_setup()
    _L3_xattn_in = {k: v for k, v in _L3_xattn_all.items() if k in ('Wq', 'Wk', 'Wv', 'Wo')}
    del _L3_xattn_all

    def _L3_ffn_setup():
        import jax, jax.numpy as jnp
        import numpy as np
        EPS = 1e-05
        key = jax.random.key(seed)
        kx, kw, kb = jax.random.split(key, 3)
        B, S, K, N = (8, 2048, 256, 256)
        x = jax.random.normal(kx, (B, S, K), dtype=jnp.float32)
        W = jax.random.normal(kw, (N, K), dtype=jnp.float32) * 0.02
        weight_scale = jnp.maximum(jnp.max(jnp.abs(W), axis=1, keepdims=True) / 127.0, EPS)
        weight_int8 = jnp.clip(jnp.round(W / weight_scale), -128, 127).astype(jnp.int8)
        bias = jax.random.normal(kb, (N,), dtype=jnp.float32) * 0.01
        return {'x': x, 'weight_int8': weight_int8, 'weight_scale': weight_scale, 'bias': bias}
    _L3_ffn_all = _L3_ffn_setup()
    _L3_ffn_in = {k: v for k, v in _L3_ffn_all.items() if k in ('weight_int8', 'weight_scale', 'bias')}
    del _L3_ffn_all
    return {'x': x, 'ctx_1024': ctx_1024, 'fside_BxSxS2_0': fside_BxSxS2_0, 'mask_BxS2_ik0': mask_BxS2_ik0, 'mask_BxS2_if0': mask_BxS2_if0, 'L0_xattn_w_q': _L0_xattn_in['w_q'], 'L0_xattn_b_q': _L0_xattn_in['b_q'], 'L0_xattn_w_k': _L0_xattn_in['w_k'], 'L0_xattn_b_k': _L0_xattn_in['b_k'], 'L0_xattn_w_v': _L0_xattn_in['w_v'], 'L0_xattn_b_v': _L0_xattn_in['b_v'], 'L0_xattn_w_o': _L0_xattn_in['w_o'], 'L0_xattn_b_o': _L0_xattn_in['b_o'], 'L0_ffn_W_r': _L0_ffn_in['W_r'], 'L0_ffn_W_k': _L0_ffn_in['W_k'], 'L0_ffn_W_v': _L0_ffn_in['W_v'], 'L0_ffn_mu_r': _L0_ffn_in['mu_r'], 'L0_ffn_mu_k': _L0_ffn_in['mu_k'], 'L1_ffn_w_router': _L1_ffn_in['w_router'], 'L1_ffn_w1': _L1_ffn_in['w1'], 'L1_ffn_w2': _L1_ffn_in['w2'], 'L1_ffn_w3': _L1_ffn_in['w3'], 'L2_xattn_W': _L2_xattn_in['W'], 'L2_xattn_b': _L2_xattn_in['b'], 'L2_ffn_gate_w': _L2_ffn_in['gate_w'], 'L2_ffn_shared_gate': _L2_ffn_in['shared_gate'], 'L2_ffn_shared_up': _L2_ffn_in['shared_up'], 'L2_ffn_shared_down': _L2_ffn_in['shared_down'], 'L2_ffn_r_gate': _L2_ffn_in['r_gate'], 'L2_ffn_r_up': _L2_ffn_in['r_up'], 'L2_ffn_r_down': _L2_ffn_in['r_down'], 'L3_xattn_Wq': _L3_xattn_in['Wq'], 'L3_xattn_Wk': _L3_xattn_in['Wk'], 'L3_xattn_Wv': _L3_xattn_in['Wv'], 'L3_xattn_Wo': _L3_xattn_in['Wo'], 'L3_ffn_weight_int8': _L3_ffn_in['weight_int8'], 'L3_ffn_weight_scale': _L3_ffn_in['weight_scale'], 'L3_ffn_bias': _L3_ffn_in['bias']}

def reference(x, ctx_1024, fside_BxSxS2_0, mask_BxS2_ik0, mask_BxS2_if0, L0_xattn_w_q, L0_xattn_b_q, L0_xattn_w_k, L0_xattn_b_k, L0_xattn_w_v, L0_xattn_b_v, L0_xattn_w_o, L0_xattn_b_o, L0_ffn_W_r, L0_ffn_W_k, L0_ffn_W_v, L0_ffn_mu_r, L0_ffn_mu_k, L1_ffn_w_router, L1_ffn_w1, L1_ffn_w2, L1_ffn_w3, L2_xattn_W, L2_xattn_b, L2_ffn_gate_w, L2_ffn_shared_gate, L2_ffn_shared_up, L2_ffn_shared_down, L2_ffn_r_gate, L2_ffn_r_up, L2_ffn_r_down, L3_xattn_Wq, L3_xattn_Wk, L3_xattn_Wv, L3_xattn_Wo, L3_ffn_weight_int8, L3_ffn_weight_scale, L3_ffn_bias):
    import jax
    import jax.numpy as jnp

    def _L0_xattn_ref(query, key, value, mask, attn_bias, w_q, b_q, w_k, b_k, w_v, b_v, w_o, b_o):
        import jax, jax.numpy as jnp
        import numpy as np
        import math
        D_MODEL = 256
        NUM_HEADS = 16
        D_K = D_MODEL // NUM_HEADS
        B, NQ, NK = (2, 512, 512)

        def proj(x, w, b, n):
            return (x @ w.T + b).reshape(x.shape[0], n, NUM_HEADS, D_K).transpose(0, 2, 1, 3)
        Q = proj(query, w_q, b_q, query.shape[1])
        K = proj(key, w_k, b_k, key.shape[1])
        V = proj(value, w_v, b_v, value.shape[1])
        scores = jnp.einsum('bhqd,bhkd->bhqk', Q, K) / math.sqrt(D_K)
        scores = scores + attn_bias[:, None, :, :]
        pad = mask[:, None, None, :] == 0
        scores = jnp.where(pad, jnp.float32(-1000000000.0), scores)
        attn = jax.nn.softmax(scores, axis=-1)
        out = jnp.einsum('bhqk,bhkd->bhqd', attn, V)
        out = out.transpose(0, 2, 1, 3).reshape(query.shape[0], query.shape[1], D_MODEL)
        return out @ w_o.T + b_o

    def _L0_ffn_ref(x, W_r, W_k, W_v, mu_r, mu_k):
        import jax, jax.numpy as jnp
        import numpy as np
        DIM = 256

        def _reference_tuple_inner(x, W_r, W_k, W_v, mu_r, mu_k):
            B, T, C = x.shape
            x_prev = jnp.concatenate([jnp.zeros((B, 1, C), x.dtype), x[:, :-1, :]], axis=1)
            xr = mu_r * x + (1.0 - mu_r) * x_prev
            xk = mu_k * x + (1.0 - mu_k) * x_prev
            r = jax.nn.sigmoid(jnp.einsum('btc,dc->btd', xr, W_r))
            k = jnp.einsum('btc,dc->btd', xk, W_k)
            k_act = jnp.square(jax.nn.relu(k))
            out = r * jnp.einsum('btc,dc->btd', k_act, W_v)
            new_state = x[:, -1, :]
            return (out, new_state)
        return _reference_tuple_inner(x, W_r, W_k, W_v, mu_r, mu_k)[0]

    def _L1_xattn_ref(x, w1, w2):
        import jax, jax.numpy as jnp
        import numpy as np
        E, T, H, F = (8, 256, 256, 1024)
        h = jnp.einsum('eth,efh->etf', x, w1)
        g = jax.nn.gelu(h, approximate=True)
        out = jnp.einsum('etf,efh->eth', g, w2)
        return out

    def _L1_ffn_ref(x, w_router, w1, w2, w3):
        import jax, jax.numpy as jnp
        import numpy as np
        B, S, D = (4, 512, 256)
        E, K = (8, 2)
        H = 352
        bsz, seqlen, dim = x.shape
        xf = x.reshape(-1, dim)
        scores = jax.nn.softmax(xf @ w_router.T, axis=-1)
        expert_weights, expert_indices = jax.lax.top_k(scores, K)
        h = jax.nn.silu(jnp.einsum('td,edh->eth', xf, w1)) * jnp.einsum('td,edh->eth', xf, w3)
        y = jnp.einsum('eth,ehd->etd', h, w2)
        y_t = jnp.swapaxes(y, 0, 1)
        sel = jnp.take_along_axis(y_t, expert_indices[:, :, None], axis=1)
        out = jnp.sum(expert_weights[:, :, None] * sel, axis=1)
        return out.reshape(bsz, seqlen, dim)

    def _L2_xattn_ref(q, k, v, W, b, mask):
        import jax, jax.numpy as jnp
        import numpy as np
        HEAD_NUM = 16
        NEG_INF = float('-inf')
        B, Sq, D = q.shape
        Sk = k.shape[1]
        H = HEAD_NUM
        dh = D // H
        qh = q.reshape(B, Sq, H, dh).transpose(0, 2, 1, 3)
        kh = k.reshape(B, Sk, H, dh).transpose(0, 2, 1, 3)
        vh = v.reshape(B, Sk, H, dh).transpose(0, 2, 1, 3)
        scores = jnp.einsum('bhqd,bhkd->bhqk', qh, kh) / jnp.sqrt(jnp.asarray(dh, q.dtype))
        pad = mask[:, None, None, :]
        causal = jnp.triu(jnp.ones((Sq, Sk), dtype=jnp.int32), k=1)[None, None]
        merged = jnp.where(causal == 1, causal, pad)
        scores = jnp.where(merged == 1, NEG_INF, scores)
        attn = jax.nn.softmax(scores, axis=-1)
        out = jnp.einsum('bhqk,bhkd->bhqd', attn, vh)
        out = out.transpose(0, 2, 1, 3).reshape(B, Sq, D)
        return out @ W.T + b

    def _L2_ffn_ref(hidden_states, gate_w, shared_gate, shared_up, shared_down, r_gate, r_up, r_down):
        import jax, jax.numpy as jnp
        import numpy as np
        B, S, H, F, E = (1, 512, 256, 512, 8)

        def _swiglu(x, wg, wu, wd):
            return jax.nn.silu(x @ wg.T) * (x @ wu.T) @ wd.T
        b, s, h = hidden_states.shape
        x = hidden_states.reshape(-1, h)
        shared_out = _swiglu(x, shared_gate, shared_up, shared_down)
        logits = x @ gate_w.T
        top_id = jnp.argmax(logits, axis=-1)
        score = jax.nn.sigmoid(jnp.max(logits, axis=-1))
        xs = x * score[:, None]

        def body(acc, ws):
            wg, wu, wd, e = ws
            xe = jnp.where((top_id == e)[:, None], xs, 0.0)
            return (acc + _swiglu(xe, wg, wu, wd), None)
        acc0 = jnp.zeros_like(x)
        routed_out, _ = jax.lax.scan(body, acc0, (r_gate, r_up, r_down, jnp.arange(E)))
        return (shared_out + routed_out).reshape(b, s, h)

    def _L3_xattn_ref(queries, keys, values, Wq, Wk, Wv, Wo):
        import jax, jax.numpy as jnp
        import numpy as np
        NUM_HEADS = 16
        D_MODEL = 256
        NEG_INF = -1e+30

        def _split_heads(x, h):
            B, S, D = x.shape
            return x.reshape(B, S, h, D // h).transpose(0, 2, 1, 3)
        h = NUM_HEADS
        q = _split_heads(queries @ Wq, h)
        k = _split_heads(keys @ Wk, h)
        v = _split_heads(values @ Wv, h)
        dh = q.shape[-1]
        scores = jnp.einsum('bhqd,bhkd->bhqk', q, k) / jnp.sqrt(jnp.float32(dh))
        scores = jnp.where(scores == 0, NEG_INF, scores)
        attn = jax.nn.softmax(scores, axis=-1)
        out = jnp.einsum('bhqk,bhkd->bhqd', attn, v)
        B, _, S, _ = out.shape
        out = out.transpose(0, 2, 1, 3).reshape(B, S, h * dh)
        return out @ Wo

    def _L3_ffn_ref(x, weight_int8, weight_scale, bias):
        import jax, jax.numpy as jnp
        import numpy as np
        EPS = 1e-05
        B, S, K = x.shape
        x2 = x.reshape(-1, K)
        x_scale = jnp.maximum(jnp.abs(x2).max() / 127.0, EPS)
        x_int8 = jnp.clip(jnp.round(x2 / x_scale), -128, 127).astype(jnp.int8)
        acc_i32 = jax.lax.dot_general(x_int8, weight_int8.T, dimension_numbers=(((1,), (0,)), ((), ())), preferred_element_type=jnp.int32)
        out = acc_i32.astype(jnp.float32) * x_scale * weight_scale.T
        out = out + bias
        return out.reshape(B, S, -1)
    x = x + _L0_xattn_ref(_layernorm(x, axis=-1), ctx_1024, ctx_1024, mask_BxS2_ik0, fside_BxSxS2_0, L0_xattn_w_q, L0_xattn_b_q, L0_xattn_w_k, L0_xattn_b_k, L0_xattn_w_v, L0_xattn_b_v, L0_xattn_w_o, L0_xattn_b_o)
    x = x + _L0_ffn_ref(_layernorm(x, axis=-1), L0_ffn_W_r, L0_ffn_W_k, L0_ffn_W_v, L0_ffn_mu_r, L0_ffn_mu_k)
    x = x + _L1_xattn_ref(_layernorm(x, axis=-1), ctx_1024, ctx_1024)
    x = x + _L1_ffn_ref(_layernorm(x, axis=-1), L1_ffn_w_router, L1_ffn_w1, L1_ffn_w2, L1_ffn_w3)
    x = x + _L2_xattn_ref(_layernorm(x, axis=-1), ctx_1024, ctx_1024, L2_xattn_W, L2_xattn_b, mask_BxS2_if0)
    x = x + _L2_ffn_ref(_layernorm(x, axis=-1), L2_ffn_gate_w, L2_ffn_shared_gate, L2_ffn_shared_up, L2_ffn_shared_down, L2_ffn_r_gate, L2_ffn_r_up, L2_ffn_r_down)
    x = x + _L3_xattn_ref(_layernorm(x, axis=-1), ctx_1024, ctx_1024, L3_xattn_Wq, L3_xattn_Wk, L3_xattn_Wv, L3_xattn_Wo)
    x = x + _L3_ffn_ref(_layernorm(x, axis=-1), L3_ffn_weight_int8, L3_ffn_weight_scale, L3_ffn_bias)
    return x

_drawn_inputs = setup_inputs


def setup_inputs(seed=0):
    import zlib

    import numpy as np

    out = dict(_drawn_inputs(seed))
    spreads = {'L0_xattn_b_q': (0.0, 0.378),
     'L0_xattn_b_k': (0.0, 0.8),
     'L0_xattn_b_v': (0.0, 0.1),
     'L0_xattn_b_o': (0.0, 0.1),
     'L2_xattn_b': (0.0, 0.8)}
    factors = {'L0_ffn_W_r': 4.229,
     'L0_ffn_mu_r': 8.0,
     'L1_ffn_w_router': 8.0,
     'L1_ffn_w1': 8.0,
     'L1_ffn_w2': 8.0,
     'L1_ffn_w3': 8.0,
     'L2_xattn_W': 8.0,
     'L2_ffn_gate_w': 8.0,
     'L2_ffn_shared_gate': 8.0,
     'L2_ffn_shared_up': 8.0,
     'L2_ffn_shared_down': 8.0,
     'L2_ffn_r_gate': 8.0,
     'L2_ffn_r_up': 8.0,
     'L2_ffn_r_down': 8.0,
     'L3_xattn_Wq': 8.0,
     'L3_xattn_Wk': 8.0,
     'L3_xattn_Wv': 8.0,
     'L3_xattn_Wo': 8.0,
     'L3_ffn_weight_scale': 8.0,
     'L3_ffn_bias': 8.0}
    for name, (base, spread) in spreads.items():
        noise = np.random.default_rng([zlib.crc32(name.encode()), seed]).standard_normal(out[name].shape)
        drawn = base * np.exp(spread * noise) if base else spread * noise
        out[name] = jnp.asarray(drawn.astype(out[name].dtype))
    for name, factor in factors.items():
        out[name] = (out[name] * factor).astype(out[name].dtype)
    return out
```

```python
from contextlib import ExitStack

import numpy as np
import concourse.bass as bass
import concourse.mybir as mybir

F32 = mybir.dt.float32
BF16 = mybir.dt.bfloat16
I32 = mybir.dt.int32
I8 = mybir.dt.int8
U32 = mybir.dt.uint32
ALU = mybir.AluOpType
ACT = mybir.ActivationFunctionType
AX = mybir.AxisListType

P = 128
B, S, D = 8, 256, 256
SK = 77
DH = 16
G = D // P
HG = P // DH
T = S // P
NT = B * T
UNITS = G * T
E = 8
F1, F2 = 352, 512
EPS = 1e-5
NEG = -1e30
PAD = -1e9
ROUND = 12582912.0
KW = HG * SK
VW = HG * (P + DH)
EW = 3 * G * F2


def at_most(n, limit):
    return min(n, limit) if isinstance(n, int) else n


def after(engine, semaphore, count):
    if not isinstance(count, int) or count > 0:
        engine.wait_ge(semaphore, count)


def software_pipeline(engine, body, slots, depth, warm, batches=B):
    total = batches * slots
    for s in range(warm * slots):
        body(s // slots, s % slots, lambda lag, s=s: lag <= s)
    with engine.Fori(warm, batches) as b:
        for j in range(slots):
            body(b, j, lambda lag: True)
    for s in range(total, total + depth):
        body(s // slots, s % slots, lambda lag, s=s: s < total + lag)


def build(nc, a):
    with ExitStack() as ctx:
        def sb(name, shape, dt=F32):
            return ctx.enter_context(nc.sbuf_tensor(name, shape, dt))

        def sem(name):
            return ctx.enter_context(nc.semaphore(name))

        X = sb("X", [P, NT, D])
        XT = sb("XT", [P, B, G, S + 1])
        ctxT = sb("ctxT", [P, G, B * SK])
        W = sb("W", [P, 4, G, D])
        WE = sb("WE", [P, E * EW])
        ident = sb("ident", [P, P])
        headmask = sb("headmask", [P, HG])
        causal = sb("causal", [P, SK])
        vecs = sb("vecs", [P, 6, G])
        rows = sb("rows", [P, 2, D])
        halfpow = sb("halfpow", [P, T])
        mv = sb("mv", [P, T, 2])
        rstd = sb("rstd", [P, T])
        epsv = sb("epsv", [P, T])
        amax = sb("amax", [P, B])
        qsc = sb("qsc", [P, 4])
        iota8 = sb("iota8", [P, E])
        LG = sb("LG", [P, NT, E])
        PR = sb("PR", [P, NT, E])
        top = sb("top", [P, NT, 8])
        topi = sb("topi", [P, NT, 8], U32)
        topf = sb("topf", [P, NT, 2])
        hot = sb("hot", [P, NT, E])
        GATE = sb("GATE", [P, NT, E])
        score = sb("score", [P, NT])
        gsum = sb("gsum", [P, NT])
        WR = sb("WR", [P, G, E])
        VEND = E * EW - B * D
        V = WE[0:SK, VEND:].rearrange("k (b d) -> k b d", b=B)

        VP = sb("VP", [SK, G, VW])
        tmp = sb("tmp", [P, 7600])
        def carve(sizes):
            at, views = 0, []
            for n in sizes:
                views.append(tmp[:, at:at + n])
                at += n
            return views
        BIASf, MASKF, KTf, KBDf, SCf, PTf, QTf, OTf = carve(
            (NT * SK, B * SK, G * B * SK, G * KW, 2 * KW, HG * P, G * S, G * S))
        small = sb("small", [P, 3, 2, HG])
        XN = sb("XN", [P, T, D])
        st = sb("st", [P, T, 6])
        BIAS = BIASf.rearrange("p (n k) -> p n k", n=NT)
        Z = BIASf.rearrange("p (u k) -> p u k", u=2)
        KT = KTf.rearrange("p (g n) -> p g n", g=G)
        KBD = KBDf.rearrange("p (g n) -> p g n", g=G)
        SC = SCf.rearrange("p (u n) -> p u n", u=2)
        PT = PTf[0:SK]
        QT = QTf.rearrange("p (g s) -> p g s", g=G)
        OT = OTf.rearrange("p (g s) -> p g s", g=G)
        MASKI = KBDf[:, 0:B * SK].bitcast(I32)
        mx, sm, rs = small[:, 0], small[:, 1], small[:, 2]
        tAf, tBf, xrf, xkf, kreluf, ksqf, rsigf, rvf = carve((G * S,) * 8)
        halves = lambda f: f.rearrange("p (g s) -> p g s", g=G)
        tA, tB, xrT, xkT, krelu, ksq = map(halves, (tAf, tBf, xrf, xkf, kreluf, ksqf))
        rsig, rv = halves(rsigf), halves(rvf)
        ctxSf, gelf = carve((G * SK, S))
        ctxS = ctxSf.rearrange("p (g k) -> p g k", g=G)
        gel = gelf[0:SK]
        XSf, SLf, HHf, HTf = carve((2 * G * P, 2 * F2, 2 * F2, 2 * F2))
        XS = XSf.rearrange("p (u g s) -> p u g s", u=2, g=G)
        SL = SLf.rearrange("p (u f) -> p u f", u=2)
        HH = HHf.rearrange("p (u f) -> p u f", u=2)
        HT = HTf.rearrange("p (u c s) -> p u c s", u=2, s=P)
        LTs = carve((S,))[0][0:E]
        W8f, WBf, QAf, QBf, QIf, R1f = carve((G * D, G * D, G * S, G * S, G * S, G * S))
        W8 = W8f.bitcast(I8)[:, 0:G * D]
        WBF = WBf.bitcast(BF16)[:, 0:G * D].rearrange("p (g n) -> p g n", g=G)
        QI = QIf.bitcast(BF16)[:, 0:G * S].rearrange("p (g s) -> p g s", g=G)
        QA, QB, R1 = map(halves, (QAf, QBf, R1f))
        PS = ctx.enter_context(nc.psum_tensor("PS", [P, 8, 512], F32))
        BANK_PT, BANK_OT, BANK_X = 4, 6, 7

        x_loaded = sem("x_loaded"); ctx_loaded = sem("ctx_loaded"); small_loaded = sem("small_loaded")
        w_loaded = sem("w_loaded"); moe_loaded = sem("moe_loaded"); mask_loaded = sem("mask_loaded")
        last_loaded = sem("last_loaded"); const_ready = sem("const_ready"); stage_done = sem("stage_done")
        kt_psum = sem("kt_psum"); v_psum = sem("v_psum"); kt_ready = sem("kt_ready"); v_ready = sem("v_ready")
        q_psum = sem("q_psum"); q_ready = sem("q_ready"); kbd_ready = sem("kbd_ready"); vp_ready = sem("vp_ready")
        s_psum = sem("s_psum"); max_ready = sem("max_ready"); shifted = sem("shifted"); exp_done = sem("exp_done")
        rsum_ready = sem("rsum_ready"); p_ready = sem("p_ready"); pt_psum = sem("pt_psum"); pt_ready = sem("pt_ready")
        pv_done = sem("pv_done"); ot_ready = sem("ot_ready")
        o_psum = sem("o_psum"); stats_ready = sem("stats_ready"); xn_ready = sem("xn_ready")
        xt_psum = sem("xt_psum"); xt_ready = sem("xt_ready"); amax_ready = sem("amax_ready")
        prev_ready = sem("prev_ready"); mixed = sem("mixed"); r_psum = sem("r_psum"); k_psum = sem("k_psum")
        r_ready = sem("r_ready"); krelu_ready = sem("krelu_ready"); ksq_ready = sem("ksq_ready")
        ctxs_ready = sem("ctxs_ready"); g_psum = sem("g_psum"); g_ready = sem("g_ready")
        lt_psum = sem("lt_psum"); lt_ready = sem("lt_ready"); lg_psum = sem("lg_psum"); lg_ready = sem("lg_ready")
        route_dve = sem("route_dve"); route_act = sem("route_act")
        xs_ready = sem("xs_ready"); h_psum = sem("h_psum"); silu_ready = sem("silu_ready"); hh_ready = sem("hh_ready")
        ht_psum = sem("ht_psum"); ht_ready = sem("ht_ready"); y_psum = sem("y_psum"); y_added = sem("y_added")
        qi_ready = sem("qi_ready"); f_psum = sem("f_psum"); f_taken = sem("f_taken")
        part_amax = sem("part_amax"); all_amax = sem("all_amax"); w8_ready = sem("w8_ready")
        held = sem("held"); x_final = sem("x_final"); stored = sem("stored")
        block = ctx.enter_context(nc.Block())

        def end_stage(engine, name):
            engine.drain().then_inc(stage_done, 1)
            engine.wait_ge(stage_done, 4 * ST[name])

        def hold(engine):
            engine.nop().then_inc(held, 1)

        def xt_of(b):
            return XT[:, bass.ds(b, 1), :, 1:S + 1].rearrange("p o g s -> p (o g) s")

        def x_of(b):
            return X[:, bass.ds(b * T, T), :]

        def repeat(ap, n):
            return ap.unsqueeze(1).to_broadcast([ap.shape[0], n, ap.shape[1]])

        def spread(ap, n):
            return ap.unsqueeze(2).to_broadcast([ap.shape[0], ap.shape[1], n])

        def l1_w(e, k):
            base = e * (2 * G * F1 + 3 * D) + k * G * F1
            return WE[:, base:base + G * F1].rearrange("p (g f) -> p g f", g=G)

        def l1_wd(e):
            base = e * (2 * G * F1 + 3 * D) + 2 * G * F1
            return WE[:, base:base + 3 * D].rearrange("p (c d) -> p c d", c=3)

        def l2_w(e, k):
            base = e * EW + k * G * F2
            return WE[:, base:base + G * F2].rearrange("p (g f) -> p g f", g=G)

        def l2_wd(e):
            base = e * EW + 2 * G * F2
            return WE[:, base:base + 4 * D].rearrange("p (c d) -> p c d", c=4)

        ST = {n: i + 1 for i, n in enumerate(
            ("setup", "a0", "f0", "m1", "r1", "e1", "n4", "a2", "r2", "s2", "e2", "n6", "a3", "q3"))}
        NORM = dict(setup=0, a0=8, f0=16, m1=24, n4=32, a2=40, n6=48, a3=56)
        SUM = dict(a0=0, f0=8, m1=16, a2=24, a3=32)
        LAYER = dict(a0=0, a2=1, a3=2)
        MOE = dict(e1=(E, F1, 0, 0), s2=(1, F2, NT * E, NT), e2=(E, F2, NT * E + NT, 2 * NT))
        L1_DMAS = 4 * E
        MOE_LOADED = dict(e1=16 * L1_DMAS, s2=16 * (L1_DMAS + 3 * E), e2=16 * (L1_DMAS + 3 * E + 3))

        @block.sync
        def _(sp):
            def square(k, name):
                sp.dma_start(W[:, k], a[name].rearrange("(g p) n -> p g n", p=P)).then_inc(w_loaded, 16)

            def everywhere(dst, name, semaphore):
                sp.dma_start(dst, a[name].partition_broadcast(P)).then_inc(semaphore, 16)

            sp.dma_start(X[:, :, :], a["x"].rearrange("b (t p) d -> p (b t) d", p=P)).then_inc(x_loaded, 16)
            sp.dma_start(ctxT[:, :, :], a["ctxT"].rearrange("(g p) n -> p g n", p=P)).then_inc(ctx_loaded, 16)
            for k, name in enumerate(("L0_wqT", "L0_wkT", "L0_wvT", "L0_woT")):
                square(k, name)
            sp.dma_start(vecs[:, 0:4], a["L0_vecs"]).then_inc(small_loaded, 16)
            everywhere(rows[:, 0], "L0_bv", small_loaded)
            everywhere(rows[:, 1], "L0_bo", small_loaded)
            everywhere(MASKI, "mask0", small_loaded)
            sp.dma_start(BIAS, a["bias"].rearrange("b (t p) k -> p (b t) k", p=P)).then_inc(small_loaded, 16)
            for e in range(E):
                for k, name in enumerate(("L1_w1", "L1_w3")):
                    sp.dma_start(l1_w(e, k), a[name][e].rearrange("(g p) f -> p g f", p=P)).then_inc(moe_loaded, 16)
                w2 = a["L1_w2"][e]
                sp.dma_start(l1_wd(e)[:, 0:2], w2[0:2 * P].rearrange("(c p) d -> p c d", p=P)).then_inc(moe_loaded, 16)
                sp.dma_start(l1_wd(e)[0:F1 - 2 * P, 2], w2[2 * P:F1]).then_inc(moe_loaded, 16)
            sp.wait_ge(stage_done, 4 * ST["a0"])
            for k, name in enumerate(("L0_WrT", "L0_WkT", "L0_WvT")):
                square(k, name)
            sp.dma_start(V, a["ctx"].rearrange("b k d -> k b d")).then_inc(ctx_loaded, 16)
            sp.wait_ge(stage_done, 4 * ST["f0"])
            square(0, "L2_WT")
            sp.dma_start(WR[:, :, :], a["L1_wrT"].rearrange("(g p) n -> p g n", p=P)).then_inc(w_loaded, 16)
            sp.wait_ge(stage_done, 4 * ST["e1"])
            everywhere(rows[:, 1], "L2_b", mask_loaded)
            everywhere(MASKI, "mask2", mask_loaded)
            sp.dma_start(WR[:, :, :], a["L2_gateT"].rearrange("(g p) n -> p g n", p=P)).then_inc(mask_loaded, 16)
            for e in range(E - 1):
                for k, name in enumerate(("L2_rgT", "L2_ruT")):
                    sp.dma_start(l2_w(e, k), a[name][e].rearrange("(g p) f -> p g f", p=P)).then_inc(moe_loaded, 16)
                sp.dma_start(l2_wd(e), a["L2_rdT"][e].rearrange("(c p) d -> p c d", p=P)).then_inc(moe_loaded, 16)
            sp.wait_ge(stage_done, 4 * ST["a2"])
            for k, name in enumerate(("L2_sgT", "L2_suT")):
                sp.dma_start(l2_w(E - 1, k), a[name].rearrange("(g p) f -> p g f", p=P)).then_inc(moe_loaded, 16)
            sp.dma_start(l2_wd(E - 1), a["L2_sdT"].rearrange("(c p) d -> p c d", p=P)).then_inc(moe_loaded, 16)
            for k, name in enumerate(("L3_Wq", "L3_Wk", "L3_Wv", "L3_Wo")):
                square(k, name)
            sp.wait_ge(stage_done, 4 * ST["s2"])
            for k, name in enumerate(("L2_rgT", "L2_ruT")):
                sp.dma_start(l2_w(E - 1, k), a[name][E - 1].rearrange("(g p) f -> p g f", p=P)).then_inc(moe_loaded, 16)
            sp.dma_start(l2_wd(E - 1), a["L2_rdT"][E - 1].rearrange("(c p) d -> p c d", p=P)).then_inc(moe_loaded, 16)
            sp.wait_ge(stage_done, 4 * ST["a3"])
            sp.dma_start(W8f.bitcast(I32)[:, 0:G * D // 4].rearrange("p (g n) -> p g n", g=G),
                         a["L3_w8T"].rearrange("(g p) n -> p g n", p=P)).then_inc(last_loaded, 16)
            everywhere(rows[:, 0], "L3_ws", last_loaded)
            everywhere(rows[:, 1], "L3_bias", last_loaded)
            with sp.Fori(0, B) as b:
                sp.wait_ge(x_final, b + 1)
                sp.dma_start(a["out"][bass.ds(b, 1)].rearrange("o (t p) d -> p (o t) d", p=P), x_of(b)).then_inc(stored, 16)
            sp.wait_ge(stored, 16 * B)

        @block.gpsimd
        def _(pool):
            def norm_rows(n, b, amax_of=None):
                pool.wait_ge(stats_ready, n + 1)
                after(pool, xt_psum, n)
                if amax_of is not None:
                    after(pool, amax_ready, b)
                pool.tensor_tensor(rstd[:, :], mv[:, :, 1], epsv[:, :], ALU.add)
                pool.drain()
                pool.tensor_tensor(rstd[:, :], rstd[:, :], halfpow[:, :], ALU.pow)
                pool.tensor_tensor(XN[:, :, :], x_of(b), mv[:, :, 0:1].to_broadcast([P, T, D]), ALU.subtract)
                pool.drain()
                pool.tensor_tensor(XN[:, :, :], XN[:, :, :], spread(rstd[:, :], D), ALU.mult).then_inc(xn_ready, 1)

            def attention(stage, keys):
                layer, norms = LAYER[stage], NORM[stage]
                u0 = B * UNITS * layer

                def block_diagonal_keys(b, g):
                    after(pool, s_psum, u0 + UNITS * b - 2 + 2 * g)
                    k = keys[:, g, bass.ds(b * SK, SK)]
                    pool.tensor_tensor(KBD[:, g].rearrange("p (h k) -> p h k", h=HG), repeat(k, HG),
                                       spread(headmask[:, :], SK), ALU.mult).then_inc(kbd_ready, 1)

                def pad_values(b, g):
                    after(pool, pv_done, u0 + UNITS * b - 2 + 2 * g)
                    v = V[:, bass.ds(b, 1), g * P:(g + 1) * P].rearrange("k o (h d) -> k (o h) d", h=HG)
                    pool.tensor_copy(VP[:, g].rearrange("k (h n) -> k h n", h=HG)[:, :, 0:DH], v).then_inc(vp_ready, 1)

                def body(b, j, live):
                    if j == 0 and live(0):
                        block_diagonal_keys(b, 0)
                    if j == 1 and live(1):
                        block_diagonal_keys(b, 1)
                    if live(1):
                        u, q = u0 + UNITS * b + j - 1, (j - 1) % 2
                        pool.wait_ge(max_ready, u + 1)
                        s = SC[:, q].rearrange("p (h k) -> p h k", h=HG)
                        pool.tensor_tensor(s, s, spread(mx[:, q], SK), ALU.subtract).then_inc(shifted, 1)
                    if j == 2 and live(2):
                        pad_values(b, 0)
                    if j == 0 and live(4):
                        pad_values(b - 1, 1)
                    if live(2):
                        u, q = u0 + UNITS * b + j - 2, j % 2
                        pool.wait_ge(rsum_ready, u + 1)
                        s = SC[:, q].rearrange("p (h k) -> p h k", h=HG)
                        pool.tensor_tensor(s, s, spread(rs[:, q], SK), ALU.mult).then_inc(p_ready, 1)
                    if j == 1 and live(9):
                        norm_rows(norms + b - 2, b - 2, amax if stage == "a3" else None)

                software_pipeline(pool, body, UNITS, 10, 2)

            pool.memset(epsv[:, :], EPS)
            pool.memset(halfpow[:, :], -0.5)
            pool.memset(ident[:, :], 0.0)
            pool.memset(headmask[:, :], 1.0)
            pool.memset(causal[:, :], 0.0)
            pool.memset(VP[:, :, :], 0.0)
            pool.memset(XT[:, :, :, 0:1], 0.0)
            for e in range(E):
                pool.memset(iota8[:, e:e + 1], float(e))
            pool.drain()
            pool.affine_select(out=ident[:, :], in_=ident[:, :], compare_op=ALU.not_equal, fill=1.0, base=0,
                               pattern=[[-1, P]], channel_multiplier=1)
            pool.affine_select(out=headmask[:, :], in_=headmask[:, :], compare_op=ALU.is_ge, fill=0.0, base=0,
                               pattern=[[-DH, HG]], channel_multiplier=1)
            pool.affine_select(out=causal[:, :], in_=causal[:, :], compare_op=ALU.is_ge, fill=NEG, base=0,
                               pattern=[[-1, SK]], channel_multiplier=1)
            pool.drain()
            pool.affine_select(out=headmask[:, :], in_=headmask[:, :], compare_op=ALU.is_ge, fill=0.0, base=DH - 1,
                               pattern=[[DH, HG]], channel_multiplier=-1)
            pool.drain().then_inc(const_ready, 1)
            pool.wait_ge(x_loaded, 16)

            def plain_norm(stage):
                norm_rows(NORM[stage], 0)
                with pool.Fori(1, B) as b:
                    norm_rows(NORM[stage] + b, b)

            plain_norm("setup")
            end_stage(pool, "setup")
            attention("a0", KT)
            end_stage(pool, "a0")

            def ffn_body(b, j, live):
                if live(0):
                    after(pool, mixed, b)
                    for dst, k in ((tA, 4), (tB, 5)):
                        for g in range(G):
                            prev = XT[:, bass.ds(b, 1), g, 0:S].rearrange("p o s -> p (o s)")
                            last = pool.tensor_tensor(dst[:, g], prev, vecs[:, k, g:g + 1].to_broadcast([P, S]), ALU.mult)
                    last.then_inc(prev_ready, 1)
                if live(1):
                    pool.wait_ge(krelu_ready, b)
                    after(pool, o_psum, SUM["f0"] + b - 1)
                    pool.tensor_tensor(ksq, krelu, krelu, ALU.mult).then_inc(ksq_ready, 1)
                    norm_rows(NORM["f0"] + b - 1, b - 1)

            software_pipeline(pool, ffn_body, 1, 2, 2)
            end_stage(pool, "f0")

            def mlp_body(b, j, live):
                if live(0):
                    after(pool, g_psum, b)
                    pool.tensor_copy(ctxS, ctxT[:, :, bass.ds(b * SK, SK)]).then_inc(ctxs_ready, 1)
                if live(1):
                    norm_rows(NORM["m1"] + b - 1, b - 1)

            software_pipeline(pool, mlp_body, 1, 2, 2)
            end_stage(pool, "m1")
            end_stage(pool, "r1")

            def moe(stage):
                experts, _, u0, x0 = MOE[stage]

                def body(b, j, live):
                    if live(0) and j % experts == 0:
                        t = j // experts
                        after(pool, h_psum, u0 + (T * b + t - 1) * experts)
                        src = XT[:, bass.ds(b, 1), :, 1 + t * P:1 + (t + 1) * P].rearrange("p o g s -> p (o g) s")
                        pool.tensor_copy(XS[:, t], src).then_inc(xs_ready, 1)

                software_pipeline(pool, body, T * experts, 0, 1)
                end_stage(pool, stage)

            moe("e1")
            plain_norm("n4")
            end_stage(pool, "n4")
            attention("a2", ctxT)
            end_stage(pool, "a2")
            end_stage(pool, "r2")
            moe("s2")
            moe("e2")
            plain_norm("n6")
            end_stage(pool, "n6")
            attention("a3", KT)
            end_stage(pool, "a3")
            pool.wait_ge(part_amax, 1)
            pool.partition_all_reduce(qsc[:, 1:2], qsc[:, 0:1], P, bass.bass_isa.ReduceOp.max).then_inc(all_amax, 1)
            end_stage(pool, "q3")

        @block.scalar
        def _(act):
            def xt_evacuate(n, b):
                act.wait_ge(xt_psum, n + 1)
                hold(act)
                act.activation(xt_of(b), PS[:, BANK_X].rearrange("p (g s) -> p g s", g=G), ACT.Copy).then_inc(xt_ready, 1)

            def plain_norm(stage):
                with act.Fori(0, B) as b:
                    xt_evacuate(NORM[stage] + b, b)

            def keys_evacuate(first, bias):
                for g in range(G):
                    act.wait_ge(kt_psum, first + g + 1)
                    dst = KT[:, g].rearrange("p (i n) -> p i n", i=2)
                    src = PS[:, 2 * g:2 * g + 2, 0:KW // 2]
                    if bias:
                        act.activation(dst, src, ACT.Identity, bias=vecs[:, 1, g:g + 1]).then_inc(kt_ready, 1)
                    else:
                        act.activation(dst, src, ACT.Copy).then_inc(kt_ready, 1)

            def attention(stage):
                layer, norms = LAYER[stage], NORM[stage]
                u0, b0 = B * UNITS * layer, B * layer

                def body(b, j, live):
                    if j == 0 and live(8):
                        act.wait_ge(pv_done, u0 + UNITS * (b - 1))
                        after(act, o_psum, SUM[stage] + b - 2)
                        act.activation(OT, PS[:, BANK_OT].rearrange("p (g s) -> p g s", g=G), ACT.Copy).then_inc(ot_ready, 1)
                    if j == 0 and live(0):
                        after(act, s_psum, u0 + UNITS * b)
                        hold(act)
                        if stage == "a2":
                            act.activation(QT, xt_of(b), ACT.Copy, scale=DH ** -0.5).then_inc(q_ready, 1)
                        else:
                            n_q = q0 + b
                            act.wait_ge(q_psum, n_q + 1)
                            for g in range(G):
                                src = PS[:, BANK_X, g * S:(g + 1) * S]
                                if stage == "a0":
                                    last = act.activation(QT[:, g], src, ACT.Identity, scale=DH ** -0.5,
                                                          bias=vecs[:, 0, g:g + 1])
                                else:
                                    last = act.activation(QT[:, g], src, ACT.Copy, scale=DH ** -0.5)
                            last.then_inc(q_ready, 1)
                    if live(2):
                        u, q = u0 + UNITS * b + j - 2, j % 2
                        act.wait_ge(shifted, u + 1)
                        act.activation(SC[:, q], SC[:, q], ACT.Exp).then_inc(exp_done, 1)
                    if live(3):
                        u = u0 + UNITS * b + j - 3
                        act.wait_ge(pt_psum, u + 1)
                        after(act, pv_done, u)
                        act.activation(PT.rearrange("k (i n) -> k i n", i=2), PS[0:SK, BANK_PT:BANK_PT + 2],
                                       ACT.Copy).then_inc(pt_ready, 1)
                    if j == 2 and live(10):
                        xt_evacuate(norms + b - 2, b - 2)

                q0 = 0 if stage == "a0" else B
                software_pipeline(act, body, UNITS, 11, 2)
                end_stage(act, stage)

            act.wait_ge(small_loaded, 16 * 5)
            keys_evacuate(0, True)
            plain_norm("setup")
            end_stage(act, "setup")
            attention("a0")

            def ffn_body(b, j, live):
                if live(0):
                    act.wait_ge(k_psum, b + 1)
                    after(act, ksq_ready, b)
                    act.activation(krelu, PS[:, 1].rearrange("p (g s) -> p g s", g=G), ACT.Relu).then_inc(krelu_ready, 1)
                    act.wait_ge(r_psum, b + 1)
                    act.wait_ge(stats_ready, NORM["f0"] + b)
                    act.activation(rsig, PS[:, 0].rearrange("p (g s) -> p g s", g=G), ACT.Sigmoid).then_inc(r_ready, 1)
                if live(2):
                    xt_evacuate(NORM["f0"] + b - 2, b - 2)

            software_pipeline(act, ffn_body, 1, 2, 2)
            end_stage(act, "f0")

            def mlp_body(b, j, live):
                if live(0):
                    act.wait_ge(g_psum, b + 1)
                    act.wait_ge(o_psum, SUM["m1"] + b)
                    act.activation(gel, PS[0:SK, 0, 0:S], ACT.Gelu_apprx_tanh).then_inc(g_ready, 1)
                if live(2):
                    xt_evacuate(NORM["m1"] + b - 2, b - 2)

            software_pipeline(act, mlp_body, 1, 2, 2)
            end_stage(act, "m1")

            def route(stage, first):
                with act.Fori(0, B) as b:
                    act.wait_ge(lt_psum, first + b + 1)
                    after(act, lg_psum, first + b)
                    act.activation(LTs, PS[0:E, 0, 0:S], ACT.Copy).then_inc(lt_ready, 1)
                act.wait_ge(route_dve, 1 if stage == "r1" else 2)
                if stage == "r1":
                    act.activation(PR[:, :, :], LG[:, :, :], ACT.Exp).then_inc(route_act, 1)
                else:
                    act.activation(score[:, :], top[:, :, 0], ACT.Sigmoid).then_inc(route_act, 1)
                end_stage(act, stage)

            def moe(stage):
                experts, F, u0, _ = MOE[stage]
                chunks = -(-F // P)

                def body(b, j, live):
                    if live(0):
                        u, q, t = u0 + T * experts * b + j, j % 2, j // experts
                        act.wait_ge(h_psum, u + 1)
                        after(act, hh_ready, u - 1)
                        s = score[:, bass.ds(T * b + t, 1)] if stage == "e2" else 1.0
                        hold(act)
                        act.activation(SL[:, q, 0:F], PS[:, 2 * q, 0:F], ACT.Silu, scale=s).then_inc(silu_ready, 1)
                    if live(1):
                        u, q = u0 + T * experts * b + j - 1, (j - 1) % 2
                        act.wait_ge(ht_psum, u + 1)
                        after(act, y_psum, u - 1)
                        for c in range(chunks):
                            n = min(P, F - c * P)
                            if n < P or c == chunks - 1:
                                act.activation(HT[0:n, q, c], PS[0:n, 4 + q, c * P:(c + 1) * P], ACT.Copy).then_inc(ht_ready, 1)
                            elif c == 0:
                                act.activation(HT[:, q, 0:chunks - 1],
                                               PS[:, 4 + q, 0:(chunks - 1) * P].rearrange("p (c s) -> p c s", s=P), ACT.Copy)

                software_pipeline(act, body, T * experts, 1, 1)
                end_stage(act, stage)

            route("r1", 0)
            moe("e1")
            plain_norm("n4")
            end_stage(act, "n4")
            attention("a2")
            route("r2", B)
            moe("s2")
            moe("e2")
            keys_evacuate(G, False)
            plain_norm("n6")
            end_stage(act, "n6")
            attention("a3")
            end_stage(act, "q3")

        @block.vector
        def _(dve):
            def add_sum(stage, b, bank=BANK_X, row=None, times=None):
                if row is not None:
                    dve.tensor_tensor(x_of(b), x_of(b), repeat(row, T), ALU.add)
                    dve.drain()
                dve.wait_ge(o_psum, SUM[stage] + b + 1)
                result = PS[:, bank].rearrange("p (t d) -> p t d", t=T)
                if times is not None:
                    dve.tensor_tensor(rv, result, times, ALU.mult)
                    dve.drain()
                    result = rv
                dve.tensor_tensor(x_of(b), x_of(b), result, ALU.add)
                dve.drain()

            def row_stats(n, b):
                dve.drain()
                for t in range(T):
                    dve.bn_stats(st[:, t], X[:, bass.ds(b * T + t, 1), :].rearrange("p o d -> p (o d)"))
                after(dve, xn_ready, n)
                hold(dve)
                dve.drain()
                for t in range(T):
                    last = dve.bn_aggr(mv[:, t], st[:, t])
                last.then_inc(stats_ready, 1)

            def plain_norm(stage):
                with dve.Fori(0, B) as b:
                    row_stats(NORM[stage] + b, b)

            def values_evacuate(first, bias):
                for i in range(4):
                    dve.wait_ge(v_psum, first + i + 1)
                    src = PS[0:SK, (4, 5, 6, 0)[i]].rearrange("k (b d) -> k b d", b=2)
                    if bias:
                        last = dve.tensor_tensor(V[:, 2 * i:2 * i + 2], src, repeat(rows[0:SK, 0], 2), ALU.add)
                    else:
                        last = dve.tensor_copy(V[:, 2 * i:2 * i + 2], src)
                last.then_inc(v_ready, 1)

            def attention(stage):
                layer, norms = LAYER[stage], NORM[stage]
                u0 = B * UNITS * layer

                def body(b, j, live):
                    if live(2):
                        u, q = u0 + UNITS * b + j - 2, j % 2
                        dve.wait_ge(exp_done, u + 1)
                        after(dve, p_ready, u - 1)
                        dve.tensor_reduce(sm[:, q], SC[:, q].rearrange("p (h k) -> p h k", h=HG), AX.X, ALU.add)
                        dve.drain()
                        dve.reciprocal(rs[:, q], sm[:, q]).then_inc(rsum_ready, 1)
                    if live(1):
                        u, q, t = u0 + UNITS * b + j - 1, (j - 1) % 2, (j - 1) % T
                        bt = b if j >= 1 else b - 1
                        dve.wait_ge(s_psum, u + 1)
                        after(dve, pt_psum, u - 1)
                        s = PS[:, 2 * q:2 * q + 2, 0:KW // 2]
                        if stage == "a3":
                            z = Z[:, q].rearrange("p (i n) -> p i n", i=2)
                            dve.tensor_scalar(z, s, 0.0, NEG, ALU.is_equal, ALU.mult)
                            dve.drain()
                            dve.tensor_tensor(SC[:, q].rearrange("p (i n) -> p i n", i=2), s, z, ALU.add)
                        else:
                            bias = BIAS[:, bass.ds(T * bt + t, 1), :].unsqueeze(1).to_broadcast([P, 2, HG // 2, SK])
                            dve.tensor_tensor(SC[:, q].rearrange("p (i h k) -> p i h k", i=2, k=SK),
                                              s.rearrange("p i (h k) -> p i h k", k=SK), bias, ALU.add)
                        dve.drain()
                        dve.tensor_reduce(mx[:, q], SC[:, q].rearrange("p (h k) -> p h k", h=HG), AX.X,
                                          ALU.max).then_inc(max_ready, 1)
                    if j == 1 and live(9):
                        add_sum(stage, b - 2, row=None if stage == "a3" else rows[:, 1])
                        row_stats(norms + b - 2, b - 2)
                    if stage == "a3" and j == 2 and live(10):
                        dve.wait_ge(xn_ready, norms + b - 1)
                        dve.tensor_reduce(amax[:, bass.ds(b - 2, 1)], XN[:, :, :], AX.XY, ALU.max,
                                          apply_absolute_value=True).then_inc(amax_ready, 1)

                software_pipeline(dve, body, UNITS, 11, 2)
                end_stage(dve, stage)

            dve.wait_ge(small_loaded, 16 * 5)
            dve.tensor_scalar(MASKF, MASKI, 0, None, ALU.not_equal)
            dve.tensor_scalar(vecs[:, 4:6], vecs[:, 2:4], -1.0, 1.0, ALU.mult, ALU.add)
            dve.drain()
            pad = KBDf[:, B * SK:2 * B * SK]
            dve.tensor_scalar(pad, MASKF, -1.0, -PAD, ALU.add, ALU.mult)
            bias4 = BIASf.rearrange("p (b t k) -> p b t k", b=B, t=T)
            by_tile = lambda ap: ap.rearrange("p (b k) -> p b k", b=B).unsqueeze(2).to_broadcast([P, B, T, SK])
            dve.tensor_tensor(bias4, bias4, by_tile(MASKF), ALU.mult)
            dve.drain()
            dve.tensor_tensor(bias4, bias4, by_tile(pad), ALU.add)
            values_evacuate(0, True)
            dve.wait_ge(kt_ready, G)
            dve.tensor_tensor(KT, KT, repeat(MASKF, G), ALU.mult)
            dve.tensor_scalar(vecs[:, 0], vecs[:, 0], DH ** -0.5, None, ALU.mult)
            dve.wait_ge(x_loaded, 16)
            plain_norm("setup")
            end_stage(dve, "setup")
            attention("a0")

            def ffn_body(b, j, live):
                if live(0):
                    dve.wait_ge(prev_ready, b + 1)
                    after(dve, k_psum, b)
                    for dst, prev, k in ((xrT, tA, 2), (xkT, tB, 3)):
                        for g in range(G):
                            now = XT[:, bass.ds(b, 1), g, 1:S + 1].rearrange("p o s -> p (o s)")
                            last = dve.scalar_tensor_tensor(out=dst[:, g], in0=now, scalar=vecs[:, k, g:g + 1],
                                                            in1=prev[:, g], op0=ALU.mult, op1=ALU.add)
                    last.then_inc(mixed, 1)
                if live(1):
                    dve.wait_ge(r_ready, b)
                    add_sum("f0", b - 1, bank=6, times=rsig)
                    row_stats(NORM["f0"] + b - 1, b - 1)

            software_pipeline(dve, ffn_body, 1, 2, 2)
            end_stage(dve, "f0")

            def mlp_body(b, j, live):
                if live(1):
                    add_sum("m1", b - 1, bank=6)
                    row_stats(NORM["m1"] + b - 1, b - 1)

            software_pipeline(dve, mlp_body, 1, 2, 2)
            end_stage(dve, "m1")

            def choose(k):
                i = topf[:, :, k:k + 1].to_broadcast([P, NT, E])
                dve.tensor_tensor(hot[:, :, :], i, iota8[:, :].unsqueeze(1).to_broadcast([P, NT, E]), ALU.is_equal)
                dve.drain()

            def route(stage, first):
                with dve.Fori(0, B) as b:
                    dve.wait_ge(lg_psum, first + b + 1)
                    dve.tensor_copy(LG[:, bass.ds(T * b, T), :], PS[:, 1, 0:T * E].rearrange("p (t e) -> p t e", t=T)).then_inc(lg_ready, 1)
                dve.drain()
                for t in range(NT):
                    dve.max(top[:, t], LG[:, t])
                dve.drain()
                for t in range(NT):
                    dve.max_index(topi[:, t], top[:, t], LG[:, t])
                dve.drain()
                dve.tensor_copy(topf[:, :, :], topi[:, :, 0:2])
                if stage == "r1":
                    dve.tensor_tensor(LG[:, :, :], LG[:, :, :], top[:, :, 0:1].to_broadcast([P, NT, E]), ALU.subtract)
                dve.drain().then_inc(route_dve, 1)
                choose(0)
                dve.tensor_copy(GATE[:, :, :], hot[:, :, :])
                if stage == "r1":
                    dve.drain()
                    choose(1)
                    dve.tensor_tensor(GATE[:, :, :], GATE[:, :, :], hot[:, :, :], ALU.add)
                    dve.wait_ge(route_act, 1)
                    dve.tensor_reduce(gsum[:, :], PR[:, :, :], AX.X, ALU.add)
                    dve.drain()
                    dve.reciprocal(gsum[:, :], gsum[:, :])
                    dve.tensor_tensor(GATE[:, :, :], GATE[:, :, :], PR[:, :, :], ALU.mult)
                    dve.drain()
                    dve.tensor_tensor(GATE[:, :, :], GATE[:, :, :], gsum[:, :].unsqueeze(2).to_broadcast([P, NT, E]), ALU.mult)
                end_stage(dve, stage)

            def moe(stage):
                experts, F, u0, _ = MOE[stage]

                def body(b, j, live):
                    if live(0):
                        u, q, t = u0 + T * experts * b + j, j % 2, j // experts
                        dve.wait_ge(silu_ready, u + 1)
                        after(dve, ht_psum, u - 1)
                        s = score[:, bass.ds(T * b + t, 1)] if stage == "e2" else 1.0
                        dve.scalar_tensor_tensor(out=HH[:, q, 0:F], in0=PS[:, 2 * q + 1, 0:F], scalar=s,
                                                 in1=SL[:, q, 0:F], op0=ALU.mult, op1=ALU.mult).then_inc(hh_ready, 1)
                    if live(2):
                        j2 = j - 2
                        u, q = u0 + T * experts * b + j2, j % 2
                        bb = b if j2 >= 0 else b - 1
                        t, e = (j2 % (T * experts)) // experts, j2 % experts
                        dve.wait_ge(y_psum, u + 1)
                        x = X[:, bass.ds(T * bb + t, 1), :].rearrange("p o d -> p (o d)")
                        y = PS[:, 6 + q, 0:D]
                        if experts == 1:
                            dve.tensor_tensor(x, x, y, ALU.add).then_inc(y_added, 1)
                        else:
                            g = GATE[:, bass.ds(T * bb + t, 1), e:e + 1].rearrange("p o e -> p (o e)")
                            dve.scalar_tensor_tensor(out=x, in0=y, scalar=g, in1=x, op0=ALU.mult,
                                                     op1=ALU.add).then_inc(y_added, 1)
                        dve.drain()

                software_pipeline(dve, body, T * experts, 2, 1)
                end_stage(dve, stage)

            route("r1", 0)
            moe("e1")
            dve.wait_ge(mask_loaded, 16 * 3)
            dve.tensor_scalar(MASKF, MASKI, 1, NEG, ALU.is_equal, ALU.mult)
            dve.drain()
            dve.tensor_copy(bias4, by_tile(MASKF))
            dve.drain()
            dve.tensor_tensor(bias4[:, :, 0], bias4[:, :, 0], causal[:, :].unsqueeze(1).to_broadcast([P, B, SK]), ALU.add)
            plain_norm("n4")
            end_stage(dve, "n4")
            attention("a2")
            route("r2", B)
            moe("s2")
            moe("e2")
            values_evacuate(4, False)
            plain_norm("n6")
            end_stage(dve, "n6")
            attention("a3")
            dve.tensor_reduce(qsc[:, 0:1], amax[:, :], AX.X, ALU.max).then_inc(part_amax, 1)
            dve.wait_ge(last_loaded, 16 * 3)
            dve.tensor_copy(WBf.bitcast(BF16)[:, 0:G * D], W8).then_inc(w8_ready, 1)
            dve.wait_ge(all_amax, 1)
            dve.tensor_scalar(qsc[:, 2:3], qsc[:, 1:2], 1.0 / 127.0, EPS, ALU.mult, ALU.max)
            dve.drain()
            dve.reciprocal(qsc[:, 3:4], qsc[:, 2:3])
            dve.drain()

            def quant_body(b, j, live):
                if live(0):
                    dve.tensor_scalar(QA, xt_of(b), qsc[:, 3:4], 127.0, ALU.mult, ALU.min)
                    dve.drain()
                    dve.tensor_scalar(QB, QA, -128.0, ROUND, ALU.max, ALU.add)
                    dve.drain()
                    after(dve, f_psum, b)
                    dve.tensor_scalar(QI, QB, -ROUND, None, ALU.add).then_inc(qi_ready, 1)
                if live(1):
                    dve.wait_ge(f_psum, b)
                    dve.scalar_tensor_tensor(out=R1, in0=PS[:, 0].rearrange("p (t d) -> p t d", t=T),
                                             scalar=qsc[:, 2:3], in1=repeat(rows[:, 0], T),
                                             op0=ALU.mult, op1=ALU.mult).then_inc(f_taken, 1)
                    dve.drain()
                    dve.tensor_tensor(R1, R1, repeat(rows[:, 1], T), ALU.add)
                    dve.drain()
                    dve.tensor_tensor(x_of(b - 1), x_of(b - 1), R1, ALU.add).then_inc(x_final, 1)
                    dve.drain()

            software_pipeline(dve, quant_body, 1, 1, 1)
            end_stage(dve, "q3")

        @block.tensor
        def _(pe):
            def transpose_rows(n):
                pe.wait_ge(xn_ready, n + 1)
                for g in range(G):
                    for t in range(T):
                        last = pe.transpose(PS[:, BANK_X, g * S + t * P:g * S + (t + 1) * P],
                                            XN[:, t, g * P:(g + 1) * P], ident[:, :])
                last.then_inc(xt_psum, 1)

            def plain_norm(stage):
                n = NORM[stage]
                transpose_rows(n)
                with pe.Fori(1, B) as b:
                    pe.wait_ge(xt_ready, n + b)
                    transpose_rows(n + b)

            def keys_and_values(k0, v0):
                for g in range(G):
                    for i in range(2):
                        for c in range(G):
                            last = pe.matmul(PS[:, 2 * g + i, 0:KW // 2], W[:, 1, c, g * P:(g + 1) * P],
                                             ctxT[:, c, i * (KW // 2):(i + 1) * (KW // 2)], start=c == 0, stop=c == G - 1)
                    last.then_inc(kt_psum, 1)
                for b in range(B):
                    if b == B - 2:
                        pe.wait_ge(kt_ready, k0 + 1)
                    for c in range(G):
                        last = pe.matmul(PS[0:SK, (4, 5, 6, 0)[b // 2], (b % 2) * D:(b % 2 + 1) * D],
                                         ctxT[:, c, b * SK:(b + 1) * SK], W[:, 2, c, :], start=c == 0, stop=c == G - 1)
                    if b % 2:
                        last.then_inc(v_psum, 1)

            def two_tiles(bank, left, right):
                for t in range(T):
                    for c in range(G):
                        last = pe.matmul(PS[:, bank, t * D:(t + 1) * D], left[:, c, t * P:(t + 1) * P], right[:, c],
                                         start=c == 0, stop=c == G - 1)
                return last

            def two_chunks(bank, weights, moving):
                for g in range(G):
                    for c in range(G):
                        last = pe.matmul(PS[:, bank, g * S:(g + 1) * S], weights[:, c, g * P:(g + 1) * P], moving(c),
                                         start=c == 0, stop=c == G - 1)
                return last

            def xt_moving(b):
                return lambda c: XT[:, bass.ds(b, 1), c, 1:S + 1].rearrange("p o s -> p (o s)")

            def attention(stage):
                layer, norms = LAYER[stage], NORM[stage]
                u0, b0 = B * UNITS * layer, B * layer
                wo = W[:, 0 if stage == "a2" else 3]

                def body(b, j, live):
                    if j == 0 and live(0) and stage != "a2":
                        after(pe, q_ready, b0 + b)
                        after(pe, xt_ready, norms + b - 2)
                        two_chunks(BANK_X, W[:, 0], xt_moving(b)).then_inc(q_psum, 1)
                    if live(1):
                        u, q = u0 + UNITS * b + j - 1, (j - 1) % 2
                        bb, jj = (b, j - 1) if j >= 1 else (b - 1, UNITS - 1)
                        g, t = jj // T, jj % T
                        pe.wait_ge(kbd_ready, G * (b0 + bb) + g + 1)
                        pe.wait_ge(q_ready, b0 + bb + 1)
                        after(pe, max_ready, u - 1)
                        for i in range(2):
                            last = pe.matmul(PS[:, 2 * q + i, 0:KW // 2], QT[:, g, t * P:(t + 1) * P],
                                             KBD[:, g, i * (KW // 2):(i + 1) * (KW // 2)], start=True, stop=True)
                        last.then_inc(s_psum, 1)
                    if live(3):
                        u, q = u0 + UNITS * b + j - 3, (j - 3) % 2
                        pe.wait_ge(p_ready, u + 1)
                        after(pe, pt_ready, u)
                        for h in range(HG):
                            last = pe.transpose(PS[0:SK, BANK_PT + h // 4, (h % 4) * P:(h % 4 + 1) * P],
                                                SC[:, q, h * SK:(h + 1) * SK], ident[:, :])
                        last.then_inc(pt_psum, 1)
                    if live(4):
                        u = u0 + UNITS * b + j - 4
                        g, t = j // T, j % T
                        pe.wait_ge(pt_ready, u + 1)
                        pe.wait_ge(vp_ready, G * (b0 + b - 1) + g + 1)
                        if j == 0:
                            after(pe, ot_ready, b0 + b - 1)
                        for h in range(HG):
                            last = pe.matmul(PS[:, BANK_OT, g * S + t * P:g * S + (t + 1) * P],
                                             VP[:, g, h * P:(h + 1) * P], PT[:, h * P:(h + 1) * P],
                                             start=h == 0, stop=h == HG - 1)
                        last.then_inc(pv_done, 1)
                    if j == 0 and live(8):
                        pe.wait_ge(ot_ready, b0 + b - 1)
                        pe.wait_ge(q_ready, at_most(b0 + b + 1, b0 + B))
                        after(pe, xt_ready, norms + b - 2)
                        two_tiles(BANK_X, OT, wo).then_inc(o_psum, 1)
                    if j == 2 and live(10):
                        transpose_rows(norms + b - 2)

                software_pipeline(pe, body, UNITS, 11, 2)
                end_stage(pe, stage)

            pe.wait_ge(ctx_loaded, 16)
            pe.wait_ge(w_loaded, 16 * 4)
            keys_and_values(0, 0)
            pe.wait_ge(const_ready, 1)
            plain_norm("setup")
            end_stage(pe, "setup")
            attention("a0")

            def ffn_body(b, j, live):
                if live(0):
                    pe.wait_ge(mixed, b + 1)
                    after(pe, r_ready, b)
                    two_tiles(0, xrT, W[:, 0]).then_inc(r_psum, 1)
                    after(pe, krelu_ready, b)
                    two_chunks(1, W[:, 1], lambda c: xkT[:, c]).then_inc(k_psum, 1)
                if live(1):
                    pe.wait_ge(ksq_ready, b)
                    pe.wait_ge(stats_ready, NORM["f0"] + b - 1)
                    two_tiles(6, ksq, W[:, 2]).then_inc(o_psum, 1)
                if live(2):
                    pe.wait_ge(xt_ready, NORM["f0"] + b - 2)
                    transpose_rows(NORM["f0"] + b - 2)

            pe.wait_ge(w_loaded, 16 * 7)
            software_pipeline(pe, ffn_body, 1, 2, 2)
            end_stage(pe, "f0")

            def mlp_body(b, j, live):
                if live(0):
                    pe.wait_ge(ctxs_ready, b + 1)
                    after(pe, g_ready, b)
                    for c in range(G):
                        last = pe.matmul(PS[0:SK, 0, 0:S], ctxS[:, c], xt_moving(b)(c), start=c == 0, stop=c == G - 1)
                    last.then_inc(g_psum, 1)
                if live(1):
                    pe.wait_ge(g_ready, b)
                    pe.wait_ge(stats_ready, NORM["m1"] + b - 1)
                    ctx_b = V[:, bass.ds(b - 1, 1), :].rearrange("k o d -> k (o d)")
                    for t in range(T):
                        last = pe.matmul(PS[:, 6, t * D:(t + 1) * D], gel[:, t * P:(t + 1) * P], ctx_b, start=True, stop=True)
                    last.then_inc(o_psum, 1)
                if live(2):
                    pe.wait_ge(xt_ready, NORM["m1"] + b - 2)
                    transpose_rows(NORM["m1"] + b - 2)

            pe.wait_ge(ctx_loaded, 16 * 2)
            software_pipeline(pe, mlp_body, 1, 2, 2)
            end_stage(pe, "m1")

            def route(stage, first):
                def body(b, j, live):
                    if live(0):
                        after(pe, lt_ready, first + b)
                        for c in range(G):
                            last = pe.matmul(PS[0:E, 0, 0:S], WR[:, c], xt_moving(b)(c), start=c == 0, stop=c == G - 1)
                        last.then_inc(lt_psum, 1)
                    if live(1):
                        pe.wait_ge(lt_ready, first + b)
                        after(pe, lg_ready, first + b - 1)
                        hold(pe)
                        for t in range(T):
                            last = pe.transpose(PS[:, 1, t * E:(t + 1) * E], LTs[:, t * P:(t + 1) * P], ident[0:E, 0:E])
                        last.then_inc(lg_psum, 1)

                software_pipeline(pe, body, 1, 1, 1)
                end_stage(pe, stage)

            def moe(stage):
                experts, F, u0, x0 = MOE[stage]
                chunks = -(-F // P)

                def weights(e):
                    if stage == "e1":
                        return l1_w(e, 0), l1_w(e, 1), l1_wd(e)
                    e = E - 1 if stage == "s2" else e
                    return l2_w(e, 0), l2_w(e, 1), l2_wd(e)

                def body(b, j, live):
                    if live(0):
                        u, q, t, e = u0 + T * experts * b + j, j % 2, j // experts, j % experts
                        pe.wait_ge(xs_ready, x0 + T * b + t + 1)
                        after(pe, hh_ready, u - 1)
                        for k, w in enumerate(weights(e)[0:2]):
                            for c in range(G):
                                last = pe.matmul(PS[:, 2 * q + k, 0:F], XS[:, t, c], w[:, c], start=c == 0, stop=c == G - 1)
                        last.then_inc(h_psum, 1)
                    if live(1):
                        u, q = u0 + T * experts * b + j - 1, (j - 1) % 2
                        pe.wait_ge(hh_ready, u + 1)
                        after(pe, ht_ready, u - 1)
                        for c in range(chunks):
                            n = min(P, F - c * P)
                            last = pe.transpose(PS[0:n, 4 + q, c * P:(c + 1) * P], HH[:, q, c * P:c * P + n], ident[:, :])
                        last.then_inc(ht_psum, 1)
                    if live(2):
                        u, q, e = u0 + T * experts * b + j - 2, j % 2, (j - 2) % experts
                        pe.wait_ge(ht_ready, u + 1)
                        after(pe, y_added, u - 1)
                        wd = weights(e)[2]
                        for c in range(chunks):
                            n = min(P, F - c * P)
                            last = pe.matmul(PS[:, 6 + q, 0:D], HT[0:n, q, c], wd[0:n, c], start=c == 0, stop=c == chunks - 1)
                        last.then_inc(y_psum, 1)

                pe.wait_ge(moe_loaded, MOE_LOADED[stage])
                software_pipeline(pe, body, T * experts, 2, 1)
                end_stage(pe, stage)

            pe.wait_ge(w_loaded, 16 * 9)
            route("r1", 0)
            moe("e1")
            plain_norm("n4")
            end_stage(pe, "n4")
            attention("a2")
            pe.wait_ge(mask_loaded, 16 * 3)
            route("r2", B)
            moe("s2")
            moe("e2")
            pe.wait_ge(w_loaded, 16 * 13)
            keys_and_values(G, 4)
            plain_norm("n6")
            end_stage(pe, "n6")
            attention("a3")
            pe.wait_ge(w8_ready, 1)
            with pe.Fori(0, B) as b:
                pe.wait_ge(qi_ready, b + 1)
                pe.wait_ge(f_taken, b)
                two_tiles(0, QI, WBF).then_inc(f_psum, 1)
            end_stage(pe, "q3")


def kernel(**inputs):
    import concourse.bacc as bacc
    from concourse.bass_utils import run_bass_kernel_spmd

    def flip(name, axes=None):
        return np.ascontiguousarray(np.transpose(inputs[name], axes))

    def columns(*names):
        return np.stack([inputs[n] for n in names]).reshape(len(names), G, P).transpose(2, 0, 1)

    ctx = np.ascontiguousarray(inputs["ctx_1024"])
    arrays = {
        "x": inputs["x"], "ctx": ctx, "ctxT": np.ascontiguousarray(ctx.reshape(-1, D).T),
        "bias": inputs["fside_BxSxS2_0"], "mask0": inputs["mask_BxS2_ik0"].reshape(-1), "mask2": inputs["mask_BxS2_if0"].reshape(-1),
        "L0_wqT": flip("L0_xattn_w_q"), "L0_wkT": flip("L0_xattn_w_k"), "L0_wvT": flip("L0_xattn_w_v"), "L0_woT": flip("L0_xattn_w_o"),
        "L0_vecs": columns("L0_xattn_b_q", "L0_xattn_b_k", "L0_ffn_mu_r", "L0_ffn_mu_k"), "L0_bv": inputs["L0_xattn_b_v"], "L0_bo": inputs["L0_xattn_b_o"],
        "L0_WrT": flip("L0_ffn_W_r"), "L0_WkT": flip("L0_ffn_W_k"), "L0_WvT": flip("L0_ffn_W_v"),
        "L1_wrT": flip("L1_ffn_w_router"), "L1_w1": inputs["L1_ffn_w1"], "L1_w2": inputs["L1_ffn_w2"], "L1_w3": inputs["L1_ffn_w3"],
        "L2_WT": flip("L2_xattn_W"), "L2_b": inputs["L2_xattn_b"], "L2_gateT": flip("L2_ffn_gate_w"),
        "L2_sgT": flip("L2_ffn_shared_gate"), "L2_suT": flip("L2_ffn_shared_up"), "L2_sdT": flip("L2_ffn_shared_down"),
        "L2_rgT": flip("L2_ffn_r_gate", (0, 2, 1)), "L2_ruT": flip("L2_ffn_r_up", (0, 2, 1)), "L2_rdT": flip("L2_ffn_r_down", (0, 2, 1)),
        "L3_Wq": inputs["L3_xattn_Wq"], "L3_Wk": inputs["L3_xattn_Wk"], "L3_Wv": inputs["L3_xattn_Wv"], "L3_Wo": inputs["L3_xattn_Wo"],
        "L3_w8T": flip("L3_ffn_weight_int8").view(np.int32), "L3_ws": inputs["L3_ffn_weight_scale"].reshape(-1), "L3_bias": inputs["L3_ffn_bias"],
    }
    arrays = {k: np.ascontiguousarray(v) for k, v in arrays.items()}
    nc = bacc.Bacc("TRN2", target_bir_lowering=False, num_devices=1)
    a = {k: nc.dram_tensor("in_" + k, v.shape, mybir.dt.from_np(v.dtype), kind="ExternalInput").ap() for k, v in arrays.items()}
    a["out"] = nc.dram_tensor("out", (B, S, D), F32, kind="ExternalOutput").ap()
    build(nc, a)
    r = run_bass_kernel_spmd(nc, [{"in_" + k: v for k, v in arrays.items()}], core_ids=[0])
    return r.results[0]["out"]
```

```python
from contextlib import ExitStack

import numpy as np
import concourse.bass as bass
import concourse.mybir as mybir

F32 = mybir.dt.float32
BF16 = mybir.dt.bfloat16
I32 = mybir.dt.int32
I8 = mybir.dt.int8
U32 = mybir.dt.uint32
ALU = mybir.AluOpType
ACT = mybir.ActivationFunctionType
AX = mybir.AxisListType

P = 128
B, S, D = 8, 256, 256
SK = 77
DH = 16
G = D // P
HG = P // DH
T = S // P
NT = B * T
UNITS = G * T
E = 8
F1, F2 = 352, 512
EPS = 1e-5
NEG = -1e30
PAD = -1e9
ROUND = 12582912.0
KW = HG * SK
VW = HG * (P + DH)
EW = 3 * G * F2


def at_most(n, limit):
    return min(n, limit) if isinstance(n, int) else n


def after(engine, semaphore, count):
    if not isinstance(count, int) or count > 0:
        engine.wait_ge(semaphore, count)


def software_pipeline(engine, body, slots, depth, warm, batches=B):
    total = batches * slots
    for s in range(warm * slots):
        body(s // slots, s % slots, lambda lag, s=s: lag <= s)
    with engine.Fori(warm, batches) as b:
        for j in range(slots):
            body(b, j, lambda lag: True)
    for s in range(total, total + depth):
        body(s // slots, s % slots, lambda lag, s=s: s < total + lag)


def build(nc, a):
    with ExitStack() as ctx:
        def sb(name, shape, dt=F32):
            return ctx.enter_context(nc.sbuf_tensor(name, shape, dt))

        def sem(name):
            return ctx.enter_context(nc.semaphore(name))

        X = sb("X", [P, NT, D])
        XT = sb("XT", [P, B, G, S + 1])
        ctxT = sb("ctxT", [P, G, B * SK])
        W = sb("W", [P, 4, G, D])
        WE = sb("WE", [P, E * EW])
        ident = sb("ident", [P, P])
        headmask = sb("headmask", [P, HG])
        causal = sb("causal", [P, SK])
        vecs = sb("vecs", [P, 6, G])
        rows = sb("rows", [P, 2, D])
        halfpow = sb("halfpow", [P, T])
        mv = sb("mv", [P, T, 2])
        rstd = sb("rstd", [P, T])
        epsv = sb("epsv", [P, T])
        amax = sb("amax", [P, B])
        qsc = sb("qsc", [P, 4])
        iota8 = sb("iota8", [P, E])
        LG = sb("LG", [P, NT, E])
        PR = sb("PR", [P, NT, E])
        top = sb("top", [P, NT, 8])
        topi = sb("topi", [P, NT, 8], U32)
        topf = sb("topf", [P, NT, 2])
        MEANS = sb("MEANS", [P, NT])
        RSTDS = sb("RSTDS", [P, NT])
        slot_u = sb("slot_u", [P, 2, NT], U32)
        gate = sb("gate", [P, 2, NT])
        owner_i = sb("owner_i", [P, 2 * NT + E - 1], I32)
        iota_i = sb("iota_i", [P, 2 * NT + E - 1], I32)
        score = sb("score", [P, NT])
        gsum = sb("gsum", [P, NT])
        WR = sb("WR", [P, G, E])
        VEND = E * EW - B * D
        V = WE[0:SK, VEND:].rearrange("k (b d) -> k b d", b=B)

        VP = sb("VP", [SK, G, VW])
        tmp = sb("tmp", [P, 7600])
        def carve(sizes):
            at, views = 0, []
            for n in sizes:
                views.append(tmp[:, at:at + n])
                at += n
            return views
        BIASf, MASKF, KTf, KBDf, SCf, PTf, QTf, OTf = carve(
            (NT * SK, B * SK, G * B * SK, G * KW, 2 * KW, HG * P, G * S, G * S))
        small = sb("small", [P, 3, 2, HG])
        XN = sb("XN", [P, T, D])
        st = sb("st", [P, T, 6])
        BIAS = BIASf.rearrange("p (n k) -> p n k", n=NT)
        Z = BIASf.rearrange("p (u k) -> p u k", u=2)
        KT = KTf.rearrange("p (g n) -> p g n", g=G)
        KBD = KBDf.rearrange("p (g n) -> p g n", g=G)
        SC = SCf.rearrange("p (u n) -> p u n", u=2)
        PT = PTf[0:SK]
        QT = QTf.rearrange("p (g s) -> p g s", g=G)
        OT = OTf.rearrange("p (g s) -> p g s", g=G)
        MASKI = KBDf[:, 0:B * SK].bitcast(I32)
        mx, sm, rs = small[:, 0], small[:, 1], small[:, 2]
        tAf, tBf, xrf, xkf, kreluf, ksqf, rsigf, rvf = carve((G * S,) * 8)
        halves = lambda f: f.rearrange("p (g s) -> p g s", g=G)
        tA, tB, xrT, xkT, krelu, ksq = map(halves, (tAf, tBf, xrf, xkf, kreluf, ksqf))
        rsig, rv = halves(rsigf), halves(rvf)
        ctxSf, gelf = carve((G * SK, S))
        ctxS = ctxSf.rearrange("p (g k) -> p g k", g=G)
        gel = gelf[0:SK]
        XSf, SLf, HHf, HTf, XRf, YOf, XDf = carve((2 * G * P, 2 * F2, 2 * F2, 2 * F2, 2 * D, 2 * D, 4 * D))
        XS = XSf.rearrange("p (u g s) -> p u g s", u=2, g=G)
        SL = SLf.rearrange("p (u f) -> p u f", u=2)
        HH = HHf.rearrange("p (u f) -> p u f", u=2)
        HT = HTf.rearrange("p (u c s) -> p u c s", u=2, s=P)
        XR, YO, XD = (f.rearrange("p (u d) -> p u d", d=D) for f in (XRf, YOf, XDf))
        YG = tmp[:, 7600 - 8 * D:7600].rearrange("p (u k d) -> p u k d", k=2, d=D)
        zeros = WE[:, E * (2 * G * F1 + 3 * D):E * (2 * G * F1 + 3 * D) + NT * D]
        LTf, tri, ones, hotf, takenf, countf, wholef, tilesf, pastf, iota_f, iota_p, owner, slotff, pickedf = carve(
            (S, P, P, 2 * NT * E, NT * E, 4 * NT * E, E * NT, 4 * E, (2 * NT + E - 1) * E, 2 * NT + E - 1, NT,
             2 * NT + E - 1, 2 * NT, 2 * NT * E))
        LTs = LTf[0:E]
        hot, picked = (f.rearrange("p (k t e) -> p k t e", k=2, e=E) for f in (hotf, pickedf))
        taken = takenf.rearrange("p (t e) -> p t e", e=E)
        count = countf.rearrange("p (k t e) -> p k t e", k=4, e=E)
        whole = wholef.rearrange("p (e t) -> p e t", e=E)
        tiles_of = tilesf.rearrange("p (k e) -> p k e", e=E)
        past = pastf.rearrange("p (i e) -> p i e", e=E)
        slot_f = slotff.rearrange("p (k t) -> p k t", k=2)
        W8f, WBf, QAf, QBf, QIf, R1f = carve((G * D, G * D, G * S, G * S, G * S, G * S))
        W8 = W8f.bitcast(I8)[:, 0:G * D]
        WBF = WBf.bitcast(BF16)[:, 0:G * D].rearrange("p (g n) -> p g n", g=G)
        QI = QIf.bitcast(BF16)[:, 0:G * S].rearrange("p (g s) -> p g s", g=G)
        QA, QB, R1 = map(halves, (QAf, QBf, R1f))
        PS = ctx.enter_context(nc.psum_tensor("PS", [P, 8, 512], F32))
        BANK_PT, BANK_OT, BANK_X = 4, 6, 7

        x_loaded = sem("x_loaded"); ctx_loaded = sem("ctx_loaded"); small_loaded = sem("small_loaded")
        w_loaded = sem("w_loaded"); moe_loaded = sem("moe_loaded"); mask_loaded = sem("mask_loaded")
        last_loaded = sem("last_loaded"); const_ready = sem("const_ready"); stage_done = sem("stage_done")
        kt_psum = sem("kt_psum"); v_psum = sem("v_psum"); kt_ready = sem("kt_ready"); v_ready = sem("v_ready")
        q_psum = sem("q_psum"); q_ready = sem("q_ready"); kbd_ready = sem("kbd_ready"); vp_ready = sem("vp_ready")
        s_psum = sem("s_psum"); max_ready = sem("max_ready"); shifted = sem("shifted"); exp_done = sem("exp_done")
        rsum_ready = sem("rsum_ready"); p_ready = sem("p_ready"); pt_psum = sem("pt_psum"); pt_ready = sem("pt_ready")
        pv_done = sem("pv_done"); ot_ready = sem("ot_ready")
        o_psum = sem("o_psum"); stats_ready = sem("stats_ready"); xn_ready = sem("xn_ready")
        xt_psum = sem("xt_psum"); xt_ready = sem("xt_ready"); amax_ready = sem("amax_ready")
        prev_ready = sem("prev_ready"); mixed = sem("mixed"); r_psum = sem("r_psum"); k_psum = sem("k_psum")
        r_ready = sem("r_ready"); krelu_ready = sem("krelu_ready"); ksq_ready = sem("ksq_ready")
        ctxs_ready = sem("ctxs_ready"); g_psum = sem("g_psum"); g_ready = sem("g_ready")
        lt_psum = sem("lt_psum"); lt_ready = sem("lt_ready"); lg_psum = sem("lg_psum"); lg_ready = sem("lg_ready")
        route_dve = sem("route_dve"); route_act = sem("route_act")
        xs_ready = sem("xs_ready"); h_psum = sem("h_psum"); silu_ready = sem("silu_ready"); hh_ready = sem("hh_ready")
        ht_psum = sem("ht_psum"); ht_ready = sem("ht_ready"); y_psum = sem("y_psum"); y_taken = sem("y_taken"); y_ready = sem("y_ready")
        rows_ready = sem("rows_ready"); scattered = [sem(f"scattered{i}") for i in range(4)]
        slots_zeroed = sem("slots_zeroed")
        rows_in = [sem(f"rows_in{i}") for i in range(2)]; rows_out = [sem(f"rows_out{i}") for i in range(2)]
        xt2_psum = sem("xt2_psum")
        gathered = [sem(f"gathered{i}") for i in range(4)]; gathered_used = sem("gathered_used"); tri_ready = sem("tri_ready")
        taken_ready = sem("taken_ready"); count_psum = sem("count_psum")
        qi_ready = sem("qi_ready"); f_psum = sem("f_psum"); f_taken = sem("f_taken")
        part_amax = sem("part_amax"); all_amax = sem("all_amax"); w8_ready = sem("w8_ready")
        held = sem("held"); x_final = sem("x_final"); stored = sem("stored")
        block = ctx.enter_context(nc.Block())

        ST = {n: i + 1 for i, n in enumerate(
            ("setup", "a0", "f0", "m1", "r1", "e1", "n4", "a2", "r2", "s2", "e2", "n6", "a3", "q3"))}
        NORM = dict(setup=0, a0=8, f0=16, m1=24, n4=32, a2=40, n6=48, a3=56)
        SUM = dict(a0=0, f0=8, m1=16, a2=24, a3=32)
        LAYER = dict(a0=0, a2=1, a3=2)
        TOPK = dict(e1=2, e2=1)
        SLOTS = {s: NT * k + E - 1 for s, k in TOPK.items()}
        FIRST = dict(e1=0, s2=SLOTS["e1"], e2=SLOTS["e1"] + NT)
        FIRST_X = dict(e1=0, e2=SLOTS["e1"])
        WIDTH = dict(e1=F1, s2=F2, e2=F2)
        BUFS = dict(e1=("xs1", "ys1"), e2=("xs2", "ys2"))
        L1_DMAS = 4 * E
        MOE_LOADED = dict(e1=16 * L1_DMAS, s2=16 * (L1_DMAS + 3 * E), e2=16 * (L1_DMAS + 3 * E + 3))

        def end_stage(engine, name):
            engine.drain().then_inc(stage_done, 1)
            engine.wait_ge(stage_done, 4 * ST[name])

        SCATTERED = 16 * TOPK["e1"] * NT // 4

        def moved(stage, q, pairs=0):
            before = {"e1": 0, "e2": (SLOTS["e1"] + 1 - q) // 2,
                      None: (SLOTS["e1"] + 1 - q) // 2 + (SLOTS["e2"] + 1 - q) // 2}[stage]
            return pairs * 16 + 16 * before

        def tile_pipeline(engine, body, tiles, depth):
            warm = -(-depth // 2) + 1
            for s in range(2 * warm):
                body((s, s % 2, s // 2), lambda lag, s=s: lag <= s)
            with engine.Fori(warm, tiles // 2) as i:
                for j in range(2):
                    body((i * 2 + j, j, i), lambda lag: True)
            for s in range(tiles // 2 * 2, tiles + depth):
                body((s, s % 2, s // 2), lambda lag, s=s: s < tiles + lag)

        def hold(engine):
            engine.nop().then_inc(held, 1)

        def xt_of(b):
            return XT[:, bass.ds(b, 1), :, 1:S + 1].rearrange("p o g s -> p (o g) s")

        def x_of(b):
            return X[:, bass.ds(b * T, T), :]

        def repeat(ap, n):
            return ap.unsqueeze(1).to_broadcast([ap.shape[0], n, ap.shape[1]])

        def spread(ap, n):
            return ap.unsqueeze(2).to_broadcast([ap.shape[0], ap.shape[1], n])

        def l1_w(e, k):
            base = e * (2 * G * F1 + 3 * D) + k * G * F1
            return WE[:, base:base + G * F1].rearrange("p (g f) -> p g f", g=G)

        def l1_wd(e):
            base = e * (2 * G * F1 + 3 * D) + 2 * G * F1
            return WE[:, base:base + 3 * D].rearrange("p (c d) -> p c d", c=3)

        def l2_w(e, k):
            base = e * EW + k * G * F2
            return WE[:, base:base + G * F2].rearrange("p (g f) -> p g f", g=G)

        def l2_wd(e):
            base = e * EW + 2 * G * F2
            return WE[:, base:base + 4 * D].rearrange("p (c d) -> p c d", c=4)

        @block.sync
        def _(sp):
            def square(k, name):
                sp.dma_start(W[:, k], a[name].rearrange("(g p) n -> p g n", p=P)).then_inc(w_loaded, 16)

            def everywhere(dst, name, semaphore):
                sp.dma_start(dst, a[name].partition_broadcast(P)).then_inc(semaphore, 16)

            sp.dma_start(X[:, :, :], a["x"].rearrange("b (t p) d -> p (b t) d", p=P)).then_inc(x_loaded, 16)
            sp.dma_start(ctxT[:, :, :], a["ctxT"].rearrange("(g p) n -> p g n", p=P)).then_inc(ctx_loaded, 16)
            for k, name in enumerate(("L0_wqT", "L0_wkT", "L0_wvT", "L0_woT")):
                square(k, name)
            sp.dma_start(vecs[:, 0:4], a["L0_vecs"]).then_inc(small_loaded, 16)
            everywhere(rows[:, 0], "L0_bv", small_loaded)
            everywhere(rows[:, 1], "L0_bo", small_loaded)
            everywhere(MASKI, "mask0", small_loaded)
            sp.dma_start(BIAS, a["bias"].rearrange("b (t p) k -> p (b t) k", p=P)).then_inc(small_loaded, 16)
            sp.wait_ge(const_ready, 1)
            for buf, n in (("xs1", SLOTS["e1"]), ("xs2", SLOTS["e2"])):
                for i in range(0, n, NT):
                    m = min(NT, n - i)
                    sp.dma_start(a[buf][i * P:(i + m) * P].rearrange("(i p) d -> p i d", p=P),
                                 zeros[:, 0:m * D].rearrange("p (i d) -> p i d", i=m)).then_inc(slots_zeroed, 16)
            for e in range(E):
                for k, name in enumerate(("L1_w1", "L1_w3")):
                    sp.dma_start(l1_w(e, k), a[name][e].rearrange("(g p) f -> p g f", p=P)).then_inc(moe_loaded, 16)
                w2 = a["L1_w2"][e]
                sp.dma_start(l1_wd(e)[:, 0:2], w2[0:2 * P].rearrange("(c p) d -> p c d", p=P)).then_inc(moe_loaded, 16)
                sp.dma_start(l1_wd(e)[0:F1 - 2 * P, 2], w2[2 * P:F1]).then_inc(moe_loaded, 16)
            sp.wait_ge(stage_done, 4 * ST["a0"])
            for k, name in enumerate(("L0_WrT", "L0_WkT", "L0_WvT")):
                square(k, name)
            sp.dma_start(V, a["ctx"].rearrange("b k d -> k b d")).then_inc(ctx_loaded, 16)
            sp.wait_ge(stage_done, 4 * ST["f0"])
            square(0, "L2_WT")
            sp.dma_start(WR[:, :, :], a["L1_wrT"].rearrange("(g p) n -> p g n", p=P)).then_inc(w_loaded, 16)

            def expert_tiles(stage):
                xs, ys = a[BUFS[stage][0]], a[BUFS[stage][1]]
                first = FIRST_X[stage]

                def body(i, live):
                    if live(0):
                        n, q = first + i[0], i[1]
                        after(sp, xt2_psum, n - 1)
                        sp.dma_start(XR[:, q], xs[bass.ds((n - first) * P, P)]).then_inc(rows_in[q], 16)
                    if live(4):
                        n, q = first + i[0] - 4, i[1]
                        sp.wait_ge(y_ready, n + 1)
                        sp.dma_start(ys[bass.ds((n - first) * P, P)], YO[:, q]).then_inc(rows_out[q], 16)

                tile_pipeline(sp, body, SLOTS[stage], 4)

            sp.wait_ge(stage_done, 4 * ST["r1"])
            for s in scattered:
                sp.wait_ge(s, SCATTERED)
            expert_tiles("e1")
            sp.wait_ge(stage_done, 4 * ST["e1"])
            everywhere(rows[:, 1], "L2_b", mask_loaded)
            everywhere(MASKI, "mask2", mask_loaded)
            sp.dma_start(WR[:, :, :], a["L2_gateT"].rearrange("(g p) n -> p g n", p=P)).then_inc(mask_loaded, 16)
            for e in range(E - 1):
                for k, name in enumerate(("L2_rgT", "L2_ruT")):
                    sp.dma_start(l2_w(e, k), a[name][e].rearrange("(g p) f -> p g f", p=P)).then_inc(moe_loaded, 16)
                sp.dma_start(l2_wd(e), a["L2_rdT"][e].rearrange("(c p) d -> p c d", p=P)).then_inc(moe_loaded, 16)
            sp.wait_ge(stage_done, 4 * ST["a2"])
            for k, name in enumerate(("L2_sgT", "L2_suT")):
                sp.dma_start(l2_w(E - 1, k), a[name].rearrange("(g p) f -> p g f", p=P)).then_inc(moe_loaded, 16)
            sp.dma_start(l2_wd(E - 1), a["L2_sdT"].rearrange("(c p) d -> p c d", p=P)).then_inc(moe_loaded, 16)
            for k, name in enumerate(("L3_Wq", "L3_Wk", "L3_Wv", "L3_Wo")):
                square(k, name)
            sp.wait_ge(stage_done, 4 * ST["s2"])
            for k, name in enumerate(("L2_rgT", "L2_ruT")):
                sp.dma_start(l2_w(E - 1, k), a[name][E - 1].rearrange("(g p) f -> p g f", p=P)).then_inc(moe_loaded, 16)
            sp.dma_start(l2_wd(E - 1), a["L2_rdT"][E - 1].rearrange("(c p) d -> p c d", p=P)).then_inc(moe_loaded, 16)
            for s in scattered[0:2]:
                sp.wait_ge(s, SCATTERED + 16 * NT // 2)
            expert_tiles("e2")
            sp.wait_ge(stage_done, 4 * ST["a3"])
            sp.dma_start(W8f.bitcast(I32)[:, 0:G * D // 4].rearrange("p (g n) -> p g n", g=G),
                         a["L3_w8T"].rearrange("(g p) n -> p g n", p=P)).then_inc(last_loaded, 16)
            everywhere(rows[:, 0], "L3_ws", last_loaded)
            everywhere(rows[:, 1], "L3_bias", last_loaded)
            with sp.Fori(0, B) as b:
                sp.wait_ge(x_final, b + 1)
                sp.dma_start(a["out"][bass.ds(b, 1)].rearrange("o (t p) d -> p (o t) d", p=P), x_of(b)).then_inc(stored, 16)
            sp.wait_ge(stored, 16 * B)

        @block.gpsimd
        def _(pool):
            def norm_rows(n, b, amax_of=None):
                pool.wait_ge(stats_ready, n + 1)
                after(pool, xt_psum, n)
                if amax_of is not None:
                    after(pool, amax_ready, b)
                pool.tensor_tensor(rstd[:, :], mv[:, :, 1], epsv[:, :], ALU.add)
                pool.drain()
                pool.tensor_tensor(rstd[:, :], rstd[:, :], halfpow[:, :], ALU.pow)
                pool.tensor_copy(MEANS[:, bass.ds(b * T, T)], mv[:, :, 0])
                pool.tensor_tensor(XN[:, :, :], x_of(b), mv[:, :, 0:1].to_broadcast([P, T, D]), ALU.subtract)
                pool.drain()
                pool.tensor_copy(RSTDS[:, bass.ds(b * T, T)], rstd[:, :])
                pool.tensor_tensor(XN[:, :, :], XN[:, :, :], spread(rstd[:, :], D), ALU.mult).then_inc(xn_ready, 1)

            def attention(stage, keys):
                layer, norms = LAYER[stage], NORM[stage]
                u0 = B * UNITS * layer

                def block_diagonal_keys(b, g):
                    after(pool, s_psum, u0 + UNITS * b - 2 + 2 * g)
                    k = keys[:, g, bass.ds(b * SK, SK)]
                    pool.tensor_tensor(KBD[:, g].rearrange("p (h k) -> p h k", h=HG), repeat(k, HG),
                                       spread(headmask[:, :], SK), ALU.mult).then_inc(kbd_ready, 1)

                def pad_values(b, g):
                    after(pool, pv_done, u0 + UNITS * b - 2 + 2 * g)
                    v = V[:, bass.ds(b, 1), g * P:(g + 1) * P].rearrange("k o (h d) -> k (o h) d", h=HG)
                    pool.tensor_copy(VP[:, g].rearrange("k (h n) -> k h n", h=HG)[:, :, 0:DH], v).then_inc(vp_ready, 1)

                def body(b, j, live):
                    if j == 0 and live(0):
                        block_diagonal_keys(b, 0)
                    if j == 1 and live(1):
                        block_diagonal_keys(b, 1)
                    if live(1):
                        u, q = u0 + UNITS * b + j - 1, (j - 1) % 2
                        pool.wait_ge(max_ready, u + 1)
                        s = SC[:, q].rearrange("p (h k) -> p h k", h=HG)
                        pool.tensor_tensor(s, s, spread(mx[:, q], SK), ALU.subtract).then_inc(shifted, 1)
                    if j == 2 and live(2):
                        pad_values(b, 0)
                    if j == 0 and live(4):
                        pad_values(b - 1, 1)
                    if live(2):
                        u, q = u0 + UNITS * b + j - 2, j % 2
                        pool.wait_ge(rsum_ready, u + 1)
                        s = SC[:, q].rearrange("p (h k) -> p h k", h=HG)
                        pool.tensor_tensor(s, s, spread(rs[:, q], SK), ALU.mult).then_inc(p_ready, 1)
                    if j == 1 and live(9):
                        norm_rows(norms + b - 2, b - 2, amax if stage == "a3" else None)

                software_pipeline(pool, body, UNITS, 10, 2)

            pool.memset(epsv[:, :], EPS)
            pool.memset(halfpow[:, :], -0.5)
            pool.memset(ident[:, :], 0.0)
            pool.memset(headmask[:, :], 1.0)
            pool.memset(causal[:, :], 0.0)
            pool.memset(VP[:, :, :], 0.0)
            pool.memset(XT[:, :, :, 0:1], 0.0)
            pool.memset(zeros, 0.0)
            pool.iota(iota_i[:, :], pattern=[[1, SLOTS["e1"]]], base=0, channel_multiplier=0)
            for e in range(E):
                pool.memset(iota8[:, e:e + 1], float(e))
            pool.drain()
            pool.affine_select(out=ident[:, :], in_=ident[:, :], compare_op=ALU.not_equal, fill=1.0, base=0,
                               pattern=[[-1, P]], channel_multiplier=1)
            pool.affine_select(out=headmask[:, :], in_=headmask[:, :], compare_op=ALU.is_ge, fill=0.0, base=0,
                               pattern=[[-DH, HG]], channel_multiplier=1)
            pool.affine_select(out=causal[:, :], in_=causal[:, :], compare_op=ALU.is_ge, fill=NEG, base=0,
                               pattern=[[-1, SK]], channel_multiplier=1)
            pool.drain()
            pool.affine_select(out=headmask[:, :], in_=headmask[:, :], compare_op=ALU.is_ge, fill=0.0, base=DH - 1,
                               pattern=[[DH, HG]], channel_multiplier=-1)
            pool.drain().then_inc(const_ready, 1)
            pool.wait_ge(x_loaded, 16)

            def plain_norm(stage):
                norm_rows(NORM[stage], 0)
                with pool.Fori(1, B) as b:
                    norm_rows(NORM[stage] + b, b)

            plain_norm("setup")
            end_stage(pool, "setup")
            attention("a0", KT)
            end_stage(pool, "a0")

            def ffn_body(b, j, live):
                if live(0):
                    after(pool, mixed, b)
                    for dst, k in ((tA, 4), (tB, 5)):
                        for g in range(G):
                            prev = XT[:, bass.ds(b, 1), g, 0:S].rearrange("p o s -> p (o s)")
                            last = pool.tensor_tensor(dst[:, g], prev, vecs[:, k, g:g + 1].to_broadcast([P, S]), ALU.mult)
                    last.then_inc(prev_ready, 1)
                if live(1):
                    pool.wait_ge(krelu_ready, b)
                    after(pool, o_psum, SUM["f0"] + b - 1)
                    pool.tensor_tensor(ksq, krelu, krelu, ALU.mult).then_inc(ksq_ready, 1)
                    norm_rows(NORM["f0"] + b - 1, b - 1)

            software_pipeline(pool, ffn_body, 1, 2, 2)
            end_stage(pool, "f0")

            def mlp_body(b, j, live):
                if live(0):
                    after(pool, g_psum, b)
                    pool.tensor_copy(ctxS, ctxT[:, :, bass.ds(b * SK, SK)]).then_inc(ctxs_ready, 1)
                if live(1):
                    norm_rows(NORM["m1"] + b - 1, b - 1)

            software_pipeline(pool, mlp_body, 1, 2, 2)
            end_stage(pool, "m1")

            def scatter(stage, first, buffers):
                slots = a[BUFS[stage][0]]
                for t in range(NT):
                    pool.wait_ge(rows_ready, first + t + 1)
                    for k in range(TOPK[stage]):
                        pool.indirect_dma_start(slots[:, :], bass.IndirectOffsetOnAxis(ap=slot_u[:, k, t:t + 1], axis=0),
                                                XD[:, t % buffers], None).then_inc(scattered[t % buffers], 16)

            def all_rows_out(following):
                for q in range(2):
                    pool.wait_ge(rows_out[q], moved(following, q))

            def gather(stage, first):
                slots = a[BUFS[stage][1]]
                K = TOPK[stage]
                for t in range(NT):
                    after(pool, gathered_used, first + t - 3)
                    for k in range(K):
                        pool.indirect_dma_start(YG[:, t % 4, k], None, slots[:, :],
                                                bass.IndirectOffsetOnAxis(ap=slot_u[:, k, t:t + 1], axis=0)).then_inc(gathered[t % 4], 16)
                    if t % T == T - 1:
                        if t // T >= 1:
                            norm_rows(NORM[dict(e1="n4", e2="n6")[stage]] + t // T - 1, t // T - 1)
                norm_rows(NORM[dict(e1="n4", e2="n6")[stage]] + B - 1, B - 1)

            def triangle():
                pool.memset(tri, 1.0)
                pool.memset(ones, 1.0)
                pool.drain()
                pool.affine_select(out=tri, in_=tri, compare_op=ALU.is_gt, fill=0.0, base=0,
                                   pattern=[[1, P]], channel_multiplier=-1)
                pool.drain().then_inc(tri_ready, 1)

            triangle()
            end_stage(pool, "r1")
            pool.wait_ge(slots_zeroed, 16 * (-(-SLOTS["e1"] // NT) - (-SLOTS["e2"] // NT)))
            scatter("e1", 0, 4)
            end_stage(pool, "e1")

            all_rows_out("e2")
            gather("e1", 0)
            end_stage(pool, "n4")
            attention("a2", ctxT)
            end_stage(pool, "a2")
            triangle()
            end_stage(pool, "r2")
            scatter("e2", NT, 2)
            end_stage(pool, "s2")
            end_stage(pool, "e2")
            all_rows_out(None)
            gather("e2", NT)
            end_stage(pool, "n6")
            attention("a3", KT)
            end_stage(pool, "a3")
            pool.wait_ge(part_amax, 1)
            pool.partition_all_reduce(qsc[:, 1:2], qsc[:, 0:1], P, bass.bass_isa.ReduceOp.max).then_inc(all_amax, 1)
            end_stage(pool, "q3")

        @block.scalar
        def _(act):
            def xt_evacuate(n, b):
                act.wait_ge(xt_psum, n + 1)
                hold(act)
                act.activation(xt_of(b), PS[:, BANK_X].rearrange("p (g s) -> p g s", g=G), ACT.Copy).then_inc(xt_ready, 1)

            def plain_norm(stage):
                with act.Fori(0, B) as b:
                    xt_evacuate(NORM[stage] + b, b)

            def keys_evacuate(first, bias):
                for g in range(G):
                    act.wait_ge(kt_psum, first + g + 1)
                    dst = KT[:, g].rearrange("p (i n) -> p i n", i=2)
                    src = PS[:, 2 * g:2 * g + 2, 0:KW // 2]
                    if bias:
                        act.activation(dst, src, ACT.Identity, bias=vecs[:, 1, g:g + 1]).then_inc(kt_ready, 1)
                    else:
                        act.activation(dst, src, ACT.Copy).then_inc(kt_ready, 1)

            def attention(stage):
                layer, norms = LAYER[stage], NORM[stage]
                u0, b0 = B * UNITS * layer, B * layer

                def body(b, j, live):
                    if j == 0 and live(8):
                        act.wait_ge(pv_done, u0 + UNITS * (b - 1))
                        after(act, o_psum, SUM[stage] + b - 2)
                        act.activation(OT, PS[:, BANK_OT].rearrange("p (g s) -> p g s", g=G), ACT.Copy).then_inc(ot_ready, 1)
                    if j == 0 and live(0):
                        after(act, s_psum, u0 + UNITS * b)
                        hold(act)
                        if stage == "a2":
                            act.activation(QT, xt_of(b), ACT.Copy, scale=DH ** -0.5).then_inc(q_ready, 1)
                        else:
                            n_q = q0 + b
                            act.wait_ge(q_psum, n_q + 1)
                            for g in range(G):
                                src = PS[:, BANK_X, g * S:(g + 1) * S]
                                if stage == "a0":
                                    last = act.activation(QT[:, g], src, ACT.Identity, scale=DH ** -0.5,
                                                          bias=vecs[:, 0, g:g + 1])
                                else:
                                    last = act.activation(QT[:, g], src, ACT.Copy, scale=DH ** -0.5)
                            last.then_inc(q_ready, 1)
                    if live(2):
                        u, q = u0 + UNITS * b + j - 2, j % 2
                        act.wait_ge(shifted, u + 1)
                        act.activation(SC[:, q], SC[:, q], ACT.Exp).then_inc(exp_done, 1)
                    if live(3):
                        u = u0 + UNITS * b + j - 3
                        act.wait_ge(pt_psum, u + 1)
                        after(act, pv_done, u)
                        act.activation(PT.rearrange("k (i n) -> k i n", i=2), PS[0:SK, BANK_PT:BANK_PT + 2],
                                       ACT.Copy).then_inc(pt_ready, 1)
                    if j == 2 and live(10):
                        xt_evacuate(norms + b - 2, b - 2)

                q0 = 0 if stage == "a0" else B
                software_pipeline(act, body, UNITS, 11, 2)
                end_stage(act, stage)

            act.wait_ge(small_loaded, 16 * 5)
            keys_evacuate(0, True)
            plain_norm("setup")
            end_stage(act, "setup")
            attention("a0")

            def ffn_body(b, j, live):
                if live(0):
                    act.wait_ge(k_psum, b + 1)
                    after(act, ksq_ready, b)
                    act.activation(krelu, PS[:, 1].rearrange("p (g s) -> p g s", g=G), ACT.Relu).then_inc(krelu_ready, 1)
                    act.wait_ge(r_psum, b + 1)
                    act.wait_ge(stats_ready, NORM["f0"] + b)
                    act.activation(rsig, PS[:, 0].rearrange("p (g s) -> p g s", g=G), ACT.Sigmoid).then_inc(r_ready, 1)
                if live(2):
                    xt_evacuate(NORM["f0"] + b - 2, b - 2)

            software_pipeline(act, ffn_body, 1, 2, 2)
            end_stage(act, "f0")

            def mlp_body(b, j, live):
                if live(0):
                    act.wait_ge(g_psum, b + 1)
                    act.wait_ge(o_psum, SUM["m1"] + b)
                    act.activation(gel, PS[0:SK, 0, 0:S], ACT.Gelu_apprx_tanh).then_inc(g_ready, 1)
                if live(2):
                    xt_evacuate(NORM["m1"] + b - 2, b - 2)

            software_pipeline(act, mlp_body, 1, 2, 2)
            end_stage(act, "m1")

            def route(stage, first):
                with act.Fori(0, B) as b:
                    act.wait_ge(lt_psum, first + b + 1)
                    after(act, lg_psum, first + b)
                    act.activation(LTs, PS[0:E, 0, 0:S], ACT.Copy).then_inc(lt_ready, 1)
                act.wait_ge(route_dve, first // B + 1)
                if stage == "r1":
                    act.activation(PR[:, :, :], LG[:, :, :], ACT.Exp).then_inc(route_act, 1)
                else:
                    act.activation(score[:, :], top[:, :, 0], ACT.Sigmoid).then_inc(route_act, 1)
                end_stage(act, stage)

            def experts(stage):
                F, u0 = WIDTH[stage], FIRST[stage]
                chunks = -(-F // P)

                def body(i, live):
                    if live(0):
                        u, q = u0 + i[0], i[1]
                        after(act, h_psum, u - 1)
                        if stage == "s2":
                            src = XT[:, bass.ds(i[2], 1), :, 1 + q * P:1 + (q + 1) * P].rearrange("p o g s -> p (o g) s")
                            hold(act)
                            act.activation(XS[:, q], src, ACT.Copy).then_inc(xs_ready, 1)
                        else:
                            act.wait_ge(xt2_psum, FIRST_X[stage] + i[0] + 1)
                            act.activation(XS[:, q], PS[:, 7, 0:D].rearrange("p (g s) -> p g s", g=G), ACT.Copy).then_inc(xs_ready, 1)
                    if live(1):
                        u, q = u0 + i[0] - 1, 1 - i[1]
                        act.wait_ge(h_psum, u + 1)
                        after(act, hh_ready, u - 1)
                        act.activation(SL[:, q, 0:F], PS[:, 2 * q, 0:F], ACT.Silu).then_inc(silu_ready, 1)
                    if live(2):
                        u, q = u0 + i[0] - 2, i[1]
                        act.wait_ge(ht_psum, u + 1)
                        after(act, y_psum, u - 1)
                        whole = F // P
                        last = act.activation(HT[:, q, 0:whole], PS[:, 4 + q, 0:whole * P].rearrange("p (c s) -> p c s", s=P), ACT.Copy)
                        if whole < chunks:
                            n = F - whole * P
                            last = act.activation(HT[0:n, q, whole], PS[0:n, 4 + q, whole * P:chunks * P], ACT.Copy)
                        last.then_inc(ht_ready, 1)

                tile_pipeline(act, body, NT if stage == "s2" else SLOTS[stage], 2)
                end_stage(act, stage)

            route("r1", 0)
            experts("e1")
            plain_norm("n4")
            end_stage(act, "n4")
            attention("a2")
            route("r2", B)
            experts("s2")
            experts("e2")
            keys_evacuate(G, False)
            plain_norm("n6")
            end_stage(act, "n6")
            attention("a3")
            end_stage(act, "q3")

        @block.vector
        def _(dve):
            def add_sum(stage, b, bank=BANK_X, row=None, times=None):
                if row is not None:
                    dve.tensor_tensor(x_of(b), x_of(b), repeat(row, T), ALU.add)
                    dve.drain()
                dve.wait_ge(o_psum, SUM[stage] + b + 1)
                result = PS[:, bank].rearrange("p (t d) -> p t d", t=T)
                if times is not None:
                    dve.tensor_tensor(rv, result, times, ALU.mult)
                    dve.drain()
                    result = rv
                dve.tensor_tensor(x_of(b), x_of(b), result, ALU.add)
                dve.drain()

            def row_stats(n, b):
                dve.drain()
                for t in range(T):
                    dve.bn_stats(st[:, t], X[:, bass.ds(b * T + t, 1), :].rearrange("p o d -> p (o d)"))
                after(dve, xn_ready, n)
                hold(dve)
                dve.drain()
                for t in range(T):
                    last = dve.bn_aggr(mv[:, t], st[:, t])
                last.then_inc(stats_ready, 1)

            def plain_norm(stage):
                with dve.Fori(0, B) as b:
                    row_stats(NORM[stage] + b, b)

            def values_evacuate(first, bias):
                for i in range(4):
                    dve.wait_ge(v_psum, first + i + 1)
                    src = PS[0:SK, (4, 5, 6, 0)[i]].rearrange("k (b d) -> k b d", b=2)
                    if bias:
                        last = dve.tensor_tensor(V[:, 2 * i:2 * i + 2], src, repeat(rows[0:SK, 0], 2), ALU.add)
                    else:
                        last = dve.tensor_copy(V[:, 2 * i:2 * i + 2], src)
                last.then_inc(v_ready, 1)

            def attention(stage):
                layer, norms = LAYER[stage], NORM[stage]
                u0 = B * UNITS * layer

                def body(b, j, live):
                    if live(2):
                        u, q = u0 + UNITS * b + j - 2, j % 2
                        dve.wait_ge(exp_done, u + 1)
                        after(dve, p_ready, u - 1)
                        dve.tensor_reduce(sm[:, q], SC[:, q].rearrange("p (h k) -> p h k", h=HG), AX.X, ALU.add)
                        dve.drain()
                        dve.reciprocal(rs[:, q], sm[:, q]).then_inc(rsum_ready, 1)
                    if live(1):
                        u, q, t = u0 + UNITS * b + j - 1, (j - 1) % 2, (j - 1) % T
                        bt = b if j >= 1 else b - 1
                        dve.wait_ge(s_psum, u + 1)
                        after(dve, pt_psum, u - 1)
                        s = PS[:, 2 * q:2 * q + 2, 0:KW // 2]
                        if stage == "a3":
                            z = Z[:, q].rearrange("p (i n) -> p i n", i=2)
                            dve.tensor_scalar(z, s, 0.0, NEG, ALU.is_equal, ALU.mult)
                            dve.drain()
                            dve.tensor_tensor(SC[:, q].rearrange("p (i n) -> p i n", i=2), s, z, ALU.add)
                        else:
                            bias = BIAS[:, bass.ds(T * bt + t, 1), :].unsqueeze(1).to_broadcast([P, 2, HG // 2, SK])
                            dve.tensor_tensor(SC[:, q].rearrange("p (i h k) -> p i h k", i=2, k=SK),
                                              s.rearrange("p i (h k) -> p i h k", k=SK), bias, ALU.add)
                        dve.drain()
                        dve.tensor_reduce(mx[:, q], SC[:, q].rearrange("p (h k) -> p h k", h=HG), AX.X,
                                          ALU.max).then_inc(max_ready, 1)
                    if j == 1 and live(9):
                        add_sum(stage, b - 2, row=None if stage == "a3" else rows[:, 1])
                        row_stats(norms + b - 2, b - 2)
                    if stage == "a3" and j == 2 and live(10):
                        dve.wait_ge(xn_ready, norms + b - 1)
                        dve.tensor_reduce(amax[:, bass.ds(b - 2, 1)], XN[:, :, :], AX.XY, ALU.max,
                                          apply_absolute_value=True).then_inc(amax_ready, 1)

                software_pipeline(dve, body, UNITS, 11, 2)
                end_stage(dve, stage)

            dve.wait_ge(small_loaded, 16 * 5)
            dve.tensor_scalar(MASKF, MASKI, 0, None, ALU.not_equal)
            dve.tensor_scalar(vecs[:, 4:6], vecs[:, 2:4], -1.0, 1.0, ALU.mult, ALU.add)
            dve.drain()
            pad = KBDf[:, B * SK:2 * B * SK]
            dve.tensor_scalar(pad, MASKF, -1.0, -PAD, ALU.add, ALU.mult)
            bias4 = BIASf.rearrange("p (b t k) -> p b t k", b=B, t=T)
            by_tile = lambda ap: ap.rearrange("p (b k) -> p b k", b=B).unsqueeze(2).to_broadcast([P, B, T, SK])
            dve.tensor_tensor(bias4, bias4, by_tile(MASKF), ALU.mult)
            dve.drain()
            dve.tensor_tensor(bias4, bias4, by_tile(pad), ALU.add)
            values_evacuate(0, True)
            dve.wait_ge(kt_ready, G)
            dve.tensor_tensor(KT, KT, repeat(MASKF, G), ALU.mult)
            dve.tensor_scalar(vecs[:, 0], vecs[:, 0], DH ** -0.5, None, ALU.mult)
            dve.wait_ge(x_loaded, 16)
            plain_norm("setup")
            end_stage(dve, "setup")
            attention("a0")

            def ffn_body(b, j, live):
                if live(0):
                    dve.wait_ge(prev_ready, b + 1)
                    after(dve, k_psum, b)
                    for dst, prev, k in ((xrT, tA, 2), (xkT, tB, 3)):
                        for g in range(G):
                            now = XT[:, bass.ds(b, 1), g, 1:S + 1].rearrange("p o s -> p (o s)")
                            last = dve.scalar_tensor_tensor(out=dst[:, g], in0=now, scalar=vecs[:, k, g:g + 1],
                                                            in1=prev[:, g], op0=ALU.mult, op1=ALU.add)
                    last.then_inc(mixed, 1)
                if live(1):
                    dve.wait_ge(r_ready, b)
                    add_sum("f0", b - 1, bank=6, times=rsig)
                    row_stats(NORM["f0"] + b - 1, b - 1)

            software_pipeline(dve, ffn_body, 1, 2, 2)
            end_stage(dve, "f0")

            def mlp_body(b, j, live):
                if live(1):
                    add_sum("m1", b - 1, bank=6)
                    row_stats(NORM["m1"] + b - 1, b - 1)

            software_pipeline(dve, mlp_body, 1, 2, 2)
            end_stage(dve, "m1")

            def running_sums(ping, pong, n, keep):
                reach = 1
                while reach < n:
                    dve.tensor_tensor(keep(pong, reach, n), keep(ping, reach, n), keep(ping, 0, n - reach), ALU.add)
                    dve.tensor_copy(keep(pong, 0, reach), keep(ping, 0, reach))
                    dve.drain()
                    ping, pong, reach = pong, ping, 2 * reach
                return ping

            def route(stage, first):
                to = dict(r1="e1", r2="e2")[stage]
                K, n_slots = TOPK[to], SLOTS[to]
                dve.tensor_copy(iota_f[:, :], iota_i[:, :])
                dve.drain()
                dve.tensor_scalar(iota_p[:, :], iota_f[:, 0:NT], float(P), None, ALU.mult)
                with dve.Fori(0, B) as b:
                    dve.wait_ge(lg_psum, first + b + 1)
                    dve.tensor_copy(LG[:, bass.ds(T * b, T), :], PS[:, 1, 0:T * E].rearrange("p (t e) -> p t e", t=T)).then_inc(lg_ready, 1)
                dve.drain()
                for t in range(NT):
                    dve.max(top[:, t], LG[:, t])
                dve.drain()
                for t in range(NT):
                    dve.max_index(topi[:, t], top[:, t], LG[:, t])
                dve.drain()
                dve.tensor_copy(topf[:, :, :], topi[:, :, 0:2])
                if stage == "r1":
                    dve.tensor_tensor(LG[:, :, :], LG[:, :, :], top[:, :, 0:1].to_broadcast([P, NT, E]), ALU.subtract)
                dve.drain().then_inc(route_dve, 1)
                for k in range(K):
                    dve.tensor_tensor(hot[:, k], topf[:, :, k:k + 1].to_broadcast([P, NT, E]),
                                      iota8[:, :].unsqueeze(1).to_broadcast([P, NT, E]), ALU.is_equal)
                dve.drain()
                if K == 2:
                    dve.tensor_tensor(taken[:, :, :], hot[:, 0], hot[:, 1], ALU.add)
                else:
                    dve.tensor_copy(taken[:, :, :], hot[:, 0])
                dve.drain().then_inc(taken_ready, 1)
                dve.wait_ge(count_psum, first // B + 1)
                dve.tensor_copy(count[:, 0], PS[:, 3, 0:NT * E].rearrange("p (t e) -> p t e", e=E))
                dve.drain()
                dve.tensor_copy(count[:, 1], count[:, 0])
                dve.drain()
                upto = running_sums(count[:, 1], count[:, 2], NT, lambda x, lo, hi: x[:, lo:hi])
                slot = count[:, 3]
                dve.tensor_tensor(slot, upto, count[:, 0], ALU.subtract)
                dve.tensor_tensor(whole[:, :, :], upto[:, NT - 1].unsqueeze(2).to_broadcast([P, E, NT]),
                                  iota_p[:, :].unsqueeze(1).to_broadcast([P, E, NT]), ALU.is_gt)
                dve.drain()
                dve.tensor_tensor(slot, slot, PS[:, 2, 0:NT * E].rearrange("p (t e) -> p t e", e=E), ALU.add)
                dve.tensor_reduce(tiles_of[:, 0], whole[:, :, :], AX.X, ALU.add)
                dve.drain()
                dve.tensor_copy(tiles_of[:, 1], tiles_of[:, 0])
                dve.drain()
                end = running_sums(tiles_of[:, 1], tiles_of[:, 2], E, lambda x, lo, hi: x[:, lo:hi])
                start = tiles_of[:, 3]
                dve.tensor_tensor(start, end, tiles_of[:, 0], ALU.subtract)
                dve.tensor_tensor(past[:, 0:n_slots], iota_f[:, 0:n_slots].unsqueeze(2).to_broadcast([P, n_slots, E]),
                                  end.unsqueeze(1).to_broadcast([P, n_slots, E]), ALU.is_ge)
                dve.drain()
                dve.tensor_scalar(start, start, float(P), None, ALU.mult)
                dve.tensor_reduce(owner[:, 0:n_slots], past[:, 0:n_slots], AX.X, ALU.add)
                dve.drain()
                dve.tensor_tensor(slot, slot, start.unsqueeze(1).to_broadcast([P, NT, E]), ALU.add)
                stride = 2 * G * F1 + 3 * D if to == "e1" else EW
                dve.tensor_scalar(owner[:, 0:n_slots], owner[:, 0:n_slots], float(E - 1), float(stride), ALU.min, ALU.mult)
                dve.drain()
                dve.tensor_copy(owner_i[:, 0:n_slots], owner[:, 0:n_slots])
                for k in range(K):
                    dve.tensor_tensor(picked[:, k], hot[:, k], slot, ALU.mult)
                dve.drain()
                for k in range(K):
                    dve.tensor_reduce(slot_f[:, k], picked[:, k], AX.X, ALU.add)
                dve.drain()
                dve.tensor_copy(slot_u[:, 0:K], slot_f[:, 0:K])
                dve.wait_ge(route_act, first // B + 1)
                if stage == "r1":
                    dve.tensor_reduce(gsum[:, :], PR[:, :, :], AX.X, ALU.add)
                    dve.drain()
                    dve.reciprocal(gsum[:, :], gsum[:, :])
                    for k in range(K):
                        dve.tensor_tensor(picked[:, k], hot[:, k], PR[:, :, :], ALU.mult)
                    dve.drain()
                    for k in range(K):
                        dve.tensor_reduce(gate[:, k], picked[:, k], AX.X, ALU.add)
                    dve.drain()
                    dve.tensor_tensor(gate[:, :], gate[:, :], gsum[:, :].unsqueeze(1).to_broadcast([P, 2, NT]), ALU.mult)
                    dve.drain()
                else:
                    dve.tensor_tensor(RSTDS[:, :], RSTDS[:, :], score[:, :], ALU.mult)
                    dve.drain()
                end_stage(dve, stage)

            def rows_out_of_x(t, buffer, sent):
                after(dve, scattered[buffer], sent)
                x = X[:, bass.ds(t, 1), :].rearrange("p o d -> p (o d)")
                dve.tensor_scalar(XD[:, buffer], x, MEANS[:, bass.ds(t, 1)], RSTDS[:, bass.ds(t, 1)],
                                  ALU.subtract, ALU.mult).then_inc(rows_ready, 1)

            def experts(stage):
                F, u0 = WIDTH[stage], FIRST[stage]

                def body(i, live):
                    if stage == "s2" and live(0):
                        rows_out_of_x(i[0], i[1], i[2] * 16 + SCATTERED)
                    if live(1):
                        u, q = u0 + i[0] - 1, 1 - i[1]
                        dve.wait_ge(silu_ready, u + 1)
                        after(dve, ht_psum, u - 1)
                        dve.tensor_tensor(HH[:, q, 0:F], PS[:, 2 * q + 1, 0:F], SL[:, q, 0:F], ALU.mult).then_inc(hh_ready, 1)
                    if live(3):
                        u, q = u0 + i[0] - 3, 1 - i[1]
                        y = PS[:, 6, 0:D]
                        if stage == "s2":
                            x = X[:, bass.ds(i[0] - 3, 1), :].rearrange("p o d -> p (o d)")
                            dve.drain()
                            dve.wait_ge(y_psum, u + 1)
                            dve.tensor_tensor(x, x, y, ALU.add).then_inc(y_taken, 1)
                        else:
                            dve.wait_ge(y_psum, u + 1)
                            after(dve, rows_out[q], moved(stage, q, i[2] - (2 if i[1] == 0 else 1)))
                            dve.tensor_copy(YO[:, q], y).then_inc(y_taken, 1)
                            dve.drain().then_inc(y_ready, 1)

                tile_pipeline(dve, body, NT if stage == "s2" else SLOTS[stage], 3)
                end_stage(dve, stage)

            def add_gathered(to, norm, first):
                K, before = TOPK[to], 0 if to == "e1" else SCATTERED
                dve.drain()
                with dve.Fori(0, B // 2) as i:
                    for j in range(2 * T):
                        t = i * 2 * T + j
                        if j:
                            dve.drain()
                        dve.wait_ge(gathered[j], i * (16 * K) + (before + 16 * K))
                        x = X[:, bass.ds(t, 1), :].rearrange("p o d -> p (o d)")
                        for k in range(K):
                            if k:
                                dve.drain()
                            if to == "e1":
                                last = dve.scalar_tensor_tensor(out=x, in0=YG[:, j, k], scalar=gate[:, k, bass.ds(t, 1)],
                                                                in1=x, op0=ALU.mult, op1=ALU.add)
                            else:
                                last = dve.tensor_tensor(x, x, YG[:, j, k], ALU.add)
                        last.then_inc(gathered_used, 1)
                        if j % T == T - 1:
                            row_stats(NORM[norm] + i * 2 + j // T, i * 2 + j // T)

            route("r1", 0)
            for t in range(NT):
                rows_out_of_x(t, t % 4, 16 * 2 * (t // 4))
            experts("e1")
            dve.wait_ge(mask_loaded, 16 * 3)
            dve.tensor_scalar(MASKF, MASKI, 1, NEG, ALU.is_equal, ALU.mult)
            dve.drain()
            dve.tensor_copy(bias4, by_tile(MASKF))
            dve.drain()
            dve.tensor_tensor(bias4[:, :, 0], bias4[:, :, 0], causal[:, :].unsqueeze(1).to_broadcast([P, B, SK]), ALU.add)
            add_gathered("e1", "n4", 0)
            end_stage(dve, "n4")
            attention("a2")
            route("r2", B)
            experts("s2")
            experts("e2")
            values_evacuate(4, False)
            add_gathered("e2", "n6", NT)
            end_stage(dve, "n6")
            attention("a3")
            dve.tensor_reduce(qsc[:, 0:1], amax[:, :], AX.X, ALU.max).then_inc(part_amax, 1)
            dve.wait_ge(last_loaded, 16 * 3)
            dve.tensor_copy(WBf.bitcast(BF16)[:, 0:G * D], W8).then_inc(w8_ready, 1)
            dve.wait_ge(all_amax, 1)
            dve.tensor_scalar(qsc[:, 2:3], qsc[:, 1:2], 1.0 / 127.0, EPS, ALU.mult, ALU.max)
            dve.drain()
            dve.reciprocal(qsc[:, 3:4], qsc[:, 2:3])
            dve.drain()

            def quant_body(b, j, live):
                if live(0):
                    dve.tensor_scalar(QA, xt_of(b), qsc[:, 3:4], 127.0, ALU.mult, ALU.min)
                    dve.drain()
                    dve.tensor_scalar(QB, QA, -128.0, ROUND, ALU.max, ALU.add)
                    dve.drain()
                    after(dve, f_psum, b)
                    dve.tensor_scalar(QI, QB, -ROUND, None, ALU.add).then_inc(qi_ready, 1)
                if live(1):
                    dve.wait_ge(f_psum, b)
                    dve.scalar_tensor_tensor(out=R1, in0=PS[:, 0].rearrange("p (t d) -> p t d", t=T),
                                             scalar=qsc[:, 2:3], in1=repeat(rows[:, 0], T),
                                             op0=ALU.mult, op1=ALU.mult).then_inc(f_taken, 1)
                    dve.drain()
                    dve.tensor_tensor(R1, R1, repeat(rows[:, 1], T), ALU.add)
                    dve.drain()
                    dve.tensor_tensor(x_of(b - 1), x_of(b - 1), R1, ALU.add).then_inc(x_final, 1)
                    dve.drain()

            software_pipeline(dve, quant_body, 1, 1, 1)
            end_stage(dve, "q3")

        @block.tensor
        def _(pe):
            def transpose_rows(n):
                pe.wait_ge(xn_ready, n + 1)
                for g in range(G):
                    for t in range(T):
                        last = pe.transpose(PS[:, BANK_X, g * S + t * P:g * S + (t + 1) * P],
                                            XN[:, t, g * P:(g + 1) * P], ident[:, :])
                last.then_inc(xt_psum, 1)

            def plain_norm(stage):
                n = NORM[stage]
                transpose_rows(n)
                with pe.Fori(1, B) as b:
                    pe.wait_ge(xt_ready, n + b)
                    transpose_rows(n + b)

            def keys_and_values(k0, v0):
                for g in range(G):
                    for i in range(2):
                        for c in range(G):
                            last = pe.matmul(PS[:, 2 * g + i, 0:KW // 2], W[:, 1, c, g * P:(g + 1) * P],
                                             ctxT[:, c, i * (KW // 2):(i + 1) * (KW // 2)], start=c == 0, stop=c == G - 1)
                    last.then_inc(kt_psum, 1)
                for b in range(B):
                    if b == B - 2:
                        pe.wait_ge(kt_ready, k0 + 1)
                    for c in range(G):
                        last = pe.matmul(PS[0:SK, (4, 5, 6, 0)[b // 2], (b % 2) * D:(b % 2 + 1) * D],
                                         ctxT[:, c, b * SK:(b + 1) * SK], W[:, 2, c, :], start=c == 0, stop=c == G - 1)
                    if b % 2:
                        last.then_inc(v_psum, 1)

            def two_tiles(bank, left, right):
                for t in range(T):
                    for c in range(G):
                        last = pe.matmul(PS[:, bank, t * D:(t + 1) * D], left[:, c, t * P:(t + 1) * P], right[:, c],
                                         start=c == 0, stop=c == G - 1)
                return last

            def two_chunks(bank, weights, moving):
                for g in range(G):
                    for c in range(G):
                        last = pe.matmul(PS[:, bank, g * S:(g + 1) * S], weights[:, c, g * P:(g + 1) * P], moving(c),
                                         start=c == 0, stop=c == G - 1)
                return last

            def xt_moving(b):
                return lambda c: XT[:, bass.ds(b, 1), c, 1:S + 1].rearrange("p o s -> p (o s)")

            def attention(stage):
                layer, norms = LAYER[stage], NORM[stage]
                u0, b0 = B * UNITS * layer, B * layer
                wo = W[:, 0 if stage == "a2" else 3]

                def body(b, j, live):
                    if j == 0 and live(0) and stage != "a2":
                        after(pe, q_ready, b0 + b)
                        after(pe, xt_ready, norms + b - 2)
                        two_chunks(BANK_X, W[:, 0], xt_moving(b)).then_inc(q_psum, 1)
                    if live(1):
                        u, q = u0 + UNITS * b + j - 1, (j - 1) % 2
                        bb, jj = (b, j - 1) if j >= 1 else (b - 1, UNITS - 1)
                        g, t = jj // T, jj % T
                        pe.wait_ge(kbd_ready, G * (b0 + bb) + g + 1)
                        pe.wait_ge(q_ready, b0 + bb + 1)
                        after(pe, max_ready, u - 1)
                        for i in range(2):
                            last = pe.matmul(PS[:, 2 * q + i, 0:KW // 2], QT[:, g, t * P:(t + 1) * P],
                                             KBD[:, g, i * (KW // 2):(i + 1) * (KW // 2)], start=True, stop=True)
                        last.then_inc(s_psum, 1)
                    if live(3):
                        u, q = u0 + UNITS * b + j - 3, (j - 3) % 2
                        pe.wait_ge(p_ready, u + 1)
                        after(pe, pt_ready, u)
                        for h in range(HG):
                            last = pe.transpose(PS[0:SK, BANK_PT + h // 4, (h % 4) * P:(h % 4 + 1) * P],
                                                SC[:, q, h * SK:(h + 1) * SK], ident[:, :])
                        last.then_inc(pt_psum, 1)
                    if live(4):
                        u = u0 + UNITS * b + j - 4
                        g, t = j // T, j % T
                        pe.wait_ge(pt_ready, u + 1)
                        pe.wait_ge(vp_ready, G * (b0 + b - 1) + g + 1)
                        if j == 0:
                            after(pe, ot_ready, b0 + b - 1)
                        for h in range(HG):
                            last = pe.matmul(PS[:, BANK_OT, g * S + t * P:g * S + (t + 1) * P],
                                             VP[:, g, h * P:(h + 1) * P], PT[:, h * P:(h + 1) * P],
                                             start=h == 0, stop=h == HG - 1)
                        last.then_inc(pv_done, 1)
                    if j == 0 and live(8):
                        pe.wait_ge(ot_ready, b0 + b - 1)
                        pe.wait_ge(q_ready, at_most(b0 + b + 1, b0 + B))
                        after(pe, xt_ready, norms + b - 2)
                        two_tiles(BANK_X, OT, wo).then_inc(o_psum, 1)
                    if j == 2 and live(10):
                        transpose_rows(norms + b - 2)

                software_pipeline(pe, body, UNITS, 11, 2)
                end_stage(pe, stage)

            pe.wait_ge(ctx_loaded, 16)
            pe.wait_ge(w_loaded, 16 * 4)
            keys_and_values(0, 0)
            pe.wait_ge(const_ready, 1)
            plain_norm("setup")
            end_stage(pe, "setup")
            attention("a0")

            def ffn_body(b, j, live):
                if live(0):
                    pe.wait_ge(mixed, b + 1)
                    after(pe, r_ready, b)
                    two_tiles(0, xrT, W[:, 0]).then_inc(r_psum, 1)
                    after(pe, krelu_ready, b)
                    two_chunks(1, W[:, 1], lambda c: xkT[:, c]).then_inc(k_psum, 1)
                if live(1):
                    pe.wait_ge(ksq_ready, b)
                    pe.wait_ge(stats_ready, NORM["f0"] + b - 1)
                    two_tiles(6, ksq, W[:, 2]).then_inc(o_psum, 1)
                if live(2):
                    pe.wait_ge(xt_ready, NORM["f0"] + b - 2)
                    transpose_rows(NORM["f0"] + b - 2)

            pe.wait_ge(w_loaded, 16 * 7)
            software_pipeline(pe, ffn_body, 1, 2, 2)
            end_stage(pe, "f0")

            def mlp_body(b, j, live):
                if live(0):
                    pe.wait_ge(ctxs_ready, b + 1)
                    after(pe, g_ready, b)
                    for c in range(G):
                        last = pe.matmul(PS[0:SK, 0, 0:S], ctxS[:, c], xt_moving(b)(c), start=c == 0, stop=c == G - 1)
                    last.then_inc(g_psum, 1)
                if live(1):
                    pe.wait_ge(g_ready, b)
                    pe.wait_ge(stats_ready, NORM["m1"] + b - 1)
                    ctx_b = V[:, bass.ds(b - 1, 1), :].rearrange("k o d -> k (o d)")
                    for t in range(T):
                        last = pe.matmul(PS[:, 6, t * D:(t + 1) * D], gel[:, t * P:(t + 1) * P], ctx_b, start=True, stop=True)
                    last.then_inc(o_psum, 1)
                if live(2):
                    pe.wait_ge(xt_ready, NORM["m1"] + b - 2)
                    transpose_rows(NORM["m1"] + b - 2)

            pe.wait_ge(ctx_loaded, 16 * 2)
            software_pipeline(pe, mlp_body, 1, 2, 2)
            end_stage(pe, "m1")

            def route(stage, first):
                def body(b, j, live):
                    if live(0):
                        after(pe, lt_ready, first + b)
                        for c in range(G):
                            last = pe.matmul(PS[0:E, 0, 0:S], WR[:, c], xt_moving(b)(c), start=c == 0, stop=c == G - 1)
                        last.then_inc(lt_psum, 1)
                    if live(1):
                        pe.wait_ge(lt_ready, first + b)
                        after(pe, lg_ready, first + b - 1)
                        hold(pe)
                        for t in range(T):
                            last = pe.transpose(PS[:, 1, t * E:(t + 1) * E], LTs[:, t * P:(t + 1) * P], ident[0:E, 0:E])
                        last.then_inc(lg_psum, 1)

                software_pipeline(pe, body, 1, 1, 1)
                pe.wait_ge(tri_ready, first // B + 1)
                pe.wait_ge(taken_ready, first // B + 1)
                every = taken[:, :, :].rearrange("p t e -> p (t e)")
                pe.matmul(PS[:, 2, 0:NT * E], tri, every, start=True, stop=True)
                pe.matmul(PS[:, 3, 0:NT * E], ones, every, start=True, stop=True).then_inc(count_psum, 1)
                end_stage(pe, stage)

            def experts(stage):
                F, u0 = WIDTH[stage], FIRST[stage]
                chunks = -(-F // P)

                def weights_at(i):
                    if stage == "s2":
                        return (E - 1) * EW
                    return pe.value_load(owner_i[0:1, bass.ds(i, 1)], min_val=0, max_val=(E - 1) * EW)

                def body(i, live):
                    if live(0) and stage != "s2":
                        n = FIRST_X[stage] + i[0]
                        pe.wait_ge(rows_in[i[1]], moved(stage, i[1], i[2] + 1))
                        after(pe, xs_ready, u0 + i[0])
                        for g in range(G):
                            last = pe.transpose(PS[:, 7, g * P:(g + 1) * P], XR[:, i[1], g * P:(g + 1) * P], ident[:, :])
                        last.then_inc(xt2_psum, 1)
                    if live(1):
                        u, q = u0 + i[0] - 1, 1 - i[1]
                        at = weights_at(i[0] - 1)
                        pe.wait_ge(xs_ready, u + 1)
                        after(pe, hh_ready, u - 1)
                        for k in range(2):
                            for c in range(G):
                                w = WE[:, bass.ds(at + (k * G + c) * F, F)]
                                last = pe.matmul(PS[:, 2 * q + k, 0:F], XS[:, q, c], w, start=c == 0, stop=c == G - 1)
                        last.then_inc(h_psum, 1)
                    if live(2):
                        u, q = u0 + i[0] - 2, i[1]
                        pe.wait_ge(hh_ready, u + 1)
                        after(pe, ht_ready, u - 1)
                        for c in range(chunks):
                            n = min(P, F - c * P)
                            last = pe.transpose(PS[0:n, 4 + q, c * P:(c + 1) * P], HH[:, q, c * P:c * P + n], ident[:, :])
                        last.then_inc(ht_psum, 1)
                    if live(3):
                        u, q = u0 + i[0] - 3, 1 - i[1]
                        at = weights_at(i[0] - 3)
                        pe.wait_ge(ht_ready, u + 1)
                        after(pe, y_taken, u)
                        for c in range(chunks):
                            n = min(P, F - c * P)
                            w = WE[0:n, bass.ds(at + 2 * G * F + c * D, D)]
                            last = pe.matmul(PS[:, 6, 0:D], HT[0:n, q, c], w, start=c == 0, stop=c == chunks - 1)
                        last.then_inc(y_psum, 1)

                pe.wait_ge(moe_loaded, MOE_LOADED[stage])
                tile_pipeline(pe, body, NT if stage == "s2" else SLOTS[stage], 3)
                end_stage(pe, stage)

            pe.wait_ge(w_loaded, 16 * 9)
            route("r1", 0)
            experts("e1")
            plain_norm("n4")
            end_stage(pe, "n4")
            attention("a2")
            pe.wait_ge(mask_loaded, 16 * 3)
            route("r2", B)
            experts("s2")
            experts("e2")
            pe.wait_ge(w_loaded, 16 * 13)
            keys_and_values(G, 4)
            plain_norm("n6")
            end_stage(pe, "n6")
            attention("a3")
            pe.wait_ge(w8_ready, 1)
            with pe.Fori(0, B) as b:
                pe.wait_ge(qi_ready, b + 1)
                pe.wait_ge(f_taken, b)
                two_tiles(0, QI, WBF).then_inc(f_psum, 1)
            end_stage(pe, "q3")


def kernel(**inputs):
    import concourse.bacc as bacc
    from concourse.bass_utils import run_bass_kernel_spmd

    def flip(name, axes=None):
        return np.ascontiguousarray(np.transpose(inputs[name], axes))

    def columns(*names):
        return np.stack([inputs[n] for n in names]).reshape(len(names), G, P).transpose(2, 0, 1)

    ctx = np.ascontiguousarray(inputs["ctx_1024"])
    arrays = {
        "x": inputs["x"], "ctx": ctx, "ctxT": np.ascontiguousarray(ctx.reshape(-1, D).T),
        "bias": inputs["fside_BxSxS2_0"], "mask0": inputs["mask_BxS2_ik0"].reshape(-1), "mask2": inputs["mask_BxS2_if0"].reshape(-1),
        "L0_wqT": flip("L0_xattn_w_q"), "L0_wkT": flip("L0_xattn_w_k"), "L0_wvT": flip("L0_xattn_w_v"), "L0_woT": flip("L0_xattn_w_o"),
        "L0_vecs": columns("L0_xattn_b_q", "L0_xattn_b_k", "L0_ffn_mu_r", "L0_ffn_mu_k"), "L0_bv": inputs["L0_xattn_b_v"], "L0_bo": inputs["L0_xattn_b_o"],
        "L0_WrT": flip("L0_ffn_W_r"), "L0_WkT": flip("L0_ffn_W_k"), "L0_WvT": flip("L0_ffn_W_v"),
        "L1_wrT": flip("L1_ffn_w_router"), "L1_w1": inputs["L1_ffn_w1"], "L1_w2": inputs["L1_ffn_w2"], "L1_w3": inputs["L1_ffn_w3"],
        "L2_WT": flip("L2_xattn_W"), "L2_b": inputs["L2_xattn_b"], "L2_gateT": flip("L2_ffn_gate_w"),
        "L2_sgT": flip("L2_ffn_shared_gate"), "L2_suT": flip("L2_ffn_shared_up"), "L2_sdT": flip("L2_ffn_shared_down"),
        "L2_rgT": flip("L2_ffn_r_gate", (0, 2, 1)), "L2_ruT": flip("L2_ffn_r_up", (0, 2, 1)), "L2_rdT": flip("L2_ffn_r_down", (0, 2, 1)),
        "L3_Wq": inputs["L3_xattn_Wq"], "L3_Wk": inputs["L3_xattn_Wk"], "L3_Wv": inputs["L3_xattn_Wv"], "L3_Wo": inputs["L3_xattn_Wo"],
        "L3_w8T": flip("L3_ffn_weight_int8").view(np.int32), "L3_ws": inputs["L3_ffn_weight_scale"].reshape(-1), "L3_bias": inputs["L3_ffn_bias"],
    }
    arrays = {k: np.ascontiguousarray(v) for k, v in arrays.items()}
    nc = bacc.Bacc("TRN2", target_bir_lowering=False, num_devices=1)
    a = {k: nc.dram_tensor("in_" + k, v.shape, mybir.dt.from_np(v.dtype), kind="ExternalInput").ap() for k, v in arrays.items()}
    for buf, tiles in (("xs1", 2 * NT + E - 1), ("ys1", 2 * NT + E - 1), ("xs2", NT + E - 1), ("ys2", NT + E - 1)):
        a[buf] = nc.dram_tensor(buf, (tiles * P, D), F32, kind="Internal").ap()
    a["out"] = nc.dram_tensor("out", (B, S, D), F32, kind="ExternalOutput").ap()
    build(nc, a)
    r = run_bass_kernel_spmd(nc, [{"in_" + k: v for k, v in arrays.items()}], core_ids=[0])
    return r.results[0]["out"]
```

```python
from contextlib import ExitStack

import numpy as np
import concourse.bass as bass
import concourse.mybir as mybir

F32 = mybir.dt.float32
BF16 = mybir.dt.bfloat16
I32 = mybir.dt.int32
I8 = mybir.dt.int8
U32 = mybir.dt.uint32
ALU = mybir.AluOpType
ACT = mybir.ActivationFunctionType
AX = mybir.AxisListType

P = 128
B, S, D = 8, 256, 256
SK = 77
DH = 16
G = D // P
HG = P // DH
T = S // P
NT = B * T
UNITS = G * T
E = 8
F1, F2 = 352, 512
EPS = 1e-5
NEG = -1e30
PAD = -1e9
ROUND = 12582912.0
KW = HG * SK
HALF = P // 2
LEFT = SK - HALF
CHUNKS = HG // 2
PW = CHUNKS * P + HG * LEFT
EW = 3 * G * F2
ZT = 12
TMP = 9056


def at_most(n, limit):
    return min(n, limit) if isinstance(n, int) else n


def after(engine, semaphore, count):
    if not isinstance(count, int) or count > 0:
        engine.wait_ge(semaphore, count)


def software_pipeline(engine, body, slots, depth, warm, batches=B):
    total = batches * slots
    for s in range(warm * slots):
        body(s // slots, s % slots, lambda lag, s=s: lag <= s)
    with engine.Fori(warm, batches) as b:
        for j in range(slots):
            body(b, j, lambda lag: True)
    for s in range(total, total + depth):
        body(s // slots, s % slots, lambda lag, s=s: s < total + lag)


def build(nc, a):
    with ExitStack() as ctx:
        def sb(name, shape, dt=F32):
            return ctx.enter_context(nc.sbuf_tensor(name, shape, dt))

        def sem(name):
            return ctx.enter_context(nc.semaphore(name))

        X = sb("X", [P, NT, D])
        XT = sb("XT", [P, B, G, S + 1])
        ctxT = sb("ctxT", [P, G, B * SK])
        W = sb("W", [P, 4, G, D])
        WE = sb("WE", [P, E * EW])
        ident = sb("ident", [P, P])
        headmask = sb("headmask", [P, HG])
        leftmask = sb("leftmask", [P, HG])
        spreader = sb("spreader", [P, HG * LEFT])
        causal = sb("causal", [P, SK])
        vecs = sb("vecs", [P, 6, G])
        rows = sb("rows", [P, 2, D])
        halfpow = sb("halfpow", [P, T])
        mv = sb("mv", [P, T, 2])
        veps = sb("veps", [P, T])
        epsv = sb("epsv", [P, T])
        amax = sb("amax", [P, B])
        qsc = sb("qsc", [P, 4])
        rank8 = sb("rank8", [P, E])
        LG = sb("LG", [P, NT, E])
        PR = sb("PR", [P, NT, E])
        top = sb("top", [P, 2, NT])
        first_rank = sb("first_rank", [P, NT])
        MEANS = sb("MEANS", [P, NT])
        RSTDS = sb("RSTDS", [P, NT])
        slot_u = sb("slot_u", [P, 2, NT], U32)
        gate = sb("gate", [P, 2, NT])
        owner_i = sb("owner_i", [P, 2 * NT + E - 1], I32)
        iota_i = sb("iota_i", [P, 2 * NT + E - 1], I32)
        score = sb("score", [P, NT])
        gsum = sb("gsum", [P, NT])
        WR = sb("WR", [P, G, E])
        VEND = E * EW - B * D
        V = WE[0:SK, VEND:].rearrange("k (b d) -> k b d", b=B)

        VP = sb("VP", [P, G, CHUNKS, 2 * DH])
        VS = sb("VS", [HG * LEFT, D])
        VL = sb("VL", [P, G, P])
        tmp = sb("tmp", [P, TMP])
        def carve(sizes, at=0):
            views = []
            for n in sizes:
                views.append(tmp[:, at:at + n])
                at += n
            return views
        BIASf, KTf, KBDf, SCf, PNf, PTf, QTf, OTf = carve(
            (NT * SK, G * B * SK, G * KW, 4 * KW, 2 * PW, (CHUNKS + 1) * P, G * S, G * S))
        small = sb("small", [P, 3, 2, HG])
        XN = sb("XN", [P, T, D])
        st = sb("st", [P, T, 6])
        BIAS = BIASf.rearrange("p (n k) -> p n k", n=NT)
        Z = BIASf.rearrange("p (u k) -> p u k", u=2)
        KT = KTf.rearrange("p (g n) -> p g n", g=G)
        KBD = KBDf.rearrange("p (g n) -> p g n", g=G)
        SC = SCf.rearrange("p (u n) -> p u n", u=4)
        MASKF = SCf[:, 0:B * SK]
        PN = PNf.rearrange("p (u n) -> p u n", u=2)
        PT = PTf
        QT = QTf.rearrange("p (g s) -> p g s", g=G)
        OT = OTf.rearrange("p (g s) -> p g s", g=G)
        MASKI = KBDf[:, 0:B * SK].bitcast(I32)
        mx, sm, rs = small[:, 0], small[:, 1], small[:, 2]
        tAf, tBf, xrf, xkf, kreluf, ksqf, rsigf, rvf = carve((G * S,) * 8)
        halves = lambda f: f.rearrange("p (g s) -> p g s", g=G)
        tA, tB, xrT, xkT, krelu, ksq = map(halves, (tAf, tBf, xrf, xkf, kreluf, ksqf))
        rsig, rv = halves(rsigf), halves(rvf)
        ctxSf, gelf = carve((G * SK, S))
        ctxS = ctxSf.rearrange("p (g k) -> p g k", g=G)
        gel = gelf[0:SK]
        XSf, SLf, HHf, HTf, XRf, YOf, XDf = carve((2 * G * P, 2 * F2, 2 * F2, 2 * F2, 2 * D, 2 * D, 4 * D))
        XS = XSf.rearrange("p (u g s) -> p u g s", u=2, g=G)
        SL = SLf.rearrange("p (u f) -> p u f", u=2)
        HH = HHf.rearrange("p (u f) -> p u f", u=2)
        HT = HTf.rearrange("p (u c s) -> p u c s", u=2, s=P)
        XR, YO, XD = (f.rearrange("p (u d) -> p u d", d=D) for f in (XRf, YOf, XDf))
        YG = tmp[:, TMP - 8 * D:TMP].rearrange("p (u k d) -> p u k d", k=2, d=D)
        shared_w = [W[:, 2 * k:2 * k + 2].rearrange("p a g d -> p (a g d)") for k in range(2)]
        shared_wd = tmp[:, TMP - 4 * D:TMP]
        zeros = WE[:, E * (2 * G * F1 + 3 * D):E * (2 * G * F1 + 3 * D) + ZT * D]
        moe_words = 2 * G * P + 3 * 2 * F2 + 2 * 2 * D + 4 * D
        tri, ones, hotf, takenf, countf, wholef, tilesf, pastf, iota_f, iota_p, owner, slotff, pickedf = carve(
            (P, P, 2 * NT * E, NT * E, 4 * NT * E, E * NT, 4 * E, (2 * NT + E - 1) * E, 2 * NT + E - 1, NT,
             2 * NT + E - 1, 2 * NT, 2 * NT * E), at=moe_words)
        LTs = tmp[0:E, 0:4 * S].rearrange("e (u n) -> e u n", u=2)
        hot, picked = (f.rearrange("p (k t e) -> p k t e", k=2, e=E) for f in (hotf, pickedf))
        taken = takenf.rearrange("p (t e) -> p t e", e=E)
        count = countf.rearrange("p (k t e) -> p k t e", k=4, e=E)
        whole = wholef.rearrange("p (e t) -> p e t", e=E)
        tiles_of = tilesf.rearrange("p (k e) -> p k e", e=E)
        past = pastf.rearrange("p (i e) -> p i e", e=E)
        slot_f = slotff.rearrange("p (k t) -> p k t", k=2)
        W8f, WBf = WE[:, 0:G * D], WE[:, G * D:2 * G * D]
        QAf, QBf, QIf, R1f = carve((G * S, G * S, G * S, G * S))
        W8 = W8f.bitcast(I8)[:, 0:G * D]
        WBF = WBf.bitcast(BF16)[:, 0:G * D].rearrange("p (g n) -> p g n", g=G)
        QI = QIf.bitcast(BF16)[:, 0:G * S].rearrange("p (g s) -> p g s", g=G)
        QA, QB, R1 = map(halves, (QAf, QBf, R1f))
        PS = ctx.enter_context(nc.psum_tensor("PS", [P, 8, 512], F32))
        BANK_PT, BANK_OT, BANK_X = 4, 6, 7
        transposed = PS[:, BANK_PT:BANK_PT + 2].rearrange("p u n -> p (u n)")
        PT_PSUM = transposed[:, 0:(CHUNKS + 1) * P]
        VL_PSUM = PS[0:HG * LEFT, BANK_X, 0:D]

        x_loaded = sem("x_loaded"); ctx_loaded = sem("ctx_loaded"); small_loaded = sem("small_loaded")
        w_loaded = sem("w_loaded"); moe_loaded = sem("moe_loaded"); shared_loaded = sem("shared_loaded")
        mask_loaded = sem("mask_loaded"); last_loaded = sem("last_loaded"); const_ready = sem("const_ready")
        stage_done = sem("stage_done")
        kt_psum = sem("kt_psum"); v_psum = sem("v_psum"); kt_ready = sem("kt_ready")
        q_psum = sem("q_psum"); q_ready = sem("q_ready"); kbd_ready = sem("kbd_ready")
        vp1_ready = sem("vp1_ready"); vp2_ready = sem("vp2_ready")
        vl_psum = sem("vl_psum"); vs_ready = sem("vs_ready"); vl_ready = sem("vl_ready")
        s_psum = sem("s_psum"); max_ready = sem("max_ready"); shifted = sem("shifted"); exp_done = sem("exp_done")
        veps_ready = sem("veps_ready"); rstd_ready = sem("rstd_ready")
        rsum_ready = sem("rsum_ready"); p_ready = sem("p_ready"); pt_psum = sem("pt_psum"); pt_ready = sem("pt_ready")
        pv_done = sem("pv_done"); ot_ready = sem("ot_ready")
        o_psum = sem("o_psum"); o_taken = sem("o_taken"); stats_ready = sem("stats_ready"); xn_ready = sem("xn_ready")
        xt_psum = sem("xt_psum"); xt_ready = sem("xt_ready")
        prev_ready = sem("prev_ready"); r_mixed = sem("r_mixed"); k_mixed = sem("k_mixed")
        r_psum = sem("r_psum"); k_psum = sem("k_psum")
        r_ready = sem("r_ready"); r_used = sem("r_used"); krelu_ready = sem("krelu_ready"); ksq_ready = sem("ksq_ready")
        ctxs_ready = sem("ctxs_ready"); g_psum = sem("g_psum"); g_ready = sem("g_ready")
        lt_psum = sem("lt_psum"); lt_ready = sem("lt_ready"); lg_psum = sem("lg_psum")
        route_dve = sem("route_dve"); route_act = sem("route_act")
        xs_ready = sem("xs_ready"); h_psum = sem("h_psum"); silu_ready = sem("silu_ready"); hh_ready = sem("hh_ready")
        ht_psum = sem("ht_psum"); ht_ready = sem("ht_ready"); y_psum = sem("y_psum"); y_taken = sem("y_taken"); y_ready = sem("y_ready")
        rows_ready = sem("rows_ready"); scattered = [sem(f"scattered{i}") for i in range(4)]
        slots_zeroed = sem("slots_zeroed")
        rows_in = [sem(f"rows_in{i}") for i in range(2)]; rows_out = [sem(f"rows_out{i}") for i in range(2)]
        xt2_psum = sem("xt2_psum")
        gathered = [sem(f"gathered{i}") for i in range(4)]; gathered_used = sem("gathered_used")
        tri_ready = sem("tri_ready")
        taken_ready = sem("taken_ready"); count_psum = sem("count_psum")
        qi_ready = sem("qi_ready"); f_psum = sem("f_psum"); f_taken = sem("f_taken")
        part_amax = sem("part_amax"); biased = sem("biased"); all_amax = sem("all_amax"); w8_ready = sem("w8_ready")
        held = sem("held"); x_final = sem("x_final"); stored = sem("stored")
        block = ctx.enter_context(nc.Block())

        ST = {n: i + 1 for i, n in enumerate(
            ("setup", "a0", "f0", "m1", "r1", "e1", "n4", "a2", "r2", "s2", "e2", "n6", "a3", "q3"))}
        NORM = dict(setup=0, a0=8, f0=16, m1=24, n4=32, a2=40, n6=48, a3=56)
        SUM = dict(a0=0, f0=8, m1=16, a2=24, a3=32)
        LAYER = dict(a0=0, a2=1, a3=2)
        ALONE = dict(a0=HG // 2, a2=HG // 2, a3=HG)
        TOPK = dict(e1=2, e2=1)
        SLOTS = {s: NT * k + E - 1 for s, k in TOPK.items()}
        FIRST = dict(e1=0, s2=SLOTS["e1"], e2=SLOTS["e1"] + NT)
        FIRST_X = dict(e1=0, e2=SLOTS["e1"])
        WIDTH = dict(e1=F1, s2=F2, e2=F2)
        BUFS = dict(e1=("xs1", "ys1"), e2=("xs2", "ys2"))
        L1_DMAS = 4 * E
        MOE_LOADED = dict(e1=16 * L1_DMAS, e2=16 * (L1_DMAS + 3 * E))

        def end_stage(engine, name):
            engine.drain().then_inc(stage_done, 1)
            engine.wait_ge(stage_done, 4 * ST[name])

        SCATTERED = 16 * TOPK["e1"] * NT // 4

        def moved(stage, q, pairs=0):
            before = {"e1": 0, "e2": (SLOTS["e1"] + 1 - q) // 2,
                      None: (SLOTS["e1"] + 1 - q) // 2 + (SLOTS["e2"] + 1 - q) // 2}[stage]
            return pairs * 16 + 16 * before

        def tile_pipeline(engine, body, tiles, depth):
            warm = -(-depth // 2) + 1
            for s in range(2 * warm):
                body((s, s % 2, s // 2), lambda lag, s=s: lag <= s)
            with engine.Fori(warm, tiles // 2) as i:
                for j in range(2):
                    body((i * 2 + j, j, i), lambda lag: True)
            for s in range(tiles // 2 * 2, tiles + depth):
                body((s, s % 2, s // 2), lambda lag, s=s: s < tiles + lag)

        def hold(engine):
            engine.nop().then_inc(held, 1)

        def xt_of(b):
            return XT[:, bass.ds(b, 1), :, 1:S + 1].rearrange("p o g s -> p (o g) s")

        def x_of(b):
            return X[:, bass.ds(b * T, T), :]

        def repeat(ap, n):
            return ap.unsqueeze(1).to_broadcast([ap.shape[0], n, ap.shape[1]])

        def spread(ap, n):
            return ap.unsqueeze(2).to_broadcast([ap.shape[0], ap.shape[1], n])

        def l1_w(e, k):
            base = e * (2 * G * F1 + 3 * D) + k * G * F1
            return WE[:, base:base + G * F1].rearrange("p (g f) -> p g f", g=G)

        def l1_wd(e):
            base = e * (2 * G * F1 + 3 * D) + 2 * G * F1
            return WE[:, base:base + 3 * D].rearrange("p (c d) -> p c d", c=3)

        def l2_w(e, k):
            base = e * EW + k * G * F2
            return WE[:, base:base + G * F2].rearrange("p (g f) -> p g f", g=G)

        def l2_wd(e):
            base = e * EW + 2 * G * F2
            return WE[:, base:base + 4 * D].rearrange("p (c d) -> p c d", c=4)

        @block.sync
        def _(sp):
            def square(k, name):
                sp.dma_start(W[:, k], a[name].rearrange("(g p) n -> p g n", p=P)).then_inc(w_loaded, 16)

            def everywhere(dst, name, semaphore):
                sp.dma_start(dst, a[name].partition_broadcast(P)).then_inc(semaphore, 16)

            sp.dma_start(X[:, :, :], a["x"].rearrange("b (t p) d -> p (b t) d", p=P)).then_inc(x_loaded, 16)
            sp.dma_start(ctxT[:, :, :], a["ctxT"].rearrange("(g p) n -> p g n", p=P)).then_inc(ctx_loaded, 16)
            for k, name in enumerate(("L0_wqT", "L0_wkT", "L0_wvT", "L0_woT")):
                square(k, name)
            sp.dma_start(vecs[:, 0:4], a["L0_vecs"]).then_inc(small_loaded, 16)
            everywhere(rows[:, 0], "L0_bv", small_loaded)
            everywhere(rows[:, 1], "L0_bo", small_loaded)
            everywhere(MASKI, "mask0", small_loaded)
            sp.dma_start(BIAS, a["bias"].rearrange("b (t p) k -> p (b t) k", p=P)).then_inc(small_loaded, 16)
            sp.wait_ge(const_ready, 1)
            for buf, n in (("xs1", SLOTS["e1"]), ("xs2", SLOTS["e2"])):
                for i in range(0, n, ZT):
                    m = min(ZT, n - i)
                    sp.dma_start(a[buf][i * P:(i + m) * P].rearrange("(i p) d -> p i d", p=P),
                                 zeros[:, 0:m * D].rearrange("p (i d) -> p i d", i=m)).then_inc(slots_zeroed, 16)
            for e in range(E):
                for k, name in enumerate(("L1_w1", "L1_w3")):
                    sp.dma_start(l1_w(e, k), a[name][e].rearrange("(g p) f -> p g f", p=P)).then_inc(moe_loaded, 16)
                w2 = a["L1_w2"][e]
                sp.dma_start(l1_wd(e)[:, 0:2], w2[0:2 * P].rearrange("(c p) d -> p c d", p=P)).then_inc(moe_loaded, 16)
                sp.dma_start(l1_wd(e)[0:F1 - 2 * P, 2], w2[2 * P:F1]).then_inc(moe_loaded, 16)
            sp.wait_ge(stage_done, 4 * ST["a0"])
            for k, name in enumerate(("L0_WrT", "L0_WkT", "L0_WvT")):
                square(k, name)
            sp.dma_start(V, a["ctx"].rearrange("b k d -> k b d")).then_inc(ctx_loaded, 16)
            sp.wait_ge(stage_done, 4 * ST["f0"])
            square(0, "L2_WT")
            sp.dma_start(WR[:, :, :], a["L1_wrT"].rearrange("(g p) n -> p g n", p=P)).then_inc(w_loaded, 16)

            def expert_tiles(stage):
                xs, ys = a[BUFS[stage][0]], a[BUFS[stage][1]]
                first = FIRST_X[stage]

                def body(i, live):
                    if live(0):
                        n, q = first + i[0], i[1]
                        after(sp, xt2_psum, n - 1)
                        sp.dma_start(XR[:, q], xs[bass.ds((n - first) * P, P)]).then_inc(rows_in[q], 16)
                    if live(4):
                        n, q = first + i[0] - 4, i[1]
                        sp.wait_ge(y_ready, n + 1)
                        sp.dma_start(ys[bass.ds((n - first) * P, P)], YO[:, q]).then_inc(rows_out[q], 16)

                tile_pipeline(sp, body, SLOTS[stage], 4)

            sp.wait_ge(stage_done, 4 * ST["r1"])
            for s in scattered:
                sp.wait_ge(s, SCATTERED)
            expert_tiles("e1")
            sp.wait_ge(stage_done, 4 * ST["e1"])
            everywhere(rows[:, 1], "L2_b", mask_loaded)
            everywhere(MASKI, "mask2", mask_loaded)
            sp.dma_start(WR[:, :, :], a["L2_gateT"].rearrange("(g p) n -> p g n", p=P)).then_inc(mask_loaded, 16)
            sp.wait_ge(stage_done, 4 * ST["n4"])
            for e in range(E - 1):
                for k, name in enumerate(("L2_rgT", "L2_ruT")):
                    sp.dma_start(l2_w(e, k), a[name][e].rearrange("(g p) f -> p g f", p=P)).then_inc(moe_loaded, 16)
                sp.dma_start(l2_wd(e), a["L2_rdT"][e].rearrange("(c p) d -> p c d", p=P)).then_inc(moe_loaded, 16)
            sp.wait_ge(stage_done, 4 * ST["a2"])
            for k, name in enumerate(("L2_sgT", "L2_suT")):
                sp.dma_start(shared_w[k].rearrange("p (g f) -> p g f", g=G),
                             a[name].rearrange("(g p) f -> p g f", p=P)).then_inc(shared_loaded, 16)
            sp.dma_start(shared_wd.rearrange("p (c d) -> p c d", c=4),
                         a["L2_sdT"].rearrange("(c p) d -> p c d", p=P)).then_inc(shared_loaded, 16)
            for k, name in enumerate(("L2_rgT", "L2_ruT")):
                sp.dma_start(l2_w(E - 1, k), a[name][E - 1].rearrange("(g p) f -> p g f", p=P)).then_inc(moe_loaded, 16)
            sp.dma_start(l2_wd(E - 1), a["L2_rdT"][E - 1].rearrange("(c p) d -> p c d", p=P)).then_inc(moe_loaded, 16)
            sp.wait_ge(stage_done, 4 * ST["s2"])
            for k, name in enumerate(("L3_Wq", "L3_Wk", "L3_Wv", "L3_Wo")):
                square(k, name)
            for s in scattered[0:2]:
                sp.wait_ge(s, SCATTERED + 16 * NT // 2)
            expert_tiles("e2")
            sp.wait_ge(stage_done, 4 * ST["e2"])
            sp.dma_start(W8f.bitcast(I32)[:, 0:G * D // 4].rearrange("p (g n) -> p g n", g=G),
                         a["L3_w8T"].rearrange("(g p) n -> p g n", p=P)).then_inc(last_loaded, 16)
            everywhere(rows[:, 0], "L3_ws", last_loaded)
            everywhere(rows[:, 1], "L3_bias", last_loaded)
            with sp.Fori(0, B) as b:
                sp.wait_ge(x_final, b + 1)
                sp.dma_start(a["out"][bass.ds(b, 1)].rearrange("o (t p) d -> p (o t) d", p=P), x_of(b)).then_inc(stored, 16)
            sp.wait_ge(stored, 16 * B)

        @block.gpsimd
        def _(pool):
            def deviations(n, b):
                after(pool, rstd_ready, n)
                pool.wait_ge(stats_ready, n + 1)
                pool.tensor_copy(MEANS[:, bass.ds(b * T, T)], mv[:, :, 0])
                pool.tensor_tensor(veps[:, :], mv[:, :, 1], epsv[:, :], ALU.add).then_inc(veps_ready, 1)
                pool.wait_ge(veps_ready, n + 1)
                pool.tensor_tensor(RSTDS[:, bass.ds(b * T, T)], veps[:, :], halfpow[:, :], ALU.pow).then_inc(rstd_ready, 1)

            def attention(stage, keys):
                layer, norms, alone = LAYER[stage], NORM[stage], ALONE[stage]
                u0, b0 = B * UNITS * layer, B * layer

                def block_diagonal_keys(b, g):
                    after(pool, s_psum, u0 + UNITS * b - 2 + 2 * g)
                    k = keys[:, g, bass.ds(b * SK, SK)]
                    pool.tensor_tensor(KBD[:, g].rearrange("p (h k) -> p h k", h=HG), repeat(k, HG),
                                       spread(headmask[:, :], SK), ALU.mult).then_inc(kbd_ready, 1)

                def first_values(b, g):
                    after(pool, pv_done, u0 + UNITS * b - 2 + 2 * g)
                    v = V[0:HALF, bass.ds(b, 1), g * P:(g + 1) * P].rearrange("k o (m i d) -> k (o m) i d", i=2, d=DH)
                    pool.tensor_copy(VP[0:HALF, g, :, 0:DH], v[:, :, 0]).then_inc(vp1_ready, 1)

                def last_values(b):
                    pool.wait_ge(vs_ready, b0 + b + 1)
                    after(pool, pv_done, u0 + UNITS * b)
                    pool.tensor_tensor(VL[0:HG * LEFT].rearrange("k g (h d) -> k g h d", h=HG),
                                       VS[:, :].rearrange("k (g h d) -> k g h d", g=G, h=HG),
                                       spread(leftmask[0:HG * LEFT, :], DH).unsqueeze(1).to_broadcast([HG * LEFT, G, HG, DH]),
                                       ALU.mult).then_inc(vl_ready, 1)

                def body(b, j, live):
                    if j == 1 and live(13):
                        deviations(norms + b - 3, b - 3)
                    if live(3) and alone < HG:
                        u, q = u0 + UNITS * b + j - 3, (j + 1) % 2
                        pool.wait_ge(max_ready, u + 1)
                        s = SC[:, (j - 3) % 4, alone * SK:].rearrange("p (h k) -> p h k", k=SK)
                        pool.tensor_tensor(s, s, spread(mx[:, q, alone:], SK), ALU.add).then_inc(shifted, 1)
                    if live(4):
                        u, q = u0 + UNITS * b + j - 4, j % 2
                        pool.wait_ge(rsum_ready, u + 1)
                        after(pool, pt_psum, u - 1)
                        s = SC[:, (j - 4) % 4].rearrange("p (h k) -> p h k", h=HG)
                        pool.tensor_tensor(PN[:, q, 0:CHUNKS * P].rearrange("p (h k) -> p h k", h=HG), s[:, :, 0:HALF],
                                           spread(rs[:, q], HALF), ALU.mult)
                        pool.tensor_tensor(PN[:, q, CHUNKS * P:PW].rearrange("p (h k) -> p h k", h=HG), s[:, :, HALF:SK],
                                           spread(rs[:, q], LEFT), ALU.mult).then_inc(p_ready, 1)
                    if j == 1 and live(5):
                        last_values(b - 1)
                    if j == 0 and live(0):
                        block_diagonal_keys(b, 0)
                    if j == 0 and live(4):
                        first_values(b - 1, 0)
                    if j == 2 and live(6):
                        first_values(b - 1, 1)
                    if j == 2 and live(0):
                        block_diagonal_keys(b, 1)

                software_pipeline(pool, body, UNITS, 10, 3)

            pool.memset(epsv[:, :], EPS)
            pool.memset(halfpow[:, :], -0.5)
            pool.memset(ident[:, :], 0.0)
            pool.memset(headmask[:, :], 1.0)
            pool.memset(causal[:, :], 0.0)
            pool.memset(VP[:, :, :, :], 0.0)
            pool.memset(leftmask[:, :], 1.0)
            pool.memset(spreader[:, :], 0.0)
            pool.memset(XT[:, :, :, 0:1], 0.0)
            pool.memset(zeros, 0.0)
            pool.iota(iota_i[:, :], pattern=[[1, SLOTS["e1"]]], base=0, channel_multiplier=0)
            for e in range(E):
                pool.memset(rank8[:, e:e + 1], float(E - e))
            pool.drain()
            pool.affine_select(out=ident[:, :], in_=ident[:, :], compare_op=ALU.not_equal, fill=1.0, base=0,
                               pattern=[[-1, P]], channel_multiplier=1)
            pool.affine_select(out=headmask[:, :], in_=headmask[:, :], compare_op=ALU.is_ge, fill=0.0, base=0,
                               pattern=[[-DH, HG]], channel_multiplier=1)
            pool.affine_select(out=causal[:, :], in_=causal[:, :], compare_op=ALU.is_ge, fill=NEG, base=0,
                               pattern=[[-1, SK]], channel_multiplier=1)
            pool.affine_select(out=leftmask[:, :], in_=leftmask[:, :], compare_op=ALU.is_ge, fill=0.0, base=0,
                               pattern=[[-LEFT, HG]], channel_multiplier=1)
            pool.affine_select(out=spreader[:, :].rearrange("p (h i) -> p h i", h=HG),
                               in_=spreader[:, :].rearrange("p (h i) -> p h i", h=HG), compare_op=ALU.not_equal, fill=1.0,
                               base=-HALF, pattern=[[0, HG], [-1, LEFT]], channel_multiplier=1)
            pool.drain()
            pool.affine_select(out=headmask[:, :], in_=headmask[:, :], compare_op=ALU.is_ge, fill=0.0, base=DH - 1,
                               pattern=[[DH, HG]], channel_multiplier=-1)
            pool.affine_select(out=leftmask[:, :], in_=leftmask[:, :], compare_op=ALU.is_ge, fill=0.0, base=LEFT - 1,
                               pattern=[[LEFT, HG]], channel_multiplier=-1)
            pool.drain().then_inc(const_ready, 1)
            pool.wait_ge(x_loaded, 16)

            def plain_norm(stage):
                with pool.Fori(0, B) as b:
                    deviations(NORM[stage] + b, b)

            plain_norm("setup")
            end_stage(pool, "setup")
            attention("a0", KT)
            end_stage(pool, "a0")

            def ffn_body(b, j, live):
                if live(0):
                    after(pool, r_mixed, b)
                    for dst, k in ((tA, 4), (tB, 5)):
                        for g in range(G):
                            prev = XT[:, bass.ds(b, 1), g, 0:S].rearrange("p o s -> p (o s)")
                            last = pool.tensor_tensor(dst[:, g], prev, vecs[:, k, g:g + 1].to_broadcast([P, S]), ALU.mult)
                    last.then_inc(prev_ready, 1)
                if live(3):
                    deviations(NORM["f0"] + b - 3, b - 3)

            software_pipeline(pool, ffn_body, 1, 3, 3)
            end_stage(pool, "f0")

            def mlp_body(b, j, live):
                if live(0):
                    after(pool, g_psum, b)
                    pool.tensor_copy(ctxS, ctxT[:, :, bass.ds(b * SK, SK)]).then_inc(ctxs_ready, 1)
                if live(2):
                    deviations(NORM["m1"] + b - 2, b - 2)

            software_pipeline(pool, mlp_body, 1, 2, 2)
            end_stage(pool, "m1")

            def scatter(stage, first, buffers):
                slots = a[BUFS[stage][0]]
                for t in range(NT):
                    pool.wait_ge(rows_ready, first + t + 1)
                    for k in range(TOPK[stage]):
                        pool.indirect_dma_start(slots[:, :], bass.IndirectOffsetOnAxis(ap=slot_u[:, k, t:t + 1], axis=0),
                                                XD[:, t % buffers], None).then_inc(scattered[t % buffers], 16)

            def all_rows_out(following):
                for q in range(2):
                    pool.wait_ge(rows_out[q], moved(following, q))

            def gather(stage, first, norms):
                slots = a[BUFS[stage][1]]
                K = TOPK[stage]
                for t in range(NT):
                    after(pool, gathered_used, first + t - 3)
                    for k in range(K):
                        pool.indirect_dma_start(YG[:, t % 4, k], None, slots[:, :],
                                                bass.IndirectOffsetOnAxis(ap=slot_u[:, k, t:t + 1], axis=0)).then_inc(gathered[t % 4], 16)
                    if t % T == T - 1 and t // T >= 2:
                        deviations(norms + t // T - 2, t // T - 2)
                for b in range(B - 2, B):
                    deviations(norms + b, b)

            def triangle():
                pool.memset(tri, 1.0)
                pool.memset(ones, 1.0)
                pool.drain()
                pool.affine_select(out=tri, in_=tri, compare_op=ALU.is_gt, fill=0.0, base=0,
                                   pattern=[[1, P]], channel_multiplier=-1)
                pool.drain().then_inc(tri_ready, 1)

            triangle()
            end_stage(pool, "r1")
            pool.wait_ge(slots_zeroed, 16 * (-(-SLOTS["e1"] // ZT) - (-SLOTS["e2"] // ZT)))
            scatter("e1", 0, 4)
            end_stage(pool, "e1")

            all_rows_out("e2")
            gather("e1", 0, NORM["n4"])
            end_stage(pool, "n4")
            attention("a2", ctxT)
            end_stage(pool, "a2")
            triangle()
            end_stage(pool, "r2")
            scatter("e2", NT, 2)
            end_stage(pool, "s2")
            end_stage(pool, "e2")
            all_rows_out(None)
            gather("e2", NT, NORM["n6"])
            end_stage(pool, "n6")
            attention("a3", KT)
            end_stage(pool, "a3")
            pool.wait_ge(part_amax, 1)
            pool.partition_all_reduce(qsc[:, 1:2], qsc[:, 0:1], P, bass.bass_isa.ReduceOp.max).then_inc(all_amax, 1)
            with pool.Fori(0, B) as b:
                pool.tensor_tensor(x_of(b), x_of(b), repeat(rows[:, 1], T), ALU.add).then_inc(biased, 1)
            end_stage(pool, "q3")

        @block.scalar
        def _(act):
            def xt_evacuate(n, b):
                act.wait_ge(xt_psum, n + 1)
                hold(act)
                act.activation(xt_of(b), PS[:, BANK_X].rearrange("p (g s) -> p g s", g=G), ACT.Copy).then_inc(xt_ready, 1)

            def plain_norm(stage):
                with act.Fori(0, B) as b:
                    xt_evacuate(NORM[stage] + b, b)

            def keys_evacuate(first, bias, between=lambda: None):
                for g in range(G):
                    act.wait_ge(kt_psum, first + g + 1)
                    dst = KT[:, g].rearrange("p (i n) -> p i n", i=2)
                    src = PS[:, 2 * g:2 * g + 2, 0:KW // 2]
                    if bias:
                        act.activation(dst, src, ACT.Identity, bias=vecs[:, 1, g:g + 1]).then_inc(kt_ready, 1)
                    else:
                        act.activation(dst, src, ACT.Copy).then_inc(kt_ready, 1)
                    between()

            def attention(stage):
                layer, norms, alone = LAYER[stage], NORM[stage], ALONE[stage]
                u0, b0, q0 = B * UNITS * layer, B * layer, 0 if stage == "a0" else B

                def queries(b):
                    after(act, s_psum, u0 + UNITS * b)
                    hold(act)
                    if stage == "a2":
                        act.activation(QT, xt_of(b), ACT.Copy, scale=DH ** -0.5).then_inc(q_ready, 1)
                        return
                    act.wait_ge(q_psum, q0 + b + 1)
                    src = PS[:, BANK_X].rearrange("p (g s) -> p g s", g=G)
                    if stage == "a3":
                        act.activation(QT, src, ACT.Copy, scale=DH ** -0.5).then_inc(q_ready, 1)
                        return
                    for g in range(G):
                        last = act.activation(QT[:, g], src[:, g], ACT.Identity, scale=DH ** -0.5, bias=vecs[:, 0, g:g + 1])
                    last.then_inc(q_ready, 1)

                def second_values(b, g):
                    after(act, pv_done, u0 + UNITS * b - 2 + 2 * g)
                    v = V[0:HALF, bass.ds(b, 1), g * P:(g + 1) * P].rearrange("k o (m i d) -> k (o m) i d", i=2, d=DH)
                    hold(act)
                    act.activation(VP[HALF:P, g, :, DH:2 * DH], v[:, :, 1], ACT.Copy).then_inc(vp2_ready, 1)

                def body(b, j, live):
                    if j == 1 and live(0):
                        queries(b)
                    if live(3):
                        u, q = u0 + UNITS * b + j - 3, (j + 1) % 2
                        act.wait_ge(max_ready, u + 1)
                        after(act, rsum_ready, u - 1)
                        for h in range(alone):
                            s = SC[:, (j - 3) % 4, h * SK:(h + 1) * SK]
                            last = act.activation(s, s, ACT.Exp, bias=mx[:, q, h:h + 1], accum_out=sm[:, q, h:h + 1])
                        if alone < HG:
                            act.wait_ge(shifted, u + 1)
                            s = SC[:, (j - 3) % 4, alone * SK:]
                            last = act.activation(s, s, ACT.Exp)
                        last.then_inc(exp_done, 1)
                    if live(5):
                        u = u0 + UNITS * b + j - 5
                        act.wait_ge(pt_psum, u + 1)
                        after(act, pv_done, u)
                        act.activation(PT, PT_PSUM, ACT.Copy).then_inc(pt_ready, 1)
                    if j == 1 and live(9):
                        act.wait_ge(pv_done, u0 + UNITS * (b - 1))
                        after(act, o_psum, SUM[stage] + b - 2)
                        act.activation(OT, PS[:, BANK_OT].rearrange("p (g s) -> p g s", g=G), ACT.Copy).then_inc(ot_ready, 1)
                    if j == 0 and live(4):
                        second_values(b - 1, 0)
                    if j == 2 and live(6):
                        second_values(b - 1, 1)
                    if j == 1 and live(13):
                        xt_evacuate(norms + b - 3, b - 3)
                    if j == 3 and live(0):
                        act.wait_ge(vl_psum, b0 + b + 1)
                        after(act, vl_ready, b0 + b)
                        act.activation(VS[:, :], VL_PSUM, ACT.Copy).then_inc(vs_ready, 1)

                software_pipeline(act, body, UNITS, 10, 3)
                end_stage(act, stage)

            first_norms = iter(range(B))

            def first_norm():
                b = next(first_norms)
                xt_evacuate(b, b)

            first_norm()
            first_norm()
            act.wait_ge(small_loaded, 16 * 5)
            keys_evacuate(0, True, between=first_norm)
            for b in first_norms:
                xt_evacuate(b, b)
            end_stage(act, "setup")
            attention("a0")

            def ffn_body(b, j, live):
                if live(0):
                    act.wait_ge(k_psum, b + 1)
                    act.activation(krelu, PS[:, 1].rearrange("p (g s) -> p g s", g=G), ACT.Relu).then_inc(krelu_ready, 1)
                    act.drain()
                    after(act, o_psum, SUM["f0"] + b)
                    act.activation(ksq, krelu, ACT.Square).then_inc(ksq_ready, 1)
                    act.wait_ge(r_psum, b + 1)
                    after(act, r_used, b)
                    act.activation(rsig, PS[:, 0].rearrange("p (g s) -> p g s", g=G), ACT.Sigmoid).then_inc(r_ready, 1)
                    act.drain()
                if live(2):
                    xt_evacuate(NORM["f0"] + b - 2, b - 2)

            software_pipeline(act, ffn_body, 1, 2, 2)
            end_stage(act, "f0")

            def mlp_body(b, j, live):
                if live(0):
                    act.wait_ge(g_psum, b + 1)
                    act.wait_ge(o_psum, SUM["m1"] + b)
                    act.activation(gel, PS[0:SK, 0, 0:S], ACT.Gelu_apprx_tanh).then_inc(g_ready, 1)
                if live(3):
                    xt_evacuate(NORM["m1"] + b - 3, b - 3)

            software_pipeline(act, mlp_body, 1, 3, 3)
            end_stage(act, "m1")

            def route(stage, first):
                for n in range(B // 2):
                    act.wait_ge(lt_psum, first + n + 1)
                    after(act, lg_psum, first + n - 1)
                    act.activation(LTs[:, n % 2], PS[0:E, 2 * (n % 2)], ACT.Copy).then_inc(lt_ready, 1)
                act.wait_ge(route_dve, first // (B // 2) + 1)
                if stage == "r1":
                    act.activation(PR[:, :, :], LG[:, :, :], ACT.Exp).then_inc(route_act, 1)
                else:
                    act.activation(score[:, :], top[:, 0], ACT.Sigmoid).then_inc(route_act, 1)
                end_stage(act, stage)

            def experts(stage):
                F, u0 = WIDTH[stage], FIRST[stage]
                chunks = -(-F // P)

                def body(i, live):
                    if live(0):
                        u, q = u0 + i[0], i[1]
                        after(act, h_psum, u - 1)
                        if stage == "s2":
                            src = XT[:, bass.ds(i[2], 1), :, 1 + q * P:1 + (q + 1) * P].rearrange("p o g s -> p (o g) s")
                            hold(act)
                            act.activation(XS[:, q], src, ACT.Copy).then_inc(xs_ready, 1)
                        else:
                            act.wait_ge(xt2_psum, FIRST_X[stage] + i[0] + 1)
                            act.activation(XS[:, q], PS[:, 7, 0:D].rearrange("p (g s) -> p g s", g=G), ACT.Copy).then_inc(xs_ready, 1)
                    if live(1):
                        u, q = u0 + i[0] - 1, 1 - i[1]
                        act.wait_ge(h_psum, u + 1)
                        after(act, hh_ready, u - 1)
                        act.activation(SL[:, q, 0:F], PS[:, 2 * q, 0:F], ACT.Silu).then_inc(silu_ready, 1)
                    if live(2):
                        u, q = u0 + i[0] - 2, i[1]
                        act.wait_ge(ht_psum, u + 1)
                        after(act, y_psum, u - 1)
                        whole = F // P
                        last = act.activation(HT[:, q, 0:whole], PS[:, 4 + q, 0:whole * P].rearrange("p (c s) -> p c s", s=P), ACT.Copy)
                        if whole < chunks:
                            n = F - whole * P
                            last = act.activation(HT[0:n, q, whole], PS[0:n, 4 + q, whole * P:chunks * P], ACT.Copy)
                        last.then_inc(ht_ready, 1)

                tile_pipeline(act, body, NT if stage == "s2" else SLOTS[stage], 2)
                end_stage(act, stage)

            route("r1", 0)
            experts("e1")
            plain_norm("n4")
            end_stage(act, "n4")
            attention("a2")
            route("r2", B // 2)
            experts("s2")
            experts("e2")
            keys_evacuate(G, False)
            plain_norm("n6")
            end_stage(act, "n6")
            attention("a3")
            end_stage(act, "q3")

        @block.vector
        def _(dve):
            def add_sum(stage, b, bank=BANK_X, times=None):
                dve.wait_ge(o_psum, SUM[stage] + b + 1)
                result = PS[:, bank].rearrange("p (t d) -> p t d", t=T)
                if times is not None:
                    dve.tensor_tensor(rv, result, times, ALU.mult).then_inc(r_used, 1)
                    dve.drain()
                    result = rv
                dve.tensor_tensor(x_of(b), x_of(b), result, ALU.add).then_inc(o_taken, 1)
                dve.drain()

            def row_stats(n, b):
                dve.drain()
                for t in range(T):
                    dve.bn_stats(st[:, t], X[:, bass.ds(b * T + t, 1), :].rearrange("p o d -> p (o d)"))
                after(dve, veps_ready, n)
                hold(dve)
                dve.drain()
                for t in range(T):
                    last = dve.bn_aggr(mv[:, t], st[:, t])
                last.then_inc(stats_ready, 1)

            def normalise(n, b):
                dve.wait_ge(rstd_ready, n + 1)
                after(dve, xt_psum, n)
                for t in range(T):
                    row = b * T + t
                    last = dve.tensor_scalar(XN[:, t], X[:, bass.ds(row, 1), :].rearrange("p o d -> p (o d)"),
                                             MEANS[:, bass.ds(row, 1)], RSTDS[:, bass.ds(row, 1)], ALU.subtract, ALU.mult)
                last.then_inc(xn_ready, 1)

            def plain_norm(stage):
                def body(b, j, live):
                    if live(0):
                        row_stats(NORM[stage] + b, b)
                    if live(1):
                        normalise(NORM[stage] + b - 1, b - 1)

                software_pipeline(dve, body, 1, 1, 1)

            def values_evacuate(first, bias):
                for i in range(4):
                    dve.wait_ge(v_psum, first + i + 1)
                    src = PS[0:SK, (4, 5, 6, 0)[i]].rearrange("k (b d) -> k b d", b=2)
                    if bias:
                        last = dve.tensor_tensor(V[:, 2 * i:2 * i + 2], src, repeat(rows[0:SK, 0], 2), ALU.add)
                    else:
                        last = dve.tensor_copy(V[:, 2 * i:2 * i + 2], src)

            def attention(stage):
                layer, norms, alone = LAYER[stage], NORM[stage], ALONE[stage]
                u0, b0 = B * UNITS * layer, B * layer

                def body(b, j, live):
                    if live(3):
                        u, q, t = u0 + UNITS * b + j - 3, (j + 1) % 2, (j + 1) % T
                        bt = b if j == 3 else b - 1
                        dve.wait_ge(s_psum, u + 1)
                        after(dve, p_ready, u - 3)
                        after(dve, exp_done, u - 1)
                        s, sc = PS[:, 2 * q:2 * q + 2, 0:KW // 2], SC[:, (j - 3) % 4]
                        if stage == "a3":
                            z = Z[:, q].rearrange("p (i n) -> p i n", i=2)
                            dve.tensor_scalar(z, s, 0.0, NEG, ALU.is_equal, ALU.mult)
                            dve.drain()
                            dve.tensor_tensor(sc.rearrange("p (i n) -> p i n", i=2), s, z, ALU.add)
                        else:
                            bias = BIAS[:, bass.ds(T * bt + t, 1), :].unsqueeze(1).to_broadcast([P, 2, HG // 2, SK])
                            dve.tensor_tensor(sc.rearrange("p (i h k) -> p i h k", i=2, k=SK),
                                              s.rearrange("p i (h k) -> p i h k", k=SK), bias, ALU.add)
                        dve.drain()
                        dve.tensor_reduce(mx[:, q], sc.rearrange("p (h k) -> p h k", h=HG), AX.X,
                                          ALU.max, negate=True).then_inc(max_ready, 1)
                    if live(4):
                        u, q = u0 + UNITS * b + j - 4, j % 2
                        dve.wait_ge(exp_done, u + 1)
                        after(dve, p_ready, u - 1)
                        if alone < HG:
                            s = SC[:, (j - 4) % 4, alone * SK:].rearrange("p (h k) -> p h k", k=SK)
                            dve.tensor_reduce(sm[:, q, alone:], s, AX.X, ALU.add)
                            dve.drain()
                        dve.reciprocal(rs[:, q], sm[:, q]).then_inc(rsum_ready, 1)
                    if j == 0 and live(8) and stage != "a3":
                        dve.tensor_tensor(x_of(b - 2), x_of(b - 2), repeat(rows[:, 1], T), ALU.add)
                        dve.drain()
                    if j == 0 and live(12):
                        row_stats(norms + b - 3, b - 3)
                    if j == 1 and live(13):
                        normalise(norms + b - 3, b - 3)
                        if stage == "a3":
                            dve.drain()
                            dve.tensor_reduce(amax[:, bass.ds(b - 3, 1)], XN[:, :, :], AX.XY, ALU.max,
                                              apply_absolute_value=True)
                            dve.drain()
                    if j == 3 and live(11):
                        add_sum(stage, b - 2)

                software_pipeline(dve, body, UNITS, 10, 3)
                end_stage(dve, stage)

            dve.wait_ge(x_loaded, 16)
            plain_norm("setup")
            dve.wait_ge(small_loaded, 16 * 5)
            dve.tensor_scalar(MASKF, MASKI, 0, None, ALU.not_equal)
            dve.tensor_scalar(vecs[:, 4:6], vecs[:, 2:4], -1.0, 1.0, ALU.mult, ALU.add)
            dve.drain()
            pad = KBDf[:, B * SK:2 * B * SK]
            dve.tensor_scalar(pad, MASKF, -1.0, -PAD, ALU.add, ALU.mult)
            bias4 = BIASf.rearrange("p (b t k) -> p b t k", b=B, t=T)
            by_tile = lambda ap: ap.rearrange("p (b k) -> p b k", b=B).unsqueeze(2).to_broadcast([P, B, T, SK])
            dve.tensor_tensor(bias4, bias4, by_tile(MASKF), ALU.mult)
            dve.drain()
            dve.tensor_tensor(bias4, bias4, by_tile(pad), ALU.add)
            values_evacuate(0, True)
            dve.memset(PS[96:P, BANK_PT + 1, 0:P], 0.0)
            dve.wait_ge(kt_ready, G)
            dve.tensor_tensor(KT, KT, repeat(MASKF, G), ALU.mult)
            dve.tensor_scalar(vecs[:, 0], vecs[:, 0], DH ** -0.5, None, ALU.mult)
            end_stage(dve, "setup")
            attention("a0")

            def ffn_body(b, j, live):
                if live(0):
                    dve.wait_ge(prev_ready, b + 1)
                    for dst, prev, k, used, ready in ((xkT, tB, 3, k_psum, k_mixed), (xrT, tA, 2, r_psum, r_mixed)):
                        after(dve, used, b)
                        for g in range(G):
                            now = XT[:, bass.ds(b, 1), g, 1:S + 1].rearrange("p o s -> p (o s)")
                            last = dve.scalar_tensor_tensor(out=dst[:, g], in0=now, scalar=vecs[:, k, g:g + 1],
                                                            in1=prev[:, g], op0=ALU.mult, op1=ALU.add)
                        last.then_inc(ready, 1)
                        if dst is xkT and live(3):
                            normalise(NORM["f0"] + b - 3, b - 3)
                elif live(3):
                    normalise(NORM["f0"] + b - 3, b - 3)
                if live(2):
                    dve.wait_ge(r_ready, b - 1)
                    add_sum("f0", b - 2, bank=6, times=rsig)
                    row_stats(NORM["f0"] + b - 2, b - 2)

            software_pipeline(dve, ffn_body, 1, 3, 3)
            end_stage(dve, "f0")

            def mlp_body(b, j, live):
                if live(2):
                    add_sum("m1", b - 2, bank=6)
                    row_stats(NORM["m1"] + b - 2, b - 2)
                if live(3):
                    normalise(NORM["m1"] + b - 3, b - 3)

            software_pipeline(dve, mlp_body, 1, 3, 3)
            end_stage(dve, "m1")

            def running_sums(ping, pong, n, keep):
                reach = 1
                while reach < n:
                    dve.tensor_tensor(keep(pong, reach, n), keep(ping, reach, n), keep(ping, 0, n - reach), ALU.add)
                    dve.tensor_copy(keep(pong, 0, reach), keep(ping, 0, reach))
                    dve.drain()
                    ping, pong, reach = pong, ping, 2 * reach
                return ping

            def route(stage, first):
                to = dict(r1="e1", r2="e2")[stage]
                K, n_slots = TOPK[to], SLOTS[to]
                dve.tensor_copy(iota_f[:, :], iota_i[:, :])
                dve.drain()
                dve.tensor_scalar(iota_p[:, :], iota_f[:, 0:NT], float(P), None, ALU.mult)
                dve.wait_ge(lg_psum, first + B // 2)
                dve.tensor_copy(LG[:, :, :], PS[:, 1, 0:NT * E].rearrange("p (t e) -> p t e", t=NT))
                dve.drain()
                logits = LG[:, :, :]
                for k in range(K):
                    if k:
                        dve.scalar_tensor_tensor(out=count[:, 1], in0=hot[:, k - 1], scalar=NEG, in1=logits,
                                                 op0=ALU.mult, op1=ALU.add)
                        dve.drain()
                        logits = count[:, 1]
                    dve.tensor_reduce(top[:, k], logits, AX.X, ALU.max)
                    dve.drain()
                    dve.tensor_tensor(count[:, 0], logits, spread(top[:, k], E), ALU.is_equal)
                    dve.drain()
                    dve.tensor_tensor(count[:, 0], count[:, 0], repeat(rank8[:, :], NT), ALU.mult)
                    dve.drain()
                    dve.tensor_reduce(first_rank[:, :], count[:, 0], AX.X, ALU.max)
                    dve.drain()
                    dve.tensor_tensor(hot[:, k], spread(first_rank[:, :], E), repeat(rank8[:, :], NT), ALU.is_equal)
                    dve.drain()
                if stage == "r1":
                    dve.tensor_tensor(LG[:, :, :], LG[:, :, :], spread(top[:, 0], E), ALU.subtract)
                dve.drain().then_inc(route_dve, 1)
                if K == 2:
                    dve.tensor_tensor(taken[:, :, :], hot[:, 0], hot[:, 1], ALU.add)
                else:
                    dve.tensor_copy(taken[:, :, :], hot[:, 0])
                dve.drain().then_inc(taken_ready, 1)
                dve.wait_ge(count_psum, first // (B // 2) + 1)
                dve.tensor_copy(count[:, 0], PS[:, 3, 0:NT * E].rearrange("p (t e) -> p t e", e=E))
                dve.drain()
                dve.tensor_copy(count[:, 1], count[:, 0])
                dve.drain()
                upto = running_sums(count[:, 1], count[:, 2], NT, lambda x, lo, hi: x[:, lo:hi])
                slot = count[:, 3]
                dve.tensor_tensor(slot, upto, count[:, 0], ALU.subtract)
                dve.tensor_tensor(whole[:, :, :], upto[:, NT - 1].unsqueeze(2).to_broadcast([P, E, NT]),
                                  iota_p[:, :].unsqueeze(1).to_broadcast([P, E, NT]), ALU.is_gt)
                dve.drain()
                dve.tensor_tensor(slot, slot, PS[:, 2, 0:NT * E].rearrange("p (t e) -> p t e", e=E), ALU.add)
                dve.tensor_reduce(tiles_of[:, 0], whole[:, :, :], AX.X, ALU.add)
                dve.drain()
                dve.tensor_copy(tiles_of[:, 1], tiles_of[:, 0])
                dve.drain()
                end = running_sums(tiles_of[:, 1], tiles_of[:, 2], E, lambda x, lo, hi: x[:, lo:hi])
                start = tiles_of[:, 3]
                dve.tensor_tensor(start, end, tiles_of[:, 0], ALU.subtract)
                dve.tensor_tensor(past[:, 0:n_slots], iota_f[:, 0:n_slots].unsqueeze(2).to_broadcast([P, n_slots, E]),
                                  end.unsqueeze(1).to_broadcast([P, n_slots, E]), ALU.is_ge)
                dve.drain()
                dve.tensor_scalar(start, start, float(P), None, ALU.mult)
                dve.tensor_reduce(owner[:, 0:n_slots], past[:, 0:n_slots], AX.X, ALU.add)
                dve.drain()
                dve.tensor_tensor(slot, slot, start.unsqueeze(1).to_broadcast([P, NT, E]), ALU.add)
                stride = 2 * G * F1 + 3 * D if to == "e1" else EW
                dve.tensor_scalar(owner[:, 0:n_slots], owner[:, 0:n_slots], float(E - 1), float(stride), ALU.min, ALU.mult)
                dve.drain()
                dve.tensor_copy(owner_i[:, 0:n_slots], owner[:, 0:n_slots])
                for k in range(K):
                    dve.tensor_tensor(picked[:, k], hot[:, k], slot, ALU.mult)
                dve.drain()
                for k in range(K):
                    dve.tensor_reduce(slot_f[:, k], picked[:, k], AX.X, ALU.add)
                dve.drain()
                dve.tensor_copy(slot_u[:, 0:K], slot_f[:, 0:K])
                if stage == "r2":
                    dve.wait_ge(route_act, first // (B // 2) + 1)
                    dve.tensor_tensor(RSTDS[:, :], RSTDS[:, :], score[:, :], ALU.mult)
                    dve.drain()
                end_stage(dve, stage)

            def rows_out_of_x(t, buffer, sent):
                after(dve, scattered[buffer], sent)
                x = X[:, bass.ds(t, 1), :].rearrange("p o d -> p (o d)")
                dve.tensor_scalar(XD[:, buffer], x, MEANS[:, bass.ds(t, 1)], RSTDS[:, bass.ds(t, 1)],
                                  ALU.subtract, ALU.mult).then_inc(rows_ready, 1)

            def experts(stage):
                F, u0 = WIDTH[stage], FIRST[stage]

                def body(i, live):
                    if stage == "s2" and live(0):
                        rows_out_of_x(i[0], i[1], i[2] * 16 + SCATTERED)
                    if live(1):
                        u, q = u0 + i[0] - 1, 1 - i[1]
                        dve.wait_ge(silu_ready, u + 1)
                        after(dve, ht_psum, u - 1)
                        dve.tensor_tensor(HH[:, q, 0:F], PS[:, 2 * q + 1, 0:F], SL[:, q, 0:F], ALU.mult).then_inc(hh_ready, 1)
                    if live(3):
                        u, q = u0 + i[0] - 3, 1 - i[1]
                        y = PS[:, 6, 0:D]
                        if stage == "s2":
                            x = X[:, bass.ds(i[0] - 3, 1), :].rearrange("p o d -> p (o d)")
                            dve.drain()
                            dve.wait_ge(y_psum, u + 1)
                            dve.tensor_tensor(x, x, y, ALU.add).then_inc(y_taken, 1)
                        else:
                            dve.wait_ge(y_psum, u + 1)
                            after(dve, rows_out[q], moved(stage, q, i[2] - (2 if i[1] == 0 else 1)))
                            dve.tensor_copy(YO[:, q], y).then_inc(y_taken, 1)
                            dve.drain().then_inc(y_ready, 1)

                tile_pipeline(dve, body, NT if stage == "s2" else SLOTS[stage], 3)
                end_stage(dve, stage)

            def add_gathered(to, norm, first):
                K, before = TOPK[to], 0 if to == "e1" else SCATTERED
                dve.drain()
                def body(i, j, live):
                    if live(0):
                        t = i * 2 * T + j
                        if j:
                            dve.drain()
                        dve.wait_ge(gathered[j], i * (16 * K) + (before + 16 * K))
                        x = X[:, bass.ds(t, 1), :].rearrange("p o d -> p (o d)")
                        for k in range(K):
                            if k:
                                dve.drain()
                            if to == "e1":
                                last = dve.scalar_tensor_tensor(out=x, in0=YG[:, j, k], scalar=gate[:, k, bass.ds(t, 1)],
                                                                in1=x, op0=ALU.mult, op1=ALU.add)
                            else:
                                last = dve.tensor_tensor(x, x, YG[:, j, k], ALU.add)
                        last.then_inc(gathered_used, 1)
                        if j % T == T - 1:
                            row_stats(NORM[norm] + i * 2 + j // T, i * 2 + j // T)
                    if j % T == 0 and live(T):
                        b = i * 2 + j // T - 1
                        dve.drain()
                        normalise(NORM[norm] + b, b)

                software_pipeline(dve, body, 2 * T, T, 1, B // 2)

            route("r1", 0)
            for t in range(NT):
                rows_out_of_x(t, t % 4, 16 * 2 * (t // 4))
            dve.wait_ge(route_act, 1)
            dve.tensor_reduce(gsum[:, :], PR[:, :, :], AX.X, ALU.add)
            dve.drain()
            dve.reciprocal(gsum[:, :], gsum[:, :])
            for k in range(TOPK["e1"]):
                dve.tensor_tensor(picked[:, k], hot[:, k], PR[:, :, :], ALU.mult)
            dve.drain()
            for k in range(TOPK["e1"]):
                dve.tensor_reduce(gate[:, k], picked[:, k], AX.X, ALU.add)
            dve.drain()
            dve.tensor_tensor(gate[:, :], gate[:, :], gsum[:, :].unsqueeze(1).to_broadcast([P, 2, NT]), ALU.mult)
            dve.drain()
            experts("e1")
            dve.wait_ge(mask_loaded, 16 * 3)
            dve.tensor_scalar(MASKF, MASKI, 1, NEG, ALU.is_equal, ALU.mult)
            dve.drain()
            dve.tensor_copy(bias4, by_tile(MASKF))
            dve.drain()
            dve.tensor_tensor(bias4[:, :, 0], bias4[:, :, 0], causal[:, :].unsqueeze(1).to_broadcast([P, B, SK]), ALU.add)
            add_gathered("e1", "n4", 0)
            end_stage(dve, "n4")
            attention("a2")
            route("r2", B // 2)
            experts("s2")
            experts("e2")
            values_evacuate(4, False)
            dve.wait_ge(last_loaded, 16 * 3)
            dve.tensor_copy(WBf.bitcast(BF16)[:, 0:G * D], W8).then_inc(w8_ready, 1)
            add_gathered("e2", "n6", NT)
            end_stage(dve, "n6")
            attention("a3")
            dve.tensor_reduce(qsc[:, 0:1], amax[:, :], AX.X, ALU.max).then_inc(part_amax, 1)
            dve.wait_ge(all_amax, 1)
            dve.tensor_scalar(qsc[:, 2:3], qsc[:, 1:2], 1.0 / 127.0, EPS, ALU.mult, ALU.max)
            dve.drain()
            dve.reciprocal(qsc[:, 3:4], qsc[:, 2:3])
            dve.drain()

            def quant_body(pair, j, live):
                n = pair * 2 + j
                if live(0):
                    dve.tensor_scalar(QA, xt_of(n), qsc[:, 3:4], 127.0, ALU.mult, ALU.min)
                if live(1):
                    dve.wait_ge(f_psum, n)
                    dve.scalar_tensor_tensor(out=R1, in0=PS[:, 0].rearrange("p (t d) -> p t d", t=T),
                                             scalar=qsc[:, 2:3], in1=repeat(rows[:, 0], T),
                                             op0=ALU.mult, op1=ALU.mult).then_inc(f_taken, 1)
                dve.drain()
                if live(0):
                    dve.tensor_scalar(QB, QA, -128.0, ROUND, ALU.max, ALU.add)
                if live(1):
                    dve.wait_ge(biased, n)
                    dve.tensor_tensor(x_of(n - 1), x_of(n - 1), R1, ALU.add).then_inc(x_final, 1)
                dve.drain()
                if live(0):
                    dve.tensor_scalar(QI, QB, -ROUND, None, ALU.add).then_inc(qi_ready, 1)

            software_pipeline(dve, quant_body, 2, 1, 1, B // 2)
            end_stage(dve, "q3")

        @block.tensor
        def _(pe):
            def transpose_rows(n):
                pe.wait_ge(xn_ready, n + 1)
                for g in range(G):
                    for t in range(T):
                        last = pe.transpose(PS[:, BANK_X, g * S + t * P:g * S + (t + 1) * P],
                                            XN[:, t, g * P:(g + 1) * P], ident[:, :])
                last.then_inc(xt_psum, 1)

            def plain_norm(stage):
                n = NORM[stage]
                transpose_rows(n)
                with pe.Fori(1, B) as b:
                    pe.wait_ge(xt_ready, n + b)
                    transpose_rows(n + b)

            def keys_and_values(k0, v0, between=lambda: None):
                for g in range(G):
                    for i in range(2):
                        for c in range(G):
                            last = pe.matmul(PS[:, 2 * g + i, 0:KW // 2], W[:, 1, c, g * P:(g + 1) * P],
                                             ctxT[:, c, i * (KW // 2):(i + 1) * (KW // 2)], start=c == 0, stop=c == G - 1)
                    last.then_inc(kt_psum, 1)
                    between()
                for b in range(B):
                    if b == B - 2:
                        pe.wait_ge(kt_ready, k0 + 1)
                    for c in range(G):
                        last = pe.matmul(PS[0:SK, (4, 5, 6, 0)[b // 2], (b % 2) * D:(b % 2 + 1) * D],
                                         ctxT[:, c, b * SK:(b + 1) * SK], W[:, 2, c, :], start=c == 0, stop=c == G - 1)
                    if b % 2:
                        last.then_inc(v_psum, 1)
                        between()

            def two_tiles(bank, left, right):
                for t in range(T):
                    for c in range(G):
                        last = pe.matmul(PS[:, bank, t * D:(t + 1) * D], left[:, c, t * P:(t + 1) * P], right[:, c],
                                         start=c == 0, stop=c == G - 1)
                return last

            def two_chunks(bank, weights, moving):
                for g in range(G):
                    for c in range(G):
                        last = pe.matmul(PS[:, bank, g * S:(g + 1) * S], weights[:, c, g * P:(g + 1) * P], moving(c),
                                         start=c == 0, stop=c == G - 1)
                return last

            def xt_moving(b):
                return lambda c: XT[:, bass.ds(b, 1), c, 1:S + 1].rearrange("p o s -> p (o s)")

            def attention(stage):
                layer, norms, alone = LAYER[stage], NORM[stage], ALONE[stage]
                u0, b0 = B * UNITS * layer, B * layer
                wo = W[:, 0 if stage == "a2" else 3]

                def body(b, j, live):
                    if live(2):
                        u, q = u0 + UNITS * b + j - 2, j % 2
                        bb, jj = (b, j - 2) if j >= 2 else (b - 1, j + 2)
                        g, t = jj // T, jj % T
                        pe.wait_ge(kbd_ready, G * (b0 + bb) + g + 1)
                        pe.wait_ge(q_ready, b0 + bb + 1)
                        after(pe, max_ready, u - 1)
                        for i in range(2):
                            last = pe.matmul(PS[:, 2 * q + i, 0:KW // 2], QT[:, g, t * P:(t + 1) * P],
                                             KBD[:, g, i * (KW // 2):(i + 1) * (KW // 2)], start=True, stop=True)
                        last.then_inc(s_psum, 1)
                    if live(5):
                        u, q = u0 + UNITS * b + j - 5, (j + 1) % 2
                        pe.wait_ge(p_ready, u + 1)
                        after(pe, pt_ready, u)
                        for c in range(CHUNKS + 1):
                            n = min(P, PW - c * P)
                            last = pe.transpose(PT_PSUM[0:n, c * P:(c + 1) * P], PN[:, q, c * P:c * P + n], ident[:, :])
                        last.then_inc(pt_psum, 1)
                    if live(6):
                        u = u0 + UNITS * b + j - 6
                        bb, jj = (b - 1, j - 2) if j >= 2 else (b - 2, j + 2)
                        g, t = jj // T, jj % T
                        pe.wait_ge(pt_ready, u + 1)
                        pe.wait_ge(vp1_ready, G * (b0 + bb) + g + 1)
                        pe.wait_ge(vp2_ready, G * (b0 + bb) + g + 1)
                        pe.wait_ge(vl_ready, b0 + bb + 1)
                        if jj == 0:
                            after(pe, ot_ready, b0 + bb)
                        cols = slice(g * S + t * P, g * S + (t + 1) * P)
                        n = HG * LEFT
                        pe.matmul(PS[:, BANK_OT, cols], VL[0:n, g], PT[0:n, CHUNKS * P:], start=True, stop=False)
                        for c in range(CHUNKS):
                            last = pe.matmul(PS[2 * DH * c:2 * DH * (c + 1), BANK_OT, cols], VP[:, g, c],
                                             PT[:, c * P:(c + 1) * P], start=False, stop=True)
                        last.then_inc(pv_done, 1)
                    if j == 0 and live(0) and stage != "a2":
                        after(pe, vs_ready, b0 + b)
                        two_chunks(BANK_X, W[:, 0], xt_moving(b)).then_inc(q_psum, 1)
                    if j == 1 and live(13):
                        pe.wait_ge(q_ready, at_most(b0 + b + 1, b0 + B))
                        pe.wait_ge(vs_ready, at_most(b0 + b, b0 + B))
                        transpose_rows(norms + b - 3)
                    if j == 2 and live(10):
                        pe.wait_ge(ot_ready, b0 + b - 1)
                        pe.wait_ge(q_ready, at_most(b0 + b + 1, b0 + B))
                        pe.wait_ge(vs_ready, at_most(b0 + b, b0 + B))
                        after(pe, xt_ready, norms + b - 2)
                        two_tiles(BANK_X, OT, wo).then_inc(o_psum, 1)
                    if j == 3 and live(0):
                        pe.wait_ge(q_ready, b0 + b + 1)
                        after(pe, o_taken, SUM[stage] + b - 1)
                        v = V[:, bass.ds(b, 1), :].rearrange("k o d -> k (o d)")
                        pe.matmul(VL_PSUM, spreader[0:SK, :], v, start=True, stop=True).then_inc(vl_psum, 1)

                software_pipeline(pe, body, UNITS, 10, 3)
                end_stage(pe, stage)

            pe.wait_ge(const_ready, 1)
            first_norms = iter(range(B))

            def first_norm():
                n = next(first_norms)
                after(pe, xt_ready, n)
                transpose_rows(n)

            first_norm()
            first_norm()
            pe.wait_ge(ctx_loaded, 16)
            pe.wait_ge(w_loaded, 16 * 4)
            keys_and_values(0, 0, between=first_norm)
            end_stage(pe, "setup")
            attention("a0")

            def ffn_body(b, j, live):
                if live(0):
                    pe.wait_ge(k_mixed, b + 1)
                    after(pe, krelu_ready, b)
                    two_chunks(1, W[:, 1], lambda c: xkT[:, c]).then_inc(k_psum, 1)
                    pe.wait_ge(r_mixed, b + 1)
                    after(pe, r_ready, b)
                    two_tiles(0, xrT, W[:, 0]).then_inc(r_psum, 1)
                if live(1):
                    pe.wait_ge(ksq_ready, b)
                    after(pe, o_taken, SUM["f0"] + b - 1)
                    two_tiles(6, ksq, W[:, 2]).then_inc(o_psum, 1)
                if live(2):
                    pe.wait_ge(xt_ready, NORM["f0"] + b - 2)
                    transpose_rows(NORM["f0"] + b - 2)

            pe.wait_ge(w_loaded, 16 * 7)
            software_pipeline(pe, ffn_body, 1, 2, 2)
            end_stage(pe, "f0")

            def mlp_body(b, j, live):
                if live(0):
                    pe.wait_ge(ctxs_ready, b + 1)
                    after(pe, g_ready, b)
                    for c in range(G):
                        last = pe.matmul(PS[0:SK, 0, 0:S], ctxS[:, c], xt_moving(b)(c), start=c == 0, stop=c == G - 1)
                    last.then_inc(g_psum, 1)
                if live(1):
                    pe.wait_ge(g_ready, b)
                    after(pe, o_taken, SUM["m1"] + b - 1)
                    ctx_b = V[:, bass.ds(b - 1, 1), :].rearrange("k o d -> k (o d)")
                    for t in range(T):
                        last = pe.matmul(PS[:, 6, t * D:(t + 1) * D], gel[:, t * P:(t + 1) * P], ctx_b, start=True, stop=True)
                    last.then_inc(o_psum, 1)
                if live(3):
                    pe.wait_ge(xt_ready, NORM["m1"] + b - 3)
                    transpose_rows(NORM["m1"] + b - 3)

            pe.wait_ge(ctx_loaded, 16 * 2)
            software_pipeline(pe, mlp_body, 1, 3, 3)
            end_stage(pe, "m1")

            def route(stage, first):
                for n in range(B // 2 + 1):
                    if n < B // 2:
                        after(pe, lt_ready, first + n - 1)
                        for c in range(G):
                            last = pe.matmul(PS[0:E, 2 * (n % 2)], WR[:, c], XT[:, 2 * n:2 * n + 2, c, 1:S + 1],
                                             start=c == 0, stop=c == G - 1)
                        last.then_inc(lt_psum, 1)
                    if n > 0:
                        pe.wait_ge(lt_ready, first + n)
                        for t in range(2 * T):
                            at = ((n - 1) * 2 * T + t) * E
                            last = pe.transpose(PS[:, 1, at:at + E], LTs[:, (n - 1) % 2, t * P:(t + 1) * P], ident[0:E, 0:E])
                        last.then_inc(lg_psum, 1)

                pe.wait_ge(tri_ready, first // (B // 2) + 1)
                pe.wait_ge(taken_ready, first // (B // 2) + 1)
                every = taken[:, :, :].rearrange("p t e -> p (t e)")
                pe.matmul(PS[:, 2, 0:NT * E], tri, every, start=True, stop=True)
                pe.matmul(PS[:, 3, 0:NT * E], ones, every, start=True, stop=True).then_inc(count_psum, 1)
                end_stage(pe, stage)

            def experts(stage):
                F, u0 = WIDTH[stage], FIRST[stage]
                chunks = -(-F // P)

                def weights_at(i):
                    return pe.value_load(owner_i[0:1, bass.ds(i, 1)], min_val=0, max_val=(E - 1) * EW)

                def body(i, live):
                    at_up = weights_at(i[0] - 1) if live(1) and stage != "s2" else None
                    at_down = weights_at(i[0] - 3) if live(3) and stage != "s2" else None
                    if live(0) and stage != "s2":
                        n = FIRST_X[stage] + i[0]
                        pe.wait_ge(rows_in[i[1]], moved(stage, i[1], i[2] + 1))
                        after(pe, xs_ready, u0 + i[0])
                        for g in range(G):
                            last = pe.transpose(PS[:, 7, g * P:(g + 1) * P], XR[:, i[1], g * P:(g + 1) * P], ident[:, :])
                        last.then_inc(xt2_psum, 1)
                    if live(1):
                        u, q = u0 + i[0] - 1, 1 - i[1]
                        pe.wait_ge(xs_ready, u + 1)
                        after(pe, hh_ready, u - 1)
                        for k in range(2):
                            for c in range(G):
                                if stage == "s2":
                                    w = shared_w[k][:, c * F:(c + 1) * F]
                                else:
                                    w = WE[:, bass.ds(at_up + (k * G + c) * F, F)]
                                last = pe.matmul(PS[:, 2 * q + k, 0:F], XS[:, q, c], w, start=c == 0, stop=c == G - 1)
                        last.then_inc(h_psum, 1)
                    if live(2):
                        u, q = u0 + i[0] - 2, i[1]
                        pe.wait_ge(hh_ready, u + 1)
                        after(pe, ht_ready, u - 1)
                        for c in range(chunks):
                            n = min(P, F - c * P)
                            last = pe.transpose(PS[0:n, 4 + q, c * P:(c + 1) * P], HH[:, q, c * P:c * P + n], ident[:, :])
                        last.then_inc(ht_psum, 1)
                    if live(3):
                        u, q = u0 + i[0] - 3, 1 - i[1]
                        pe.wait_ge(ht_ready, u + 1)
                        after(pe, y_taken, u)
                        for c in range(chunks):
                            n = min(P, F - c * P)
                            if stage == "s2":
                                w = shared_wd[0:n, c * D:(c + 1) * D]
                            else:
                                w = WE[0:n, bass.ds(at_down + 2 * G * F + c * D, D)]
                            last = pe.matmul(PS[:, 6, 0:D], HT[0:n, q, c], w, start=c == 0, stop=c == chunks - 1)
                        last.then_inc(y_psum, 1)

                if stage == "s2":
                    pe.wait_ge(shared_loaded, 16 * 3)
                else:
                    pe.wait_ge(moe_loaded, MOE_LOADED[stage])
                tile_pipeline(pe, body, NT if stage == "s2" else SLOTS[stage], 3)
                end_stage(pe, stage)

            pe.wait_ge(w_loaded, 16 * 9)
            route("r1", 0)
            experts("e1")
            plain_norm("n4")
            end_stage(pe, "n4")
            attention("a2")
            pe.wait_ge(mask_loaded, 16 * 3)
            route("r2", B // 2)
            experts("s2")
            experts("e2")
            pe.wait_ge(w_loaded, 16 * 13)
            keys_and_values(G, 4)
            plain_norm("n6")
            end_stage(pe, "n6")
            attention("a3")
            pe.wait_ge(w8_ready, 1)
            with pe.Fori(0, B) as b:
                pe.wait_ge(qi_ready, b + 1)
                pe.wait_ge(f_taken, b)
                two_tiles(0, QI, WBF).then_inc(f_psum, 1)
            end_stage(pe, "q3")


def kernel(**inputs):
    import concourse.bacc as bacc
    from concourse.bass_utils import run_bass_kernel_spmd

    def flip(name, axes=None):
        return np.ascontiguousarray(np.transpose(inputs[name], axes))

    def columns(*names):
        return np.stack([inputs[n] for n in names]).reshape(len(names), G, P).transpose(2, 0, 1)

    ctx = np.ascontiguousarray(inputs["ctx_1024"])
    arrays = {
        "x": inputs["x"], "ctx": ctx, "ctxT": np.ascontiguousarray(ctx.reshape(-1, D).T),
        "bias": inputs["fside_BxSxS2_0"], "mask0": inputs["mask_BxS2_ik0"].reshape(-1), "mask2": inputs["mask_BxS2_if0"].reshape(-1),
        "L0_wqT": flip("L0_xattn_w_q"), "L0_wkT": flip("L0_xattn_w_k"), "L0_wvT": flip("L0_xattn_w_v"), "L0_woT": flip("L0_xattn_w_o"),
        "L0_vecs": columns("L0_xattn_b_q", "L0_xattn_b_k", "L0_ffn_mu_r", "L0_ffn_mu_k"), "L0_bv": inputs["L0_xattn_b_v"], "L0_bo": inputs["L0_xattn_b_o"],
        "L0_WrT": flip("L0_ffn_W_r"), "L0_WkT": flip("L0_ffn_W_k"), "L0_WvT": flip("L0_ffn_W_v"),
        "L1_wrT": flip("L1_ffn_w_router"), "L1_w1": inputs["L1_ffn_w1"], "L1_w2": inputs["L1_ffn_w2"], "L1_w3": inputs["L1_ffn_w3"],
        "L2_WT": flip("L2_xattn_W"), "L2_b": inputs["L2_xattn_b"], "L2_gateT": flip("L2_ffn_gate_w"),
        "L2_sgT": flip("L2_ffn_shared_gate"), "L2_suT": flip("L2_ffn_shared_up"), "L2_sdT": flip("L2_ffn_shared_down"),
        "L2_rgT": flip("L2_ffn_r_gate", (0, 2, 1)), "L2_ruT": flip("L2_ffn_r_up", (0, 2, 1)), "L2_rdT": flip("L2_ffn_r_down", (0, 2, 1)),
        "L3_Wq": inputs["L3_xattn_Wq"], "L3_Wk": inputs["L3_xattn_Wk"], "L3_Wv": inputs["L3_xattn_Wv"], "L3_Wo": inputs["L3_xattn_Wo"],
        "L3_w8T": flip("L3_ffn_weight_int8").view(np.int32), "L3_ws": inputs["L3_ffn_weight_scale"].reshape(-1), "L3_bias": inputs["L3_ffn_bias"],
    }
    arrays = {k: np.ascontiguousarray(v) for k, v in arrays.items()}
    nc = bacc.Bacc("TRN2", target_bir_lowering=False, num_devices=1)
    a = {k: nc.dram_tensor("in_" + k, v.shape, mybir.dt.from_np(v.dtype), kind="ExternalInput").ap() for k, v in arrays.items()}
    for buf, tiles in (("xs1", 2 * NT + E - 1), ("ys1", 2 * NT + E - 1), ("xs2", NT + E - 1), ("ys2", NT + E - 1)):
        a[buf] = nc.dram_tensor(buf, (tiles * P, D), F32, kind="Internal").ap()
    a["out"] = nc.dram_tensor("out", (B, S, D), F32, kind="ExternalOutput").ap()
    build(nc, a)
    r = run_bass_kernel_spmd(nc, [{"in_" + k: v for k, v in arrays.items()}], core_ids=[0])
    return r.results[0]["out"]
```
